# Optimizing a Trainium2 kernel written in Bass

```python
import numpy as np
import jax
import jax.numpy as jnp

def _softmax(x, axis=-1):
    return jax.nn.softmax(x, axis=axis)

def _gelu(x):
    return jax.nn.gelu(x, approximate=True)

def _silu(x):
    return jax.nn.silu(x)

def _sigmoid(x):
    return jax.nn.sigmoid(x)

def _layernorm(x, axis=-1, eps=1e-05):
    m = jnp.mean(x, axis=axis, keepdims=True)
    v = jnp.var(x, axis=axis, keepdims=True)
    return (x - m) / jnp.sqrt(v + eps)

def _scatter_add(tgt, idx, src, axis=0):
    return tgt.at[idx].add(src)

def _segment_sum(src, seg, n):
    return jax.ops.segment_sum(src, seg, n)
kernel_name = 'mk_gnn_ffn_d1_gnn_r8_59fa8b'

def setup_inputs(seed: int=0):
    np.random.seed(seed)
    _w = jnp.asarray

    def _rec_inputs():
        import jax
        import jax.numpy as jnp
        _gk = jax.random.key(seed)
        x = -0.0003713 + 1 * jax.random.normal(jax.random.fold_in(_gk, 1), (6250, 256), jnp.float32)
        src = jax.random.randint(jax.random.fold_in(_gk, 2), (200000,), 0, 6250, jnp.int32)
        dst = jnp.minimum((6250 * jax.random.uniform(jax.random.fold_in(_gk, 3), (200000,)) ** 2.0).astype(jnp.int32), 49999)
        _o = jnp.argsort(dst, stable=True)
        src = src[_o]
        dst = dst[_o]
        return (x, src, dst)
    x, src, dst = _rec_inputs()

    def _L0_gnn_setup():
        import jax, jax.numpy as jnp
        import numpy as np
        N, E, FIN, H, FO = (6250, 100000, 256, 8, 32)
        key = jax.random.key(seed)
        ks = jax.random.split(key, 7)
        node_features = jax.random.normal(ks[0], (N, FIN), dtype=jnp.float32)
        edge_index = jax.random.randint(ks[1], (2, E), 0, N, dtype=jnp.int32).astype(jnp.int64)
        Wp = jax.random.normal(ks[2], (H * FO, FIN), dtype=jnp.float32) * (1.0 / np.sqrt(FIN))
        a_src = jax.random.normal(ks[3], (1, H, FO), dtype=jnp.float32) * 0.1
        a_trg = jax.random.normal(ks[4], (1, H, FO), dtype=jnp.float32) * 0.1
        Wskip = jax.random.normal(ks[5], (H * FO, FIN), dtype=jnp.float32) * (1.0 / np.sqrt(FIN))
        bias = jnp.zeros((H * FO,), dtype=jnp.float32)
        return {'node_features': node_features, 'edge_index': edge_index, 'Wp': Wp, 'a_src': a_src, 'a_trg': a_trg, 'Wskip': Wskip, 'bias': bias}
    _L0_gnn_all = _L0_gnn_setup()
    _L0_gnn_in = {k: v for k, v in _L0_gnn_all.items() if k in ('Wp', 'a_src', 'a_trg', 'Wskip', 'bias')}
    del _L0_gnn_all

    def _L0_ffn_setup():
        import jax, jax.numpy as jnp
        import numpy as np
        TOP_K = 2
        LN_EPS = 1e-05
        key = jax.random.key(seed)
        ks = jax.random.split(key, 8)
        B, S, D, E, H = (16, 1024, 256, 8, 1024)
        x = jax.random.normal(ks[0], (B, S, D), dtype=jnp.float32)
        Wr = jax.random.normal(ks[1], (D, E), dtype=jnp.float32) * 0.1
        br = jnp.zeros((E,), dtype=jnp.float32)
        ln_g = jnp.ones((E, D), dtype=jnp.float32)
        ln_b = jnp.zeros((E, D), dtype=jnp.float32)
        W1 = jax.random.normal(ks[2], (E, D, H), dtype=jnp.float32) * (1.0 / np.sqrt(D))
        b1 = jnp.zeros((E, H), dtype=jnp.float32)
        W2 = jax.random.normal(ks[3], (E, H, D), dtype=jnp.float32) * (1.0 / np.sqrt(H))
        b2 = jnp.zeros((E, D), dtype=jnp.float32)
        return {'x': x, 'Wr': Wr, 'br': br, 'ln_g': ln_g, 'ln_b': ln_b, 'W1': W1, 'b1': b1, 'W2': W2, 'b2': b2}
    _L0_ffn_all = _L0_ffn_setup()
    _L0_ffn_in = {k: v for k, v in _L0_ffn_all.items() if k in ('Wr', 'br', 'ln_g', 'ln_b', 'W1', 'b1', 'W2', 'b2')}
    del _L0_ffn_all
    return {'x': x, 'src': src, 'dst': dst, 'L0_gnn_Wp': _L0_gnn_in['Wp'], 'L0_gnn_a_src': _L0_gnn_in['a_src'], 'L0_gnn_a_trg': _L0_gnn_in['a_trg'], 'L0_gnn_Wskip': _L0_gnn_in['Wskip'], 'L0_gnn_bias': _L0_gnn_in['bias'], 'L0_ffn_Wr': _L0_ffn_in['Wr'], 'L0_ffn_br': _L0_ffn_in['br'], 'L0_ffn_ln_g': _L0_ffn_in['ln_g'], 'L0_ffn_ln_b': _L0_ffn_in['ln_b'], 'L0_ffn_W1': _L0_ffn_in['W1'], 'L0_ffn_b1': _L0_ffn_in['b1'], 'L0_ffn_W2': _L0_ffn_in['W2'], 'L0_ffn_b2': _L0_ffn_in['b2']}

def reference(x, src, dst, L0_gnn_Wp, L0_gnn_a_src, L0_gnn_a_trg, L0_gnn_Wskip, L0_gnn_bias, L0_ffn_Wr, L0_ffn_br, L0_ffn_ln_g, L0_ffn_ln_b, L0_ffn_W1, L0_ffn_b1, L0_ffn_W2, L0_ffn_b2):
    import jax
    import jax.numpy as jnp

    def _L0_gnn_ref(node_features, edge_index, Wp, a_src, a_trg, Wskip, bias):
        import jax, jax.numpy as jnp
        import numpy as np
        N, E, FIN, H, FO = (6250, 100000, 256, 8, 32)
        x = node_features
        src, trg = (edge_index[0], edge_index[1])
        proj = (x @ Wp.T).reshape(-1, H, FO)
        scores_src = jnp.sum(proj * a_src, axis=-1)
        scores_trg = jnp.sum(proj * a_trg, axis=-1)
        s = scores_src[src] + scores_trg[trg]
        s = jax.nn.leaky_relu(s, negative_slope=0.2)
        s = s - jnp.max(s)
        exp_s = jnp.exp(s)
        denom = jax.ops.segment_sum(exp_s, trg, num_segments=N)
        attn = exp_s / (denom[trg] + 1e-16)
        weighted = proj[src] * attn[:, :, None]
        out = jax.ops.segment_sum(weighted, trg, num_segments=N)
        out = out + (x @ Wskip.T).reshape(-1, H, FO)
        out = out.reshape(-1, H * FO) + bias
        return jax.nn.elu(out)

    def _L0_ffn_ref(x, Wr, br, ln_g, ln_b, W1, b1, W2, b2):
        import jax, jax.numpy as jnp
        import numpy as np
        TOP_K = 2
        LN_EPS = 1e-05
        B, S, D = x.shape
        N = B * S
        xt = x.reshape(N, D)
        logits = xt @ Wr + br
        probs = jax.nn.softmax(logits, axis=-1)
        top_p, top_idx = jax.lax.top_k(probs, TOP_K)
        weights = top_p / top_p.sum(axis=-1, keepdims=True)
        mu = xt.mean(axis=-1, keepdims=True)
        var = ((xt - mu) ** 2).mean(axis=-1, keepdims=True)
        xn = (xt - mu) * jax.lax.rsqrt(var + LN_EPS)
        xe = xn[None, :, :] * ln_g[:, None, :] + ln_b[:, None, :]
        h = jax.nn.gelu(jnp.einsum('end,edh->enh', xe, W1) + b1[:, None, :], approximate=False)
        y = jnp.einsum('enh,ehd->end', h, W2) + b2[:, None, :]
        y_tok = jnp.transpose(y, (1, 0, 2))
        sel = jnp.take_along_axis(y_tok, top_idx[:, :, None], axis=1)
        out = (weights[:, :, None] * sel).sum(axis=1)
        return out.reshape(B, S, D)
    edge_index = jnp.stack([src, dst])
    x = x + _L0_gnn_ref(_layernorm(x, axis=-1), edge_index, L0_gnn_Wp, L0_gnn_a_src, L0_gnn_a_trg, L0_gnn_Wskip, L0_gnn_bias)
    x = x + _L0_ffn_ref(_layernorm(x, axis=-1)[None], L0_ffn_Wr, L0_ffn_br, L0_ffn_ln_g, L0_ffn_ln_b, L0_ffn_W1, L0_ffn_b1, L0_ffn_W2, L0_ffn_b2)[0]
    return x

_drawn_inputs = setup_inputs


def setup_inputs(seed=0):
    import zlib

    import numpy as np

    out = dict(_drawn_inputs(seed))
    spreads = {'L0_gnn_bias': (0.0, 0.1),
     'L0_ffn_br': (0.0, 0.1),
     'L0_ffn_ln_g': (1.0, 0.2),
     'L0_ffn_ln_b': (0.0, 0.1),
     'L0_ffn_b1': (0.0, 0.1),
     'L0_ffn_b2': (0.0, 0.1)}
    factors = {}
    for name, (base, spread) in spreads.items():
        noise = np.random.default_rng([zlib.crc32(name.encode()), seed]).standard_normal(out[name].shape)
        drawn = base * np.exp(spread * noise) if base else spread * noise
        out[name] = jnp.asarray(drawn.astype(out[name].dtype))
    for name, factor in factors.items():
        out[name] = (out[name] * factor).astype(out[name].dtype)
    return out
```

```python
from contextlib import ExitStack

import concourse.bass as bass
from concourse import mybir

F32 = mybir.dt.float32
BF16 = mybir.dt.bfloat16
I32 = mybir.dt.int32
U32 = mybir.dt.uint32
ALU = mybir.AluOpType
ACT = mybir.ActivationFunctionType
X = mybir.AxisListType.X

P = 128
N, D = 6250, 256
E = 200000
H, FO = 8, 32
NX, HID = 8, 1024
LN_EPS = 1e-5
SLOPE = 0.2
DEN_EPS = 1e-16

NP = 125
NT = N // NP
KD = D // P
ROW = D + H

SUB = 128
G = 4
EROW = G * SUB
NSUB = -(-E // SUB)
EC = -(-E // (P * EROW))
EFULL = E // EROW
ETAIL = E - EFULL * EROW
COLS = EC * P * G
NO_NODE = 16384
BIG = 4096

TOK = 256
HALF = TOK // P
JH = HID // P
CAP = -(-(N + TOK) // TOK) * TOK
FILL = TOK
XROW = D + 1


def tile(t, n=NP):
    return bass.ds(t * n, n)


def value_of(engine, count):
    return engine.snap(engine.to_reg(count))


def m_v(mv, t):
    return mv[:, bass.ds(t, 1), :].rearrange("p a k -> p (a k)")


def gnn_ffn(nc, x, src, dst, Wp, a_src, a_trg, Wskip, bias, Wr, br, ln_g, ln_b, W1, b1, W2, b2, out):
    table = nc.dram_tensor("proj_table", (N, ROW), F32).ap()
    skip_rows = nc.dram_tensor("skip_rows", (N, D), F32).ap()
    xg = nc.dram_tensor("tokens_by_expert", (NX * CAP, XROW), F32).ap()
    y2 = nc.dram_tensor("results_by_token", (2 * N + P, D), F32).ap()

    with ExitStack() as ctx:
        def sb(name, shape, dt=F32):
            return ctx.enter_context(nc.sbuf_tensor(name, shape, dt))

        bank = [ctx.enter_context(nc.psum_tensor(f"bank{k}", [P, 512], F32)) for k in range(8)]
        m = dict(
            iota=sb("iota", [P, P]), iota_p=sb("iota_p", [P, 1]), ident=sb("ident", [P, P]),
            lower=sb("lower", [P, P]), ones=sb("ones", [P, P]), zero16=sb("zero16", [P, ROW], BF16),
            begun=ctx.enter_context(nc.semaphore("begun")), neg_block=sb("neg_block", [P, NT]),
            cap_row=sb("cap_row", [P, NX]), st=sb("st", [NP, NT, H + 1]),
            acc=sb("acc", [NP, NT, ROW]), neg_bound=sb("neg_bound", [P, 1]),
            ln_eps=sb("ln_eps", [P, 1]), eps=sb("eps", [P, 1]), runmax=sb("runmax", [P, H]),
            gaps=sb("gaps", [NP, NT]), weights=sb("weights", [NP, NT, 2]),
            result_row=sb("result_row", [NP, NT, 2]), counts=sb("counts", [1, NX, 4], I32),
            br=sb("br", [NP, NX]), wr=sb("wr", [P, KD, NX]),
        )
        with ExitStack() as edge_ctx:
            def esb(name, shape, dt=F32):
                return edge_ctx.enter_context(nc.sbuf_tensor(name, shape, dt))

            m.update(src_tab=esb("src_tab", [P, COLS], I32), dst_tab=esb("dst_tab", [P, COLS]),
                     ranges=esb("ranges", [1, NT, 4], I32))
            edge_tables(nc, m, bank, src, dst)
            node_phase(nc, m, bank, x, Wp, a_src, a_trg, Wskip, bias, Wr, br, table, skip_rows)
            edge_phase(nc, m, bank, table)
        route_phase(nc, m, bank, x, skip_rows, xg)
        expert_phase(nc, m, bank, xg, y2, ln_g, ln_b, W1, b1, W2, b2)
        combine_phase(nc, m, y2, out)


def edge_tables(nc, m, bank, src, dst):
    with ExitStack() as ctx:
        def sb(name, shape, dt=F32):
            return ctx.enter_context(nc.sbuf_tensor(name, shape, dt))

        def sem(name):
            return ctx.enter_context(nc.semaphore(name))

        raw = {"src": sb("src_raw", [P, EC, EROW], I32), "dst": sb("dst_raw", [P, EC, EROW], I32)}
        rows = {"src": sb("src_rows", [P, EC, EROW]), "dst": sb("dst_rows", [P, EC, EROW])}
        lowest = sb("lowest", [P, EC * G])
        highest = sb("highest", [P, EC * G])
        number = sb("number", [P, EC * G])
        starts = sb("starts", [P, NT])
        starts_ok = sb("starts_ok", [P, NT, EC * G])
        touched = sb("touched", [P, NT, EC * G])
        scored = sb("scored", [P, 2, NT, EC * G])
        best = sb("best", [P, 2, NT])
        best_col = sb("best_col", [2 * NT, 1])
        row, whole = sb("range_row", [1, 8, NT]), sb("range_whole", [1, NT], I32)
        iota_done, consts, padded, loaded = sem("iota_done"), sem("consts"), sem("padded"), sem("edges_loaded")
        as_float, turned = sem("as_float"), sem("turned")
        dst_out, src_out = sem("dst_out"), sem("src_out")
        dve_step, pe_step, best_ready = sem("range_dve"), sem("range_pe"), sem("best_ready")
        iota, ident = m["iota"], m["ident"]

        block = ctx.enter_context(nc.Block())

        @block.gpsimd
        def _(pool):
            nc.gpsimd.iota(iota[:], [[1, P]], base=0, channel_multiplier=0,
                           allow_small_or_imprecise_dtypes=True).then_inc(iota_done, 1)
            nc.gpsimd.iota(m["iota_p"][:], [[0, 1]], base=0, channel_multiplier=1,
                           allow_small_or_imprecise_dtypes=True).then_inc(iota_done, 1)
            nc.gpsimd.iota(m["result_row"][:], [[2 * NP, NT], [1, 2]], base=0, channel_multiplier=2,
                           allow_small_or_imprecise_dtypes=True).then_inc(iota_done, 1)
            nc.gpsimd.iota(number[:], [[P * G, EC], [1, G]], base=1, channel_multiplier=G,
                           allow_small_or_imprecise_dtypes=True).then_inc(iota_done, 1)
            nc.gpsimd.iota(starts[:], [[NP, NT]], base=0, channel_multiplier=0,
                           allow_small_or_imprecise_dtypes=True).then_inc(iota_done, 1)

        @block.sync
        def _(sp):
            sp.wait_ge(padded, 2)
            for name, flat in (("dst", dst), ("src", src)):
                to = raw[name]
                whole = (EC - 1) * P * EROW
                sp.dma_start(to[:, 0:EC - 1, :], flat[0:whole].rearrange("(c p e) -> p c e", p=P, e=EROW)
                             ).then_inc(loaded, 16)
                rest = EFULL - (EC - 1) * P
                sp.dma_start(to[0:rest, EC - 1, :], flat[whole:whole + rest * EROW].rearrange("(p e) -> p e", e=EROW)
                             ).then_inc(loaded, 16)
                sp.dma_start(to[rest:rest + 1, EC - 1, 0:ETAIL], flat[EFULL * EROW:E].rearrange("(p e) -> p e", p=1)
                             ).then_inc(loaded, 16)

        @block.vector
        def _(dve):
            steps = [0]

            def step(ins):
                steps[0] += 1
                ins.then_inc(dve_step, 1)

            def settle():
                dve.wait_ge(dve_step, steps[0])

            nc.vector.memset(raw["dst"][:, EC - 1, :], NO_NODE).then_inc(padded, 1)
            nc.vector.memset(raw["src"][:, EC - 1, :], 0).then_inc(padded, 1)
            nc.vector.memset(m["ones"][:], 1.0).then_inc(m["begun"], 1)
            nc.vector.memset(m["zero16"][:], 0.0)
            nc.vector.memset(m["st"][:], 1.0)
            nc.vector.memset(m["ln_eps"][:], LN_EPS)
            nc.vector.memset(m["runmax"][:], 0.0)
            dve.wait_ge(iota_done, 5)
            nc.vector.tensor_scalar(ident[:], iota[:], m["iota_p"][:], None, ALU.is_equal).then_inc(consts, 1)
            nc.vector.tensor_scalar(m["lower"][:], iota[:], m["iota_p"][:], None, ALU.is_gt).then_inc(consts, 1)
            nc.vector.tensor_scalar(m["neg_block"][:], starts[:], -1.0, None, ALU.mult).then_inc(consts, 1)
            nc.vector.tensor_scalar(m["cap_row"][:], iota[:, 0:NX], float(CAP), None, ALU.mult).then_inc(consts, 1)
            dve.wait_ge(loaded, 16 * 6)
            for name in ("dst", "src"):
                nc.vector.tensor_copy(rows[name][:], raw[name][:]).then_inc(as_float, 1)
            for c in range(EC):
                dve.wait_ge(turned, 2 * c + 1)
                nc.vector.tensor_copy(
                    m["dst_tab"][:, c * P * G:(c + 1) * P * G].rearrange("p (r j) -> p j r", j=G),
                    bank[2 * (c % 2)][:].rearrange("p (j r) -> p j r", j=G)).then_inc(dst_out, 1)
            by_sub = rows["dst"][:].rearrange("p c (j e) -> p (c j) e", j=G)
            step(nc.vector.tensor_reduce(lowest[:], by_sub, X, ALU.min))
            step(nc.vector.tensor_reduce(highest[:], by_sub, X, ALU.max))
            settle()
            shape = [P, NT, EC * G]

            def over_blocks(v):
                return v[:].unsqueeze(1).to_broadcast(shape)

            start_b = starts[:].unsqueeze(2).to_broadcast(shape)
            step(nc.vector.tensor_tensor(starts_ok[:], over_blocks(highest), start_b, ALU.is_ge))
            step(nc.vector.tensor_scalar(lowest[:], lowest[:], -float(NP - 1), None, ALU.add))
            settle()
            step(nc.vector.tensor_tensor(touched[:], start_b, over_blocks(lowest), ALU.is_ge))
            settle()
            step(nc.vector.tensor_tensor(touched[:], touched[:], starts_ok[:], ALU.mult))
            settle()
            step(nc.vector.tensor_tensor(scored[:, 0], touched[:], over_blocks(number), ALU.mult))
            settle()
            step(nc.vector.tensor_scalar(number[:], number[:], -1.0, float(BIG), ALU.mult, ALU.add))
            settle()
            step(nc.vector.tensor_tensor(scored[:, 1], touched[:], over_blocks(number), ALU.mult))
            settle()
            nc.vector.tensor_reduce(best[:], scored[:], X, ALU.max).then_inc(best_ready, 1)
            dve.wait_ge(pe_step, 1)
            nc.vector.tensor_reduce(best_col[:], bank[4][0:2 * NT, 0:P], X, ALU.max).then_inc(best_ready, 1)
            dve.wait_ge(pe_step, 2)
            LAST, FIRST, LO, END, CNT, GE, GS, ZERO = range(8)
            step(nc.vector.tensor_copy(row[:, LAST:FIRST + 1, :].rearrange("p a b -> p (a b)"),
                                       bank[5][0:1, 0:2 * NT]))
            step(nc.vector.memset(row[:, ZERO], 0.0))
            settle()
            step(nc.vector.tensor_scalar(row[:, LO], row[:, FIRST], -1.0, float(BIG - 1), ALU.mult, ALU.add))
            settle()
            step(nc.vector.tensor_scalar(row[:, LO], row[:, LO], float(NSUB - 1), 0.0, ALU.min, ALU.max))
            settle()
            step(nc.vector.tensor_tensor(row[:, END], row[:, LAST], row[:, LO], ALU.subtract))
            settle()
            step(nc.vector.tensor_scalar(row[:, END], row[:, END], 1.0, float(G - 1), ALU.max, ALU.add))
            settle()
            step(nc.vector.tensor_copy(whole[:], row[:, END]))
            settle()
            step(nc.vector.tensor_scalar(whole[:], whole[:], G.bit_length() - 1, None, ALU.arith_shift_right))
            settle()
            step(nc.vector.tensor_copy(row[:, CNT], whole[:]))
            settle()
            step(nc.vector.tensor_tensor_scan(row[:, GE], row[:, CNT], row[:, ZERO], 0.0, ALU.add, ALU.add))
            settle()
            step(nc.vector.tensor_tensor(row[:, GS], row[:, GE], row[:, CNT], ALU.subtract))
            settle()
            for k, r in enumerate((LO, GS, GE, ZERO)):
                step(nc.vector.tensor_copy(m["ranges"][:, :, k], row[:, r]))
            settle()

        @block.tensor
        def _(pe):
            pe.wait_ge(consts, 1)
            n = 0
            for c in range(EC):
                for k, name in enumerate(("dst", "src")):
                    if c == 0:
                        pe.wait_ge(as_float, k + 1)
                    if c >= 2:
                        pe.wait_ge((dst_out, src_out)[k], c - 1)
                    for j in range(G):
                        mm = nc.tensor.transpose(bank[2 * (c % 2) + k][:, j * P:(j + 1) * P],
                                                 rows[name][:, c, j * P:(j + 1) * P], ident[:])
                    mm.then_inc(turned, 1)
            pe.wait_ge(best_ready, 1)
            nc.tensor.transpose(bank[4][0:2 * NT, 0:P], best[:].rearrange("p a b -> p (a b)"),
                                ident[:]).then_inc(pe_step, 1)
            pe.wait_ge(best_ready, 2)
            nc.tensor.matmul(bank[5][0:1, 0:2 * NT], best_col[:], ident[0:2 * NT, 0:2 * NT],
                             start=True, stop=True).then_inc(pe_step, 1)

        @block.scalar
        def _(act):
            for c in range(EC):
                act.wait_ge(turned, 2 * c + 2)
                nc.scalar.copy(m["src_tab"][:, c * P * G:(c + 1) * P * G].rearrange("p (r j) -> p j r", j=G),
                               bank[2 * (c % 2) + 1][:].rearrange("p (j r) -> p j r", j=G)).then_inc(src_out, 1)


def node_phase(nc, m, bank, x, Wp, a_src, a_trg, Wskip, bias, Wr, br, table, skip_rows):
    with ExitStack() as ctx:
        def sb(name, shape, dt=F32):
            return ctx.enter_context(nc.sbuf_tensor(name, shape, dt))

        def sem(name):
            return ctx.enter_context(nc.semaphore(name))

        def sems(name, n=2):
            return [sem(f"{name}{k}") for k in range(n)]

        wp, wskip = sb("wp", [P, KD, D]), sb("wskip", [P, KD, D])
        a_cols = sb("a_cols", [P, 2, KD])
        a_heads = sb("a_heads", [P, KD, 2 * H])
        bias_b = sb("bias_b", [NP, D])
        w_table, w_skip = sb("w_table", [P, KD, ROW]), sb("w_skip", [P, KD, ROW])
        xin, xn, xt = sb("xin", [NP, 2, D]), sb("xn", [NP, 2, D]), sb("xt", [P, 2, KD, NP])
        stats, mv = sb("stats", [NP, 2, 6]), sb("mv", [NP, 2, 2])
        std, rstd = sb("std", [NP, 2]), sb("rstd", [NP, 2])
        trow, srow = sb("trow", [NP, 2, ROW]), sb("srow", [NP, 2, D])
        maxima, top, bound = sb("maxima", [NP, 2, H]), sb("top", [P, 2]), sb("bound", [P, 2])
        begun = m["begun"]
        w_loaded, heads_zero, heads = sem("w_loaded"), sem("heads_zero"), sem("heads")
        w_turned, w_ready, max_step, max_pe = sem("w_turned"), sem("w_ready"), sem("max_step"), sem("max_pe")
        x_loaded, norm_step, std_done, xn_ready = (sems(s) for s in ("x_loaded", "norm_step", "std_done", "xn_ready"))
        xt_psum, xt_ready, projected, trow_ready, srow_ready, dve_out = (sems(s) for s in (
            "xt_psum", "xt_ready", "projected", "trow_ready", "srow_ready", "dve_out"))
        trow_stored, srow_stored = sems("trow_stored"), sems("srow_stored")
        block = ctx.enter_context(nc.Block())
        LOADS = 7

        @block.sync
        def _(sp):
            sp.dma_start(wp[:], Wp.rearrange("(c p) d -> p c d", p=P)).then_inc(w_loaded, 16)
            sp.dma_start(wskip[:], Wskip.rearrange("(c p) d -> p c d", p=P)).then_inc(w_loaded, 16)
            with nc.allow_non_contiguous_dma(reason="256 words, once"):
                for k, a in enumerate((a_src, a_trg)):
                    sp.dma_start(a_cols[:, k, :], a.rearrange("o (c q) f -> (q f) (o c)", c=KD)).then_inc(w_loaded, 16)
            sp.dma_start(bias_b[:], bias.rearrange("(o d) -> o d", o=1).to_broadcast([NP, D])).then_inc(w_loaded, 16)
            sp.dma_start(m["wr"][:], Wr.rearrange("(k p) e -> p k e", p=P)).then_inc(w_loaded, 16)
            sp.dma_start(m["br"][:], br.rearrange("(o e) -> o e", o=1).to_broadcast([NP, NX])).then_inc(w_loaded, 16)
            with sp.Fori(0, NT // 2) as i:
                for u in range(2):
                    sp.wait_ge(xn_ready[u], i)
                    sp.dma_start(xin[:, u, :], x[tile(2 * i + u), :]).then_inc(x_loaded[u], 16)

        @block.vector
        def _(dve):
            nc.vector.memset(a_heads[:], 0.0).then_inc(heads_zero, 1)
            nc.vector.memset(maxima[:], -3e38).then_inc(heads_zero, 1)
            dve.wait_ge(w_loaded, 16 * LOADS)
            dve.wait_ge(heads_zero, 2)
            for k in range(2):
                for c in range(KD):
                    for q in range(P // FO):
                        at = slice(q * FO, (q + 1) * FO)
                        h = k * H + c * (P // FO) + q
                        nc.vector.tensor_copy(a_heads[at, c, h:h + 1], a_cols[at, k, c:c + 1]).then_inc(heads, 1)
            for k in range(KD):
                dve.wait_ge(w_turned, k + 1)
                for w, b, s in ((w_table, 3 * k, 0), (w_skip, 3 * k + 1, H)):
                    nc.vector.tensor_copy(w[:, k, 0:D], bank[b][:, 0:D]).then_inc(w_ready, 1)
                    nc.vector.tensor_copy(w[:, k, D:ROW], bank[3 * k + 2][:, s:s + H]).then_inc(w_ready, 1)
            with dve.Fori(0, NT // 2) as i:
                for u in range(2):
                    dve.wait_ge(x_loaded[u], 16 * (i + 1))
                    nc.vector.bn_stats(stats[:, u, :], xin[:, u, :]).then_inc(norm_step[u], 1)
                    after = value_of(dve, 3 * i + 1)
                    dve.wait_ge(begun, 1)
                    dve.wait_ge(norm_step[u], after)
                    nc.vector.bn_aggr(mv[:, u, :], stats[:, u, :]).then_inc(norm_step[u], 1)
                    dve.wait_ge(std_done[u], i + 1)
                    nc.vector.reciprocal(rstd[:, u:u + 1], std[:, u:u + 1]).then_inc(norm_step[u], 1)
                    dve.wait_ge(norm_step[u], 3 * i + 3)
                    dve.wait_ge(xt_psum[u], i)
                    nc.vector.tensor_scalar(xn[:, u, :], xin[:, u, :], mv[:, u, 0:1], rstd[:, u:u + 1],
                                            ALU.subtract, ALU.mult).then_inc(xn_ready[u], 1)
                for u in range(2):
                    t = 2 * i + u
                    ps = bank[4 + u]
                    dve.wait_ge(projected[u], i + 1)
                    dve.wait_ge(srow_stored[u], 16 * i)
                    nc.vector.tensor_tensor(srow[:, u, :], ps[0:NP, 0:D], bias_b[:], ALU.add
                                            ).then_inc(srow_ready[u], 1)
                    nc.vector.tensor_copy(m["st"][:, bass.ds(t, 1), 0:H].rearrange("p a h -> p (a h)"),
                                          ps[0:NP, D:ROW])
                    dve.wait_ge(dve_out[1 - u], 2 * i + 2 * u)
                    dve.wait_ge(trow_ready[u], i + 1)
                    nc.vector.tensor_tensor(maxima[:, 0, :], maxima[:, 0, :], trow[:, u, D:ROW], ALU.max
                                            ).then_inc(dve_out[u], 1)
                    nc.vector.tensor_tensor(maxima[:, 1, :], maxima[:, 1, :], ps[0:NP, D:ROW], ALU.max
                                            ).then_inc(dve_out[u], 1)
            dve.wait_ge(dve_out[1], NT)
            nc.vector.tensor_reduce(top[0:NP, :], maxima[:], X, ALU.max).then_inc(max_step, 1)
            dve.wait_ge(max_pe, 1)
            nc.vector.tensor_reduce(bound[0:2, 0:1], bank[6][0:2, 0:NP], X, ALU.max).then_inc(max_step, 1)
            dve.wait_ge(max_pe, 2)
            nc.vector.tensor_copy(bound[:, 1:2], bank[7][:, 0:1]).then_inc(max_step, 1)
            dve.wait_ge(max_step, 3)
            nc.vector.tensor_scalar(top[:, 0:1], bound[:, 1:2], SLOPE, None, ALU.mult).then_inc(max_step, 1)
            dve.wait_ge(max_step, 4)
            nc.vector.tensor_tensor(top[:, 1:2], top[:, 0:1], bound[:, 1:2], ALU.max).then_inc(max_step, 1)
            dve.wait_ge(max_step, 5)
            nc.vector.tensor_scalar(m["neg_bound"][:], top[:, 1:2], -1.0, None, ALU.mult)

        @block.tensor
        def _(pe):
            pe.wait_ge(w_loaded, 16 * LOADS)
            for k in range(KD):
                at = slice(k * P, (k + 1) * P)
                for c in range(KD):
                    nc.tensor.transpose(bank[3 * k][:, c * P:(c + 1) * P], wp[:, c, at], m["ident"][:])
                    nc.tensor.transpose(bank[3 * k + 1][:, c * P:(c + 1) * P], wskip[:, c, at], m["ident"][:])
                if k == 0:
                    pe.wait_ge(heads, 2 * H)
                for c in range(KD):
                    mm = nc.tensor.matmul(bank[3 * k + 2][:, 0:2 * H], wp[:, c, at], a_heads[:, c, :],
                                          start=(c == 0), stop=(c == KD - 1))
                mm.then_inc(w_turned, 1)
            pe.wait_ge(w_ready, 4 * KD)
            with pe.Fori(0, NT // 2) as i:
                for u in range(2):
                    pe.wait_ge(xn_ready[u], i + 1)
                    pe.wait_ge(xt_ready[u], i)
                    for k in range(KD):
                        mm = nc.tensor.transpose(bank[u][:, k * P:k * P + NP], xn[:, u, k * P:(k + 1) * P],
                                                 m["ident"][0:NP, 0:NP])
                    mm.then_inc(xt_psum[u], 1)
                for u in range(2):
                    pe.wait_ge(xt_ready[u], i + 1)
                    pe.wait_ge(trow_ready[u], i)
                    pe.wait_ge(dve_out[u], 2 * i)
                    for w, b in ((w_table, 2 + u), (w_skip, 4 + u)):
                        for k in range(KD):
                            mm = nc.tensor.matmul(bank[b][0:NP, 0:ROW], xt[:, u, k, :], w[:, k, :],
                                                  start=(k == 0), stop=(k == KD - 1))
                    mm.then_inc(projected[u], 1)
            pe.wait_ge(max_step, 1)
            nc.tensor.transpose(bank[6][0:2, 0:NP], top[0:NP, :], m["ident"][0:NP, 0:NP]).then_inc(max_pe, 1)
            pe.wait_ge(max_step, 2)
            nc.tensor.matmul(bank[7][:, 0:1], m["ones"][0:2, :], bound[0:2, 0:1], start=True,
                             stop=True).then_inc(max_pe, 1)

        @block.scalar
        def _(act):
            with act.Fori(0, NT // 2) as i:
                for u in range(2):
                    act.wait_ge(norm_step[u], 3 * i + 2)
                    nc.scalar.activation(std[:, u:u + 1], mv[:, u, 1:2], ACT.Sqrt, bias=m["ln_eps"][0:NP, :]
                                         ).then_inc(std_done[u], 1)
                for u in range(2):
                    act.wait_ge(xt_psum[u], i + 1)
                    act.wait_ge(projected[u], i)
                    nc.scalar.copy(xt[:, u, :, :], bank[u][:, 0:KD * P].rearrange("p (k n) -> p k n", k=KD)[:, :, 0:NP]
                                   ).then_inc(xt_ready[u], 1)
                for u in range(2):
                    t = 2 * i + u
                    act.wait_ge(projected[u], i + 1)
                    act.wait_ge(trow_stored[u], 16 * i)
                    act.wait_ge(dve_out[u], 2 * i)
                    nc.scalar.copy(trow[:, u, :], bank[2 + u][0:NP, 0:ROW]).then_inc(trow_ready[u], 1)
                    act.wait_ge(trow_ready[u], i + 1)
                    act.dma_start(table[tile(t), :], trow[:, u, :]).then_inc(trow_stored[u], 16)
                    act.wait_ge(srow_ready[u], i + 1)
                    act.dma_start(skip_rows[tile(t), :], srow[:, u, :]).then_inc(srow_stored[u], 16)
            for u in range(2):
                act.wait_ge(trow_stored[u], 16 * (NT // 2))
                act.wait_ge(srow_stored[u], 16 * (NT // 2))


def edge_phase(nc, m, bank, table):
    with ExitStack() as ctx:
        def sb(name, shape, dt=F32):
            return ctx.enter_context(nc.sbuf_tensor(name, shape, dt))

        def sem(name):
            return ctx.enter_context(nc.semaphore(name))

        def sems(name, n=G):
            return [sem(f"{name}{k}") for k in range(n)]

        idx = [sb(f"idx{k}", [P, G // 2], I32) for k in range(2)]
        rows = [sb(f"rows{j}", [P, ROW]) for j in range(G)]
        weighed = [sb(f"weighed{j}", [P, ROW]) for j in range(G)]
        onehot = [sb(f"onehot{j}", [P, NP]) for j in range(G)]
        onehot_t = [sb(f"onehot_t{j}", [NP, P]) for j in range(G)]
        exps = [sb(f"exps{j}", [P, 2, H]) for j in range(G)]
        top, peak = sb("edge_top", [P, 1]), sb("peak", [1, 1])
        acc_bank, turn_bank, z_bank = bank[0], bank[1:3], bank[4:8]
        idx_ready = sems("idx_ready", 2)
        gathered, onehot_ready, turned, turn_copied, z_ready, weight_ready, exp_ready, weighed_ready, max_done, summed = (
            sems(s) for s in ("gathered", "onehot_ready", "turned", "turn_copied", "z_ready", "weight_ready",
                              "exp_ready", "weighed_ready", "max_done", "summed"))
        begun = m["begun"]
        block_summed, acc_copied, peak_dve, peak_pe = sem("block_summed"), sem("acc_copied"), sem("peak_dve"), sem("peak_pe")
        block = ctx.enter_context(nc.Block())

        def block_range(engine, b):
            _, got = nc.values_load_multi_w_load_instructions(
                m["ranges"][0:1, bass.ds(b, 1), 0:3].rearrange("p a k -> p (a k)"),
                engines=[engine.engine], min_val=0, max_val=NT * NSUB)
            return got

        def edge_column(engine, g, first, lo):
            return nc.s_assert_within(engine.snap((g - first) * G + lo), 0, COLS - G)

        @block.gpsimd
        def _(pool):
            with pool.Fori(0, NT) as b:
                lo, first, end = block_range(pool, b)
                with pool.Fori(first, end) as g:
                    col = edge_column(pool, g, first, lo)
                    after = value_of(pool, g + 1)

                    def load_idx(k):
                        for j in (2 * k, 2 * k + 1):
                            pool.wait_ge(gathered[j], 16 * g)
                        nc.gpsimd.tensor_copy(idx[k][:], m["src_tab"][:, bass.ds(col + 2 * k, 2)]).then_inc(idx_ready[k], 1)

                    for j in range(G):
                        if j == 0:
                            load_idx(0)
                        if j == 2:
                            load_idx(1)
                        pool.wait_ge(begun, 1)
                        if j % 2 == 0:
                            pool.wait_ge(idx_ready[j // 2], after)
                        pool.wait_ge(weighed_ready[j], g)
                        nc.gpsimd.indirect_dma_start(
                            rows[j][:], None, table,
                            bass.IndirectOffsetOnAxis(ap=idx[j // 2][:, j % 2:j % 2 + 1], axis=0)
                        ).then_inc(gathered[j], 16)

        @block.tensor
        def _(pe):
            with pe.Fori(0, NT) as b:
                lo, first, end = block_range(pe, b)
                pe.wait_ge(acc_copied, b)
                nc.tensor.matmul(acc_bank[0:NP, 0:ROW], m["zero16"][:, 0:NP], m["zero16"][:], start=True,
                                 stop=False, skip_group_check=True)
                with pe.Fori(first, end) as g:

                    def turn(j):
                        pe.wait_ge(onehot_ready[j], g + 1)
                        pe.wait_ge(turn_copied[(j + 2) % G], g + 1 if j >= 2 else g)
                        nc.tensor.transpose(turn_bank[j % 2][0:NP, 0:P], onehot[j][:], m["ident"][:]
                                            ).then_inc(turned[j], 1)

                    def target_scores(j):
                        pe.wait_ge(turn_copied[j], g + 1)
                        pe.wait_ge(max_done[j], g)
                        nc.tensor.matmul(z_bank[j][:, 0:H + 1], onehot_t[j][:],
                                         m["st"][:, bass.ds(b, 1), :].rearrange("p a h -> p (a h)"),
                                         start=True, stop=False, skip_group_check=True)

                    def source_scores(j):
                        pe.wait_ge(gathered[j], 16 * (g + 1))
                        nc.tensor.matmul(z_bank[j][:, 0:H], m["ident"][:], rows[j][:, D:ROW], start=False,
                                         stop=True, skip_group_check=True).then_inc(z_ready[j], 1)

                    def sum_up(j):
                        pe.wait_ge(weighed_ready[j], g + 1)
                        nc.tensor.matmul(acc_bank[0:NP, 0:ROW], onehot[j][:], weighed[j][:], start=False,
                                         stop=False, skip_group_check=True).then_inc(summed[j], 1)

                    turn(0)
                    turn(1)
                    target_scores(0)
                    source_scores(0)
                    target_scores(1)
                    source_scores(1)
                    turn(2)
                    target_scores(2)
                    sum_up(0)
                    source_scores(2)
                    turn(3)
                    target_scores(3)
                    sum_up(1)
                    source_scores(3)
                    sum_up(2)
                    sum_up(3)
                nc.tensor.matmul(acc_bank[0:NP, 0:ROW], m["zero16"][:, 0:NP], m["zero16"][:], start=False,
                                 stop=True, skip_group_check=True).then_inc(block_summed, 1)
            pe.wait_ge(peak_dve, 1)
            nc.tensor.transpose(bank[1][0:1, 0:P], top[:], m["ident"][:]).then_inc(peak_pe, 1)
            pe.wait_ge(peak_dve, 2)
            nc.tensor.matmul(bank[2][:, 0:1], m["ones"][0:1, :], peak[:], start=True, stop=True).then_inc(peak_pe, 1)

        @block.vector
        def _(dve):
            with dve.Fori(0, NT) as b:
                lo, first, end = block_range(dve, b)
                with dve.Fori(first, end) as g:
                    col = edge_column(dve, g, first, lo)

                    def compare(j):
                        dve.wait_ge(summed[j], g)
                        nc.vector.tensor_scalar(onehot[j][:], m["iota"][:, 0:NP], m["dst_tab"][:, bass.ds(col + j, 1)],
                                                m["neg_block"][:, bass.ds(b, 1)], ALU.subtract,
                                                ALU.is_equal).then_inc(onehot_ready[j], 1)

                    compare(0)
                    compare(1)
                    for j in range(G):
                        if j + 2 < G:
                            compare(j + 2)
                        dve.wait_ge(exp_ready[j], 2 * (g + 1))
                        nc.vector.tensor_tensor(weighed[j][:, D:ROW], exps[j][:, 0, :], exps[j][:, 1, :], ALU.max
                                                ).then_inc(weight_ready[j], 1)
                        dve.wait_ge(weight_ready[j], g + 1)
                        nc.vector.tensor_tensor(
                            weighed[j][:, 0:D].rearrange("p (h f) -> p h f", h=H),
                            rows[j][:, 0:D].rearrange("p (h f) -> p h f", h=H),
                            weighed[j][:, D:ROW].unsqueeze(2).to_broadcast([P, H, FO]), ALU.mult
                        ).then_inc(weighed_ready[j], 1)
                        dve.wait_ge(max_done[(j - 1) % G], g + 1 if j else g)
                        nc.vector.scalar_tensor_tensor(m["runmax"][:], weighed[j][:, D:ROW], z_bank[j][:, H:H + 1],
                                                       m["runmax"][:], ALU.mult, ALU.max).then_inc(max_done[j], 1)
                dve.wait_ge(max_done[G - 1], end)
            dve.wait_ge(block_summed, NT)
            nc.vector.tensor_reduce(top[:], m["runmax"][:], X, ALU.max).then_inc(peak_dve, 1)
            dve.wait_ge(peak_pe, 1)
            nc.vector.tensor_reduce(peak[:], bank[1][0:1, 0:P], X, ALU.max).then_inc(peak_dve, 1)
            dve.wait_ge(peak_pe, 2)
            nc.vector.tensor_scalar(m["eps"][:], bank[2][:, 0:1], DEN_EPS, None, ALU.mult)

        @block.scalar
        def _(act):
            with act.Fori(0, NT) as b:
                lo, first, end = block_range(act, b)
                with act.Fori(first, end) as g:

                    def copy_turned(j):
                        act.wait_ge(turned[j], g + 1)
                        nc.scalar.copy(onehot_t[j][:], turn_bank[j % 2][0:NP, 0:P]).then_inc(turn_copied[j], 1)

                    def exponentials(j):
                        act.wait_ge(z_ready[j], g + 1)
                        act.wait_ge(weight_ready[j], g)
                        for k, slope in enumerate((1.0, SLOPE)):
                            nc.scalar.activation(exps[j][:, k, :], z_bank[j][:, 0:H], ACT.Exp, scale=slope,
                                                 bias=m["neg_bound"][:]).then_inc(exp_ready[j], 1)

                    copy_turned(0)
                    copy_turned(1)
                    exponentials(0)
                    copy_turned(2)
                    exponentials(1)
                    copy_turned(3)
                    exponentials(2)
                    exponentials(3)
                act.wait_ge(block_summed, b + 1)
                nc.scalar.copy(m["acc"][:, bass.ds(b, 1), :].rearrange("p a d -> p (a d)"), acc_bank[0:NP, 0:ROW]
                               ).then_inc(acc_copied, 1)


def route_phase(nc, m, bank, x, skip_rows, xg):
    with ExitStack() as ctx:
        def sb(name, shape, dt=F32):
            return ctx.enter_context(nc.sbuf_tensor(name, shape, dt))

        def sem(name):
            return ctx.enter_context(nc.semaphore(name))

        def sems(name, n=2):
            return [sem(f"{name}{k}") for k in range(n)]

        xin, skin = sb("r_xin", [NP, 2, D]), sb("r_skip", [NP, 2, D])
        den = sb("den", [NP, 2, H])
        att, low, ex = sb("att", [NP, 2, D]), sb("low", [NP, 2, D]), sb("ex", [NP, 2, D])
        stats, mv = sb("r_stats", [NP, 2, 6]), sb("r_mv", [NP, NT, 2])
        mv_tile = sb("mv_tile", [NP, 2])
        std1, rstd1, var2, std2, rstd2 = (sb(s, [NP, NT]) for s in ("std1", "rstd1", "var2", "std2", "rstd2"))
        xl, xlt, xn = sb("xl", [NP, 2, D]), sb("xlt", [P, 2, KD, NP]), sb("r_xn", [NP, 2, 2, XROW])
        logits, top8, pick8 = sb("logits", [NP, NX]), sb("top8", [NP, 8]), sb("pick8", [NP, 8], U32)
        pick = sb("pick", [NP, 2])
        one = sb("one", [NP, 2, NX])
        mask, before, rank = sb("mask", [NP, NX]), sb("before", [NP, NX]), sb("rank", [NP, NX])
        place, junk = sb("place", [NP, 2]), sb("junk", [NP, 2, NX])
        slot = [[sb(f"slot{u}{k}", [NP, 1], I32) for k in range(2)] for u in range(2)]
        padding = sb("padding", [P, FILL // P, XROW])
        crow, cwhole = sb("count_row", [1, 6, NX]), sb("count_whole", [1, NX], I32)
        wtmp = sb("wtmp", [NP, NT])

        begun = m["begun"]
        loaded = sems("r_loaded")
        res_step, dve_step, norm_dve, norm_act, end_step = (
            sem(s) for s in ("res_step", "route_step", "norm_dve", "norm_act", "end_step"))
        low_ready, ex_ready, xl_ready, xlt_psum, xlt_ready, xn_ready, logit_psum, mask_ready, ranked = (sems(s) for s in (
            "low_ready", "ex_ready", "xl_ready", "xlt_psum", "xlt_ready", "r_xn_ready", "logit_psum", "mask_ready",
            "ranked"))
        x_used, slot_ready, sent = sems("x_used"), sems("slot_ready"), sems("sent")
        zero_ready, counted, count_ready, filled = (
            sem(s) for s in ("zero_ready", "counted", "count_ready", "filled"))
        block = ctx.enter_context(nc.Block())

        @block.sync
        def _(sp):
            with sp.Fori(0, NT // 2) as i:
                for u in range(2):
                    sp.wait_ge(x_used[u], i)
                    sp.dma_start(xin[:, u, :], x[tile(2 * i + u), :]).then_inc(loaded[u], 16)
                    sp.dma_start(skin[:, u, :], skip_rows[tile(2 * i + u), :]).then_inc(loaded[u], 16)
            sp.wait_ge(zero_ready, 1 + FILL // P)
            sp.wait_ge(count_ready, 1)
            with sp.Fori(0, NX) as e:
                n = nc.values_load(m["counts"][0:1, bass.ds(e, 1), 0:1].rearrange("p a k -> p (a k)"),
                                   engines=[sp.engine], min_val=0, max_val=N)
                sp.dma_start(xg[bass.ds(e * CAP + n, FILL), :].rearrange("(h p) d -> p h d", p=P), padding[:]
                             ).then_inc(filled, 16)
            sp.wait_ge(filled, 16 * NX)

        @block.vector
        def _(dve):
            nc.vector.memset(padding[:, :, 0:D], 0.0).then_inc(zero_ready, 1)
            for h in range(FILL // P):
                nc.vector.tensor_scalar(padding[:, h, D:XROW], m["iota_p"][:], float(2 * N), None, ALU.add
                                        ).then_inc(zero_ready, 1)
            nc.vector.memset(before[:], 0.0).then_inc(zero_ready, 1)
            RES_STEPS = 14
            with dve.Fori(0, NT // 2) as i:
                steps = [0]

                def step(ins):
                    steps[0] += 1
                    ins.then_inc(res_step, 1)

                def settle(constant=None):
                    count = value_of(dve, steps[0] + i * RES_STEPS)
                    if constant is not None:
                        dve.wait_ge(constant, 1)
                    dve.wait_ge(res_step, count)

                for u in range(2):
                    t = 2 * i + u
                    x1 = m["acc"][:, bass.ds(t, 1), 0:D].rearrange("p a d -> p (a d)")
                    sums = m["acc"][:, bass.ds(t, 1), D:ROW].rearrange("p a d -> p (a d)")
                    step(nc.vector.tensor_scalar(den[:, u, :], sums, m["eps"][0:NP, :], None, ALU.add))
                    settle()
                    step(nc.vector.reciprocal(den[:, u, :], den[:, u, :]))
                    settle()
                    step(nc.vector.tensor_tensor(
                        att[:, u, :].rearrange("p (h f) -> p h f", h=H), x1.rearrange("p (h f) -> p h f", h=H),
                        den[:, u, :].unsqueeze(2).to_broadcast([NP, H, FO]), ALU.mult))
                    settle()
                    dve.wait_ge(loaded[u], 32 * (i + 1))
                    step(nc.vector.tensor_tensor(att[:, u, :], att[:, u, :], skin[:, u, :], ALU.add))
                    settle()
                    nc.vector.tensor_scalar(low[:, u, :], att[:, u, :], 0.0, None, ALU.min
                                            ).then_inc(low_ready[u], 1)
                for u in range(2):
                    t = 2 * i + u
                    x1 = m["acc"][:, bass.ds(t, 1), 0:D].rearrange("p a d -> p (a d)")
                    dve.wait_ge(ex_ready[u], i + 1)
                    step(nc.vector.scalar_tensor_tensor(att[:, u, :], att[:, u, :], 0.0, ex[:, u, :], ALU.max, ALU.add))
                    settle()
                    nc.vector.scalar_tensor_tensor(x1, att[:, u, :], -1.0, xin[:, u, :], ALU.add, ALU.add
                                                   ).then_inc(x_used[u], 1)
                    after = value_of(dve, i + 1)
                    dve.wait_ge(begun, 1)
                    dve.wait_ge(x_used[u], after)
                    step(nc.vector.bn_stats(stats[:, u, :], x1))
                    settle(begun)
                    step(nc.vector.bn_aggr(mv_tile[:], stats[:, u, :]))
                    settle()
                    nc.vector.tensor_copy(m_v(mv, t), mv_tile[:]).then_inc(norm_dve, 1)
                assert steps[0] == RES_STEPS, steps[0]
            dve.wait_ge(norm_act, 1)
            nc.vector.reciprocal(rstd1[:], std1[:]).then_inc(norm_dve, 1)
            dve.wait_ge(norm_dve, NT + 1)
            nc.vector.tensor_tensor(var2[:], rstd1[:], rstd1[:], ALU.mult).then_inc(norm_dve, 1)
            dve.wait_ge(norm_dve, NT + 2)
            nc.vector.tensor_tensor(var2[:], var2[:], mv[:, :, 1], ALU.mult).then_inc(norm_dve, 1)
            dve.wait_ge(norm_act, 2)
            nc.vector.reciprocal(rstd2[:], std2[:]).then_inc(norm_dve, 1)
            PER = 22
            with dve.Fori(0, NT // 2) as i:
                route = [0]

                def step(ins):
                    route[0] += 1
                    ins.then_inc(dve_step, 1)

                def settle(constant=None):
                    count = value_of(dve, route[0] + i * PER)
                    if constant is not None:
                        dve.wait_ge(constant, 1)
                    dve.wait_ge(dve_step, count)

                for u in range(2):
                    t = 2 * i + u
                    x1 = m["acc"][:, bass.ds(t, 1), 0:D].rearrange("p a d -> p (a d)")
                    dve.wait_ge(xlt_psum[u], i)
                    dve.wait_ge(xn_ready[u], i)
                    nc.vector.tensor_scalar(xl[:, u, :], x1, m_v(mv, t)[:, 0:1], rstd1[:, bass.ds(t, 1)],
                                            ALU.subtract, ALU.mult).then_inc(xl_ready[u], 1)
                for u in range(2):
                    t = 2 * i + u
                    dve.wait_ge(logit_psum[u], i + 1)
                    step(nc.vector.tensor_tensor(logits[:], bank[4 + u][0:NP, 0:NX], m["br"][:], ALU.add))
                    settle(begun)
                    step(nc.vector.max(top8[:], logits[:]))
                    settle(begun)
                    step(nc.vector.max_index(pick8[:], top8[:], logits[:]))
                    step(nc.vector.tensor_tensor(m["gaps"][:, bass.ds(t, 1)], top8[:, 1:2], top8[:, 0:1], ALU.subtract))
                    settle()
                    step(nc.vector.tensor_copy(pick[:], pick8[:, 0:2]))
                    settle()
                    for k in range(2):
                        step(nc.vector.tensor_scalar(one[:, k, :], m["iota"][0:NP, 0:NX], pick[:, k:k + 1], None,
                                                     ALU.is_equal))
                    settle()
                    nc.vector.tensor_tensor(mask[:], one[:, 0, :], one[:, 1, :], ALU.add).then_inc(mask_ready[u], 1)
                    dve.wait_ge(ranked[u], i + 1)
                    step(nc.vector.tensor_tensor(rank[:], bank[6 + u][0:NP, 0:NX], m["cap_row"][0:NP, :], ALU.add))
                    step(nc.vector.tensor_tensor(before[:], before[:], mask[:], ALU.add))
                    settle()
                    step(nc.vector.tensor_tensor(junk[:], one[:], rank[:].unsqueeze(1).to_broadcast([NP, 2, NX]),
                                                 ALU.mult))
                    settle()
                    step(nc.vector.tensor_reduce(place[:], junk[:], X, ALU.add))
                    settle()
                    dve.wait_ge(sent[u], 32 * i)
                    for k in range(2):
                        nc.vector.tensor_copy(slot[u][k][:], place[:, k:k + 1]).then_inc(slot_ready[u], 1)
                    nc.vector.tensor_copy(xn[:, u, :, D:XROW].rearrange("p k o -> p (k o)"),
                                          m["result_row"][:, bass.ds(t, 1), :].rearrange("p a k -> p (a k)")
                                          ).then_inc(slot_ready[u], 1)
                    dve.wait_ge(slot_ready[u], 3 * (i + 1))
                assert route[0] == PER, route[0]
            dve.wait_ge(counted, 1)
            last = [0]

            def then(ins):
                last[0] += 1
                ins.then_inc(end_step, 1)
                dve.wait_ge(end_step, last[0])

            CNT, UP, TILES, GE, GS, ZERO = range(6)
            then(nc.vector.tensor_copy(crow[:, CNT], bank[3][0:1, 0:NX]))
            then(nc.vector.memset(crow[:, ZERO], 0.0))
            then(nc.vector.tensor_scalar(crow[:, UP], crow[:, CNT], 1.0, float(TOK - 1), ALU.max, ALU.add))
            then(nc.vector.tensor_copy(cwhole[:], crow[:, UP]))
            then(nc.vector.tensor_scalar(cwhole[:], cwhole[:], TOK.bit_length() - 1, None, ALU.arith_shift_right))
            then(nc.vector.tensor_copy(crow[:, TILES], cwhole[:]))
            then(nc.vector.tensor_tensor_scan(crow[:, GE], crow[:, TILES], crow[:, ZERO], 0.0, ALU.add, ALU.add))
            then(nc.vector.tensor_tensor(crow[:, GS], crow[:, GE], crow[:, TILES], ALU.subtract))
            for k, r in enumerate((CNT, GS, GE)):
                then(nc.vector.tensor_copy(m["counts"][:, :, k], crow[:, r]))
            nc.vector.tensor_copy(m["counts"][:, :, 3], crow[:, ZERO]).then_inc(count_ready, 1)
            dve.wait_ge(norm_act, 3)
            then(nc.vector.tensor_scalar(wtmp[:], m["gaps"][:], 1.0, None, ALU.add))
            then(nc.vector.reciprocal(m["weights"][:, :, 0], wtmp[:]))
            then(nc.vector.tensor_tensor(m["weights"][:, :, 1], m["weights"][:, :, 0], m["gaps"][:], ALU.mult))

        @block.scalar
        def _(act):
            with act.Fori(0, NT // 2) as i:
                for u in range(2):
                    act.wait_ge(low_ready[u], i + 1)
                    nc.scalar.activation(ex[:, u, :], low[:, u, :], ACT.Exp).then_inc(ex_ready[u], 1)
            act.wait_ge(norm_dve, NT)
            nc.scalar.activation(std1[:], mv[:, :, 1], ACT.Sqrt, bias=m["ln_eps"][0:NP, :]).then_inc(norm_act, 1)
            act.wait_ge(norm_dve, NT + 3)
            nc.scalar.activation(std2[:], var2[:], ACT.Sqrt, bias=m["ln_eps"][0:NP, :]).then_inc(norm_act, 1)
            act.wait_ge(norm_dve, NT + 4)
            with act.Fori(0, NT // 2) as i:
                for u in range(2):
                    act.wait_ge(xlt_psum[u], i + 1)
                    nc.scalar.copy(xlt[:, u, :, :], bank[u][:, 0:KD * P].rearrange("p (k n) -> p k n", k=KD)[:, :, 0:NP]
                                   ).then_inc(xlt_ready[u], 1)
                for u in range(2):
                    act.wait_ge(sent[u], 32 * i)
                    nc.scalar.activation(xn[:, u, :, 0:D], xl[:, u, :].unsqueeze(1).to_broadcast([NP, 2, D]), ACT.Copy,
                                         scale=rstd2[:, bass.ds(2 * i + u, 1)]
                                         ).then_inc(xn_ready[u], 1)
            act.wait_ge(count_ready, 1)
            nc.scalar.activation(m["gaps"][:], m["gaps"][:], ACT.Exp).then_inc(norm_act, 1)

        @block.tensor
        def _(pe):
            pe.wait_ge(zero_ready, 2 + FILL // P)
            with pe.Fori(0, NT // 2) as i:
                for u in range(2):
                    pe.wait_ge(xl_ready[u], i + 1)
                    for k in range(KD):
                        mm = nc.tensor.transpose(bank[u][:, k * P:k * P + NP], xl[:, u, k * P:(k + 1) * P],
                                                 m["ident"][0:NP, 0:NP])
                    mm.then_inc(xlt_psum[u], 1)
                for u in range(2):
                    pe.wait_ge(xlt_ready[u], i + 1)
                    for k in range(KD):
                        mm = nc.tensor.matmul(bank[4 + u][0:NP, 0:NX], xlt[:, u, k, :], m["wr"][:, k, :],
                                              start=(k == 0), stop=(k == KD - 1))
                    mm.then_inc(logit_psum[u], 1)
                for u in range(2):
                    pe.wait_ge(mask_ready[u], i + 1)
                    nc.tensor.matmul(bank[6 + u][0:NP, 0:NX], m["ones"][0:NP, 0:NP], before[:], start=True, stop=False)
                    nc.tensor.matmul(bank[6 + u][0:NP, 0:NX], m["lower"][0:NP, 0:NP], mask[:], start=False,
                                     stop=True).then_inc(ranked[u], 1)
            pe.wait_ge(slot_ready[1], 3 * (NT // 2))
            nc.tensor.matmul(bank[3][0:1, 0:NX], m["ones"][0:NP, 0:1], before[:], start=True,
                             stop=True).then_inc(counted, 1)

        @block.gpsimd
        def _(pool):
            with pool.Fori(0, NT // 2) as i:
                for u in range(2):
                    three, after = value_of(pool, 3 * (i + 1)), value_of(pool, i + 1)
                    pool.wait_ge(begun, 1)
                    pool.wait_ge(slot_ready[u], three)
                    pool.wait_ge(xn_ready[u], after)
                    for k in range(2):
                        nc.gpsimd.indirect_dma_start(
                            xg, bass.IndirectOffsetOnAxis(ap=slot[u][k][:], axis=0), xn[:, u, k, :], None
                        ).then_inc(sent[u], 16)
            for u in range(2):
                pool.wait_ge(sent[u], 32 * (NT // 2))


def expert_phase(nc, m, bank, xg, y2, ln_g, ln_b, W1, b1, W2, b2):
    with ExitStack() as ctx:
        def sb(name, shape, dt=F32):
            return ctx.enter_context(nc.sbuf_tensor(name, shape, dt))

        def sem(name):
            return ctx.enter_context(nc.semaphore(name))

        def sems(name, n=2):
            return [sem(f"{name}{k}") for k in range(n)]

        w1, w2 = sb("w1", [P, 2, KD, HID]), sb("w2", [P, 2, JH, D])
        gain, shift, b1c = sb("gain", [P, 2, KD]), sb("shift", [P, 2, KD]), sb("b1c", [P, 2, JH])
        b2b = sb("b2b", [P, 2, D])
        xrow = sb("xrow", [P, HALF, XROW])
        xt = sb("f_xt", [P, KD, TOK])
        hid = sb("hid", [P, JH, TOK])
        yrow = sb("yrow", [P, HALF, D])
        goes_to = [sb(f"goes_to{h}", [P, 1], I32) for h in range(HALF)]
        x_bank, y_bank, h_bank = bank[0:HALF], bank[5:5 + HALF], [bank[k] for k in (2, 3, 4, 7)]
        HB = len(h_bank)
        w_loaded, w_used = sems("f_w_loaded"), sems("f_w_used")
        row_loaded, row_used, xt_ready, goes_ready, stored, y_psum, y_ready = (sems(s, HALF) for s in (
            "f_row_loaded", "f_row_used", "f_xt_ready", "f_goes_ready", "f_stored", "f_y_psum", "f_y_ready"))
        h_psum, h_ready = sems("f_h_psum", HB), sems("f_h_ready", HB)
        block = ctx.enter_context(nc.Block())
        W_LOADS = 6

        def tiles_of(engine, e):
            _, got = nc.values_load_multi_w_load_instructions(
                m["counts"][0:1, bass.ds(e, 1), 1:3].rearrange("p a k -> p (a k)"),
                engines=[engine.engine], min_val=0, max_val=NX * CAP // TOK)
            return got

        @block.sync
        def _(sp):
            with sp.Fori(0, NX) as e:
                first, end = tiles_of(sp, e)
                with sp.Fori(first, end) as g:
                    row = nc.s_assert_within(sp.snap((g - first) * TOK + e * CAP), 0, NX * CAP - TOK)
                    for h in range(HALF):
                        sp.wait_ge(row_used[h], g)
                        sp.wait_ge(goes_ready[h], g)
                        sp.dma_start(xrow[:, h, :], xg[bass.ds(row + h * P, P), :]).then_inc(row_loaded[h], 16)

        @block.tensor
        def _(pe):
            with pe.Fori(0, NX // 2) as i:
                for s in range(2):
                    first, end = tiles_of(pe, 2 * i + s)
                    with pe.Fori(first, end) as g:
                        for h in range(HALF):
                            pe.wait_ge(row_loaded[h], 16 * (g + 1))
                            pe.wait_ge(xt_ready[h], g)
                            for k in range(KD):
                                mm = nc.tensor.transpose(x_bank[h][:, k * P:(k + 1) * P],
                                                         xrow[:, h, k * P:(k + 1) * P], m["ident"][:])
                            mm.then_inc(row_used[h], 1)
                        pe.wait_ge(w_loaded[s], 16 * W_LOADS * (i + 1))
                        for h in range(HALF):
                            pe.wait_ge(xt_ready[h], g + 1)
                        for j in range(JH):
                            pe.wait_ge(h_ready[j % HB], JH // HB * g + j // HB)
                            for k in range(KD):
                                mm = nc.tensor.matmul(h_bank[j % HB][:, 0:TOK],
                                                      w1[:, s, k, j * P:(j + 1) * P], xt[:, k, :],
                                                      start=(k == 0), stop=(k == KD - 1))
                            mm.then_inc(h_psum[j % HB], 1)
                        for h in range(HALF):
                            pe.wait_ge(y_ready[h], g)
                        for j in range(JH):
                            pe.wait_ge(h_ready[j % HB], JH // HB * g + j // HB + 1)
                            for h in range(HALF):
                                mm = nc.tensor.matmul(y_bank[h][:, 0:D], hid[:, j, h * P:(h + 1) * P],
                                                      w2[:, s, j, :], start=(j == 0), stop=(j == JH - 1))
                                if j == JH - 1:
                                    mm.then_inc(y_psum[h], 1)

        @block.scalar
        def _(act):
            def load(e, s):
                def one(w):
                    return w[bass.ds(e, 1)]

                with nc.allow_non_contiguous_dma(reason="small rows of parameters, once an expert"):
                    for to, of in (
                        (w1[:, s, :, :], one(W1).rearrange("o (k p) h -> p (o k) h", p=P)),
                        (w2[:, s, :, :], one(W2).rearrange("o (j p) d -> p (o j) d", p=P)),
                        (gain[:, s, :], one(ln_g).rearrange("o (k p) -> p (o k)", p=P)),
                        (shift[:, s, :], one(ln_b).rearrange("o (k p) -> p (o k)", p=P)),
                        (b1c[:, s, :], one(b1).rearrange("o (j p) -> p (o j)", p=P)),
                        (b2b[:, s, :], one(b2).to_broadcast([P, D])),
                    ):
                        act.dma_start(to, of).then_inc(w_loaded[s], 16)

            def gelus(e, i, s):
                first, end = tiles_of(act, e)
                with act.Fori(first, end) as g:
                    act.wait_ge(w_loaded[s], 16 * W_LOADS * (i + 1))
                    for j in range(JH):
                        act.wait_ge(h_psum[j % HB], JH // HB * g + j // HB + 1)
                        nc.scalar.activation(hid[:, j, :], h_bank[j % HB][:, 0:TOK], ACT.Gelu,
                                             bias=b1c[:, s, j:j + 1]).then_inc(h_ready[j % HB], 1)

            load(0, 0)
            with act.Fori(0, NX // 2 - 1) as i:
                act.wait_ge(w_used[1], i)
                load(2 * i + 1, 1)
                gelus(2 * i, i, 0)
                act.wait_ge(w_used[0], i + 1)
                load(2 * i + 2, 0)
                gelus(2 * i + 1, i, 1)
            act.wait_ge(w_used[1], NX // 2 - 1)
            load(NX - 1, 1)
            gelus(NX - 2, NX // 2 - 1, 0)
            gelus(NX - 1, NX // 2 - 1, 1)

        @block.vector
        def _(dve):
            with dve.Fori(0, NX // 2) as i:
                for s in range(2):
                    first, end = tiles_of(dve, 2 * i + s)
                    with dve.Fori(first, end) as g:
                        dve.wait_ge(w_loaded[s], 16 * W_LOADS * (i + 1))
                        dve.wait_ge(h_psum[HB - 1], JH // HB * g)
                        for h in range(HALF):
                            dve.wait_ge(row_used[h], g + 1)
                            for k in range(KD):
                                ins = nc.vector.tensor_scalar(xt[:, k, h * P:(h + 1) * P],
                                                              x_bank[h][:, k * P:(k + 1) * P],
                                                              gain[:, s, k:k + 1], shift[:, s, k:k + 1],
                                                              ALU.mult, ALU.add)
                            ins.then_inc(xt_ready[h], 1)
                        for h in range(HALF):
                            dve.wait_ge(stored[h], 16 * g)
                            nc.vector.tensor_copy(goes_to[h][:], xrow[:, h, D:XROW]).then_inc(goes_ready[h], 1)
                        for h in range(HALF):
                            dve.wait_ge(y_psum[h], g + 1)
                            nc.vector.tensor_tensor(yrow[:, h, :], y_bank[h][:, 0:D], b2b[:, s, :], ALU.add
                                                    ).then_inc(y_ready[h], 1)
                    for h in range(HALF):
                        dve.wait_ge(y_ready[h], end)
                    dve.sem_inc(w_used[s], 1)

        @block.gpsimd
        def _(pool):
            with pool.Fori(0, NX) as e:
                first, end = tiles_of(pool, e)
                with pool.Fori(first, end) as g:
                    after = value_of(pool, g + 1)
                    sent, sent_after = value_of(pool, 16 * g), value_of(pool, 16 * (g + 1))
                    for h in range(HALF):
                        pool.wait_ge(m["begun"], 1)
                        pool.wait_ge(goes_ready[h], after)
                        pool.wait_ge(y_ready[h], after)
                        pool.wait_ge(stored[0], sent_after if h else sent)
                        pool.wait_ge(stored[1], sent)
                        nc.gpsimd.indirect_dma_start(
                            y2, bass.IndirectOffsetOnAxis(ap=goes_to[h][:], axis=0), yrow[:, h, :], None
                        ).then_inc(stored[h], 16)
                for h in range(HALF):
                    pool.wait_ge(stored[h], end * 16)


def combine_phase(nc, m, y2, out):
    with ExitStack() as ctx:
        def sb(name, shape, dt=F32):
            return ctx.enter_context(nc.sbuf_tensor(name, shape, dt))

        def sems(name, n=2):
            return [ctx.enter_context(nc.semaphore(f"{name}{k}")) for k in range(n)]

        y, mid, total = sb("c_y", [NP, 2, 2, D]), sb("c_mid", [NP, 2, D]), sb("c_total", [NP, 2, D])
        loaded, summed, stored = sems("c_loaded"), sems("c_summed"), sems("c_stored")
        block = ctx.enter_context(nc.Block())

        @block.sync
        def _(sp):
            with sp.Fori(0, NT // 2) as i:
                for u in range(2):
                    sp.wait_ge(summed[u], 2 * i)
                    sp.dma_start(y[:, u, :, :], y2[bass.ds((2 * i + u) * 2 * NP, 2 * NP), :]
                                 .rearrange("(p k) d -> p k d", k=2)).then_inc(loaded[u], 16)

        @block.vector
        def _(dve):
            with dve.Fori(0, NT // 2) as i:
                for u in range(2):
                    t = 2 * i + u
                    w = m["weights"][:, bass.ds(t, 1), :].rearrange("p a k -> p (a k)")
                    dve.wait_ge(loaded[u], 16 * (i + 1))
                    nc.vector.scalar_tensor_tensor(
                        mid[:, u, :], y[:, u, 0, :], w[:, 0:1], m["acc"][:, bass.ds(t, 1), 0:D].rearrange("p a d -> p (a d)"),
                        ALU.mult, ALU.add).then_inc(summed[u], 1)
                    dve.wait_ge(summed[u], 2 * i + 1)
                    dve.wait_ge(stored[u], 16 * i)
                    nc.vector.scalar_tensor_tensor(total[:, u, :], y[:, u, 1, :], w[:, 1:2], mid[:, u, :],
                                                   ALU.mult, ALU.add).then_inc(summed[u], 1)

        @block.scalar
        def _(act):
            with act.Fori(0, NT // 2) as i:
                for u in range(2):
                    act.wait_ge(summed[u], 2 * (i + 1))
                    act.dma_start(out[tile(2 * i + u), :], total[:, u, :]).then_inc(stored[u], 16)
            for u in range(2):
                act.wait_ge(stored[u], 16 * (NT // 2))


_INS = ['x', 'src', 'dst', 'L0_gnn_Wp', 'L0_gnn_a_src', 'L0_gnn_a_trg', 'L0_gnn_Wskip', 'L0_gnn_bias',
        'L0_ffn_Wr', 'L0_ffn_br', 'L0_ffn_ln_g', 'L0_ffn_ln_b', 'L0_ffn_W1', 'L0_ffn_b1', 'L0_ffn_W2', 'L0_ffn_b2']


def kernel(**inputs):
    import numpy as _np
    import concourse.bacc as _bacc
    from concourse import mybir as _mybir
    from concourse.bass_utils import run_bass_kernel_spmd as _run

    nc = _bacc.Bacc("TRN2", target_bir_lowering=False, num_devices=1)
    arrays, args = {}, []
    for name in _INS:
        a = _np.ascontiguousarray(inputs[name])
        arrays[f"in_{name}_dram"] = a
        args.append(nc.dram_tensor(f"in_{name}_dram", a.shape, _mybir.dt.from_np(a.dtype), kind="ExternalInput").ap())
    args.append(nc.dram_tensor("out_0_dram", (N, D), _mybir.dt.float32, kind="ExternalOutput").ap())
    gnn_ffn(nc, *args)
    r = _run(nc, [arrays], core_ids=[0])
    return r.results[0]["out_0_dram"]
```

```python
from contextlib import ExitStack

import concourse.bass as bass
from concourse import mybir

F32 = mybir.dt.float32
F32R = mybir.dt.float32r
BF16 = mybir.dt.bfloat16
I32 = mybir.dt.int32
U32 = mybir.dt.uint32
ALU = mybir.AluOpType
ACT = mybir.ActivationFunctionType
X = mybir.AxisListType.X

P = 128
N, D = 6250, 256
E = 200000
H, FO = 8, 32
NX, HID = 8, 1024
LN_EPS = 1e-5
SLOPE = 0.2
DEN_EPS = 1e-16

NP = 125
NT = N // NP
KD = D // P
ROW = D + H

SUB = 128
SET, K = 3, 3
G = SET * K
DIV_BITS = 14
DIV_BY = -(-(1 << DIV_BITS) // G)
Q = 4
EROW = Q * SUB
ST = H + 2
NSUB = -(-E // SUB)
EC = -(-E // (P * EROW))
EFULL = E // EROW
ETAIL = E - EFULL * EROW
COLS = EC * P * Q
NO_NODE = 16384
BIG = 4096

BY_TABLE = "the chip's own tables hold it, clamped to this range"

TOK = 256
HALF = TOK // P
JH = HID // P
CAP = -(-(N + TOK) // TOK) * TOK
FILL = TOK
XROW = D + 1


def tile(t, n=NP):
    return bass.ds(t * n, n)


def value_of(engine, count):
    return engine.snap(engine.to_reg(count))


def m_v(mv, t):
    return mv[:, bass.ds(t, 1), :].rearrange("p a k -> p (a k)")


def gnn_ffn(nc, x, src, dst, Wp, a_src, a_trg, Wskip, bias, Wr, br, ln_g, ln_b, W1, b1, W2, b2, out):
    table = nc.dram_tensor("proj_table", (N, ROW), F32).ap()
    skip_rows = nc.dram_tensor("skip_rows", (N, D), F32).ap()
    xg = nc.dram_tensor("tokens_by_expert", (NX * CAP, XROW), F32).ap()
    y2 = nc.dram_tensor("results_by_token", (2 * N + P, D), F32).ap()

    with ExitStack() as ctx:
        def sb(name, shape, dt=F32):
            return ctx.enter_context(nc.sbuf_tensor(name, shape, dt))

        bank = [ctx.enter_context(nc.psum_tensor(f"bank{k}", [P, 512], F32)) for k in range(8)]
        m = dict(
            iota=sb("iota", [P, P]), iota_p=sb("iota_p", [P, 1]), ident=sb("ident", [P, P]),
            lower=sb("lower", [P, P]), ones=sb("ones", [P, P]), zero16=sb("zero16", [P, ROW], BF16),
            begun=ctx.enter_context(nc.semaphore("begun")), block_start=sb("block_start", [P, NT + 1]),
            cap_row=sb("cap_row", [P, NX]), ident_r=sb("ident_r", [P, P], F32R),
            st=sb("st", [NP, NT + 1, ST]), st_parts=sb("st_parts", [NP, NT + 1, 2, ST], F32R),
            acc=sb("acc", [NP, NT, ROW]), neg_bound=sb("neg_bound", [P, 1]),
            ln_eps=sb("ln_eps", [P, 1]), eps=sb("eps", [P, 1]),
            gaps=sb("gaps", [NP, NT]), warm=[sb(f"warm{k}", [P, 1]) for k in range(3)], weights=sb("weights", [NP, NT, 2]),
            result_row=sb("result_row", [NP, NT, 2]), counts=sb("counts", [1, NX, 4], I32),
            br=sb("br", [NP, NX]), wr=sb("wr", [P, KD, NX]),
        )
        with ExitStack() as edge_ctx:
            def esb(name, shape, dt=F32):
                return edge_ctx.enter_context(nc.sbuf_tensor(name, shape, dt))

            m.update(src_tab=esb("src_tab", [P, COLS], I32), dst_tab=esb("dst_tab", [P, COLS]),
                     ranges=esb("ranges", [1, NT, 4], I32))
            edge_tables(nc, m, bank, src, dst)
            node_phase(nc, m, bank, x, Wp, a_src, a_trg, Wskip, bias, Wr, br, table, skip_rows)
            edge_phase(nc, m, bank, table)
        route_phase(nc, m, bank, x, skip_rows, xg)
        expert_phase(nc, m, bank, xg, y2, ln_g, ln_b, W1, b1, W2, b2)
        combine_phase(nc, m, y2, out)


def edge_tables(nc, m, bank, src, dst):
    with ExitStack() as ctx:
        def sb(name, shape, dt=F32):
            return ctx.enter_context(nc.sbuf_tensor(name, shape, dt))

        def sem(name):
            return ctx.enter_context(nc.semaphore(name))

        raw = {"src": sb("src_raw", [P, EC, EROW], I32), "dst": sb("dst_raw", [P, EC, EROW], I32)}
        rows = {"src": sb("src_rows", [P, EC, EROW]), "dst": sb("dst_rows", [P, EC, EROW])}
        lowest = sb("lowest", [P, EC * Q])
        highest = sb("highest", [P, EC * Q])
        number = sb("number", [P, EC * Q])
        starts = sb("starts", [P, NT])
        starts_ok = sb("starts_ok", [P, NT, EC * Q])
        touched = sb("touched", [P, NT, EC * Q])
        scored = sb("scored", [P, 2, NT, EC * Q])
        best = sb("best", [P, 2, NT])
        best_col = sb("best_col", [2 * NT, 1])
        row, whole = sb("range_row", [1, 8, NT]), sb("range_whole", [1, NT], I32)
        iota_done, consts, loaded = sem("iota_done"), sem("consts"), sem("edges_loaded")
        pe_input, turned = sem("pe_input"), sem("turned")
        dst_out, src_out = sem("dst_out"), sem("src_out")
        dve_step, pe_step = sem("range_dve"), sem("range_pe")
        iota, ident = m["iota"], m["ident"]

        block = ctx.enter_context(nc.Block())

        @block.gpsimd
        def _(pool):
            nc.gpsimd.iota(iota[:], [[1, P]], base=0, channel_multiplier=0,
                           allow_small_or_imprecise_dtypes=True).then_inc(iota_done, 1)
            nc.gpsimd.iota(m["iota_p"][:], [[0, 1]], base=0, channel_multiplier=1,
                           allow_small_or_imprecise_dtypes=True).then_inc(iota_done, 1)
            nc.gpsimd.iota(m["result_row"][:], [[2 * NP, NT], [1, 2]], base=0, channel_multiplier=2,
                           allow_small_or_imprecise_dtypes=True).then_inc(iota_done, 1)
            nc.gpsimd.iota(number[:], [[P * Q, EC], [1, Q]], base=1, channel_multiplier=Q,
                           allow_small_or_imprecise_dtypes=True).then_inc(iota_done, 1)
            nc.gpsimd.iota(starts[:], [[NP, NT]], base=0, channel_multiplier=0,
                           allow_small_or_imprecise_dtypes=True).then_inc(iota_done, 1)

        @block.sync
        def _(sp):
            sp.wait_ge(consts, 2)
            for name, flat in (("dst", dst), ("src", src)):
                to = raw[name]
                whole = (EC - 1) * P * EROW
                sp.dma_start(to[:, 0:EC - 1, :], flat[0:whole].rearrange("(c p e) -> p c e", p=P, e=EROW)
                             ).then_inc(loaded, 16)
                rest = EFULL - (EC - 1) * P
                sp.dma_start(to[0:rest, EC - 1, :], flat[whole:whole + rest * EROW].rearrange("(p e) -> p e", e=EROW)
                             ).then_inc(loaded, 16)
                sp.dma_start(to[rest:rest + 1, EC - 1, 0:ETAIL], flat[EFULL * EROW:E].rearrange("(p e) -> p e", p=1)
                             ).then_inc(loaded, 16)

        @block.vector
        def _(dve):
            steps = [0]

            def step(ins):
                steps[0] += 1
                ins.then_inc(dve_step, 1)

            def settle():
                dve.wait_ge(dve_step, steps[0])

            nc.vector.memset(raw["dst"][:, EC - 1, :], NO_NODE).then_inc(consts, 1)
            nc.vector.memset(raw["src"][:, EC - 1, :], 0).then_inc(consts, 1)
            nc.vector.memset(m["ones"][:], 1.0).then_inc(m["begun"], 1)
            nc.vector.memset(m["zero16"][:], 0.0)
            nc.vector.memset(m["st"][:], 1.0)
            nc.vector.memset(m["ln_eps"][:], LN_EPS)
            dve.wait_ge(iota_done, 5)
            nc.vector.tensor_scalar(ident[:], iota[:], m["iota_p"][:], None, ALU.is_equal).then_inc(consts, 1)
            nc.vector.tensor_scalar(m["lower"][:], iota[:], m["iota_p"][:], None, ALU.is_gt).then_inc(consts, 1)
            nc.vector.tensor_scalar(m["ident_r"][:], iota[:], m["iota_p"][:], None, ALU.is_equal)
            nc.vector.memset(m["block_start"][:, NT:NT + 1], 0.0)
            nc.vector.tensor_copy(m["block_start"][:, 0:NT], starts[:]).then_inc(consts, 1)
            nc.vector.tensor_scalar(m["cap_row"][:], iota[:, 0:NX], float(CAP), None, ALU.mult).then_inc(consts, 1)
            dve.wait_ge(loaded, 16 * 6)
            for name in ("dst", "src"):
                nc.vector.tensor_copy(rows[name][:], raw[name][:]).then_inc(pe_input, 1)
            for c in range(EC):
                dve.wait_ge(turned, 2 * c + 1)
                nc.vector.tensor_copy(
                    m["dst_tab"][:, c * P * Q:(c + 1) * P * Q].rearrange("p (r j) -> p j r", j=Q),
                    bank[2 * (c % 2)][:].rearrange("p (j r) -> p j r", j=Q)).then_inc(dst_out, 1)
            by_sub = rows["dst"][:].rearrange("p c (j e) -> p (c j) e", j=Q)
            step(nc.vector.tensor_reduce(lowest[:], by_sub, X, ALU.min))
            step(nc.vector.tensor_reduce(highest[:], by_sub, X, ALU.max))
            settle()
            shape = [P, NT, EC * Q]

            def over_blocks(v):
                return v[:].unsqueeze(1).to_broadcast(shape)

            start_b = starts[:].unsqueeze(2).to_broadcast(shape)
            step(nc.vector.tensor_tensor(starts_ok[:], over_blocks(highest), start_b, ALU.is_ge))
            step(nc.vector.tensor_scalar(lowest[:], lowest[:], -float(NP - 1), None, ALU.add))
            settle()
            step(nc.vector.tensor_tensor(touched[:], start_b, over_blocks(lowest), ALU.is_ge))
            settle()
            step(nc.vector.tensor_tensor(touched[:], touched[:], starts_ok[:], ALU.mult))
            settle()
            step(nc.vector.tensor_tensor(scored[:, 0], touched[:], over_blocks(number), ALU.mult))
            settle()
            step(nc.vector.tensor_scalar(number[:], number[:], -1.0, float(BIG), ALU.mult, ALU.add))
            settle()
            step(nc.vector.tensor_tensor(scored[:, 1], touched[:], over_blocks(number), ALU.mult))
            settle()
            nc.vector.tensor_reduce(best[:], scored[:], X, ALU.max).then_inc(pe_input, 1)
            dve.wait_ge(pe_step, 1)
            nc.vector.tensor_reduce(best_col[:], bank[4][0:2 * NT, 0:P], X, ALU.max).then_inc(pe_input, 1)
            dve.wait_ge(pe_step, 2)
            LAST, FIRST, LO, END, CNT, GE, GS, ZERO = range(8)
            step(nc.vector.tensor_copy(row[:, LAST:FIRST + 1, :].rearrange("p a b -> p (a b)"),
                                       bank[5][0:1, 0:2 * NT]))
            step(nc.vector.memset(row[:, ZERO], 0.0))
            settle()
            step(nc.vector.tensor_scalar(row[:, LO], row[:, FIRST], -1.0, float(BIG - 1), ALU.mult, ALU.add))
            settle()
            step(nc.vector.tensor_scalar(row[:, LO], row[:, LO], float(NSUB - 1), 0.0, ALU.min, ALU.max))
            settle()
            step(nc.vector.tensor_tensor(row[:, END], row[:, LAST], row[:, LO], ALU.subtract))
            settle()
            step(nc.vector.tensor_scalar(row[:, END], row[:, END], 1.0, float(G - 1), ALU.max, ALU.add))
            settle()
            step(nc.vector.tensor_scalar(row[:, END], row[:, END], float(DIV_BY), None, ALU.mult))
            settle()
            step(nc.vector.tensor_copy(whole[:], row[:, END]))
            settle()
            step(nc.vector.tensor_scalar(whole[:], whole[:], DIV_BITS, None, ALU.arith_shift_right))
            settle()
            step(nc.vector.tensor_copy(row[:, CNT], whole[:]))
            settle()
            step(nc.vector.tensor_tensor_scan(row[:, GE], row[:, CNT], row[:, ZERO], 0.0, ALU.add, ALU.add))
            settle()
            step(nc.vector.tensor_tensor(row[:, GS], row[:, GE], row[:, CNT], ALU.subtract))
            settle()
            step(nc.vector.tensor_scalar(row[:, GS], row[:, GS], 1.0, None, ALU.add))
            settle()
            for k, r in enumerate((LO, GS, GE)):
                step(nc.vector.tensor_copy(m["ranges"][:, :, k], row[:, r]))
            step(nc.vector.tensor_copy(m["ranges"][:, 0:NT - 1, 3], row[:, LO, 1:NT]))
            step(nc.vector.tensor_copy(m["ranges"][:, NT - 1, 3:4], row[:, LO, NT - 1:NT]))
            settle()

        @block.tensor
        def _(pe):
            pe.wait_ge(consts, 3)
            n = 0
            for c in range(EC):
                for k, name in enumerate(("dst", "src")):
                    if c == 0:
                        pe.wait_ge(pe_input, k + 1)
                    if c >= 2:
                        pe.wait_ge((dst_out, src_out)[k], c - 1)
                    for j in range(Q):
                        mm = nc.tensor.transpose(bank[2 * (c % 2) + k][:, j * P:(j + 1) * P],
                                                 rows[name][:, c, j * P:(j + 1) * P], ident[:])
                    mm.then_inc(turned, 1)
            pe.wait_ge(pe_input, 3)
            nc.tensor.transpose(bank[4][0:2 * NT, 0:P], best[:].rearrange("p a b -> p (a b)"),
                                ident[:]).then_inc(pe_step, 1)
            pe.wait_ge(pe_input, 4)
            nc.tensor.matmul(bank[5][0:1, 0:2 * NT], best_col[:], ident[0:2 * NT, 0:2 * NT],
                             start=True, stop=True).then_inc(pe_step, 1)

        @block.scalar
        def _(act):
            for c in range(EC):
                act.wait_ge(turned, 2 * c + 2)
                nc.scalar.copy(m["src_tab"][:, c * P * Q:(c + 1) * P * Q].rearrange("p (r j) -> p j r", j=Q),
                               bank[2 * (c % 2) + 1][:].rearrange("p (j r) -> p j r", j=Q)).then_inc(src_out, 1)


def node_phase(nc, m, bank, x, Wp, a_src, a_trg, Wskip, bias, Wr, br, table, skip_rows):
    with ExitStack() as ctx:
        def sb(name, shape, dt=F32):
            return ctx.enter_context(nc.sbuf_tensor(name, shape, dt))

        def sem(name):
            return ctx.enter_context(nc.semaphore(name))

        def sems(name, n=2):
            return [sem(f"{name}{k}") for k in range(n)]

        wp, wskip = sb("wp", [P, KD, D]), sb("wskip", [P, KD, D])
        a_cols = sb("a_cols", [P, 2, KD])
        a_heads = sb("a_heads", [P, KD, 2 * H])
        bias_b = sb("bias_b", [NP, D])
        w_table, w_skip = sb("w_table", [P, KD, ROW]), sb("w_skip", [P, KD, ROW])
        xin, xn, xt = sb("xin", [NP, 2, D]), sb("xn", [NP, 2, D]), sb("xt", [P, 2, KD, NP])
        stats, mv = sb("stats", [NP, 2, 6]), sb("mv", [NP, 2, 2])
        std, rstd = sb("std", [NP, 2]), sb("rstd", [NP, 2])
        trow, srow = sb("trow", [NP, 2, ROW]), sb("srow", [NP, 2, D])
        maxima, top, bound = sb("maxima", [NP, 2, H]), sb("top", [P, 2]), sb("bound", [P, 2])
        begun, st_high = m["begun"], sem("st_high")
        w_loaded, heads_zero, heads = sem("w_loaded"), sem("heads_zero"), sem("heads")
        w_turned, w_ready, max_step, max_pe = sem("w_turned"), sem("w_ready"), sem("max_step"), sem("max_pe")
        x_loaded, norm_step, std_done, xn_ready = (sems(s) for s in ("x_loaded", "norm_step", "std_done", "xn_ready"))
        xt_psum, xt_ready, projected, trow_ready, srow_ready, dve_out = (sems(s) for s in (
            "xt_psum", "xt_ready", "projected", "trow_ready", "srow_ready", "dve_out"))
        trow_stored, srow_stored = sems("trow_stored"), sems("srow_stored")
        block = ctx.enter_context(nc.Block())
        LOADS = 7

        @block.sync
        def _(sp):
            sp.dma_start(wp[:], Wp.rearrange("(c p) d -> p c d", p=P)).then_inc(w_loaded, 16)
            sp.dma_start(wskip[:], Wskip.rearrange("(c p) d -> p c d", p=P)).then_inc(w_loaded, 16)
            with nc.allow_non_contiguous_dma(reason="256 words, once"):
                for k, a in enumerate((a_src, a_trg)):
                    sp.dma_start(a_cols[:, k, :], a.rearrange("o (c q) f -> (q f) (o c)", c=KD)).then_inc(w_loaded, 16)
            sp.dma_start(bias_b[:], bias.rearrange("(o d) -> o d", o=1).to_broadcast([NP, D])).then_inc(w_loaded, 16)
            sp.dma_start(m["wr"][:], Wr.rearrange("(k p) e -> p k e", p=P)).then_inc(w_loaded, 16)
            sp.dma_start(m["br"][:], br.rearrange("(o e) -> o e", o=1).to_broadcast([NP, NX])).then_inc(w_loaded, 16)
            with sp.Fori(0, NT // 2) as i:
                for u in range(2):
                    sp.wait_ge(xn_ready[u], i)
                    sp.dma_start(xin[:, u, :], x[tile(2 * i + u), :]).then_inc(x_loaded[u], 16)

        @block.vector
        def _(dve):
            nc.vector.memset(a_heads[:], 0.0).then_inc(heads_zero, 1)
            nc.vector.memset(maxima[:], -3e38).then_inc(heads_zero, 1)
            dve.wait_ge(w_loaded, 16 * LOADS)
            dve.wait_ge(heads_zero, 2)
            for k in range(2):
                for c in range(KD):
                    for q in range(P // FO):
                        at = slice(q * FO, (q + 1) * FO)
                        h = k * H + c * (P // FO) + q
                        nc.vector.tensor_copy(a_heads[at, c, h:h + 1], a_cols[at, k, c:c + 1]).then_inc(heads, 1)
            for k in range(KD):
                dve.wait_ge(w_turned, k + 1)
                for w, b, s in ((w_table, 3 * k, 0), (w_skip, 3 * k + 1, H)):
                    nc.vector.tensor_copy(w[:, k, 0:D], bank[b][:, 0:D]).then_inc(w_ready, 1)
                    nc.vector.tensor_copy(w[:, k, D:ROW], bank[3 * k + 2][:, s:s + H]).then_inc(w_ready, 1)
            with dve.Fori(0, NT // 2) as i:
                for u in range(2):
                    dve.wait_ge(x_loaded[u], 16 * (i + 1))
                    nc.vector.bn_stats(stats[:, u, :], xin[:, u, :]).then_inc(norm_step[u], 1)
                    after = value_of(dve, 3 * i + 1)
                    dve.wait_ge(begun, 1)
                    dve.wait_ge(norm_step[u], after)
                    nc.vector.bn_aggr(mv[:, u, :], stats[:, u, :]).then_inc(norm_step[u], 1)
                    dve.wait_ge(std_done[u], i + 1)
                    nc.vector.reciprocal(rstd[:, u:u + 1], std[:, u:u + 1]).then_inc(norm_step[u], 1)
                    dve.wait_ge(norm_step[u], 3 * i + 3)
                    dve.wait_ge(xt_psum[u], i)
                    nc.vector.tensor_scalar(xn[:, u, :], xin[:, u, :], mv[:, u, 0:1], rstd[:, u:u + 1],
                                            ALU.subtract, ALU.mult).then_inc(xn_ready[u], 1)
                for u in range(2):
                    t = 2 * i + u
                    ps = bank[4 + u]
                    dve.wait_ge(projected[u], i + 1)
                    dve.wait_ge(srow_stored[u], 16 * i)
                    nc.vector.tensor_tensor(srow[:, u, :], ps[0:NP, 0:D], bias_b[:], ALU.add
                                            ).then_inc(srow_ready[u], 1)
                    nc.vector.tensor_copy(m["st"][:, bass.ds(t, 1), 0:H].rearrange("p a h -> p (a h)"),
                                          ps[0:NP, D:ROW])
                    dve.wait_ge(dve_out[1 - u], 2 * i + 2 * u)
                    dve.wait_ge(trow_ready[u], i + 1)
                    nc.vector.tensor_tensor(maxima[:, 0, :], maxima[:, 0, :], trow[:, u, D:ROW], ALU.max
                                            ).then_inc(dve_out[u], 1)
                    nc.vector.tensor_tensor(maxima[:, 1, :], maxima[:, 1, :], ps[0:NP, D:ROW], ALU.max
                                            ).then_inc(dve_out[u], 1)
            dve.wait_ge(dve_out[1], NT)
            nc.vector.tensor_copy(m["st_parts"][:, :, 0], m["st"][:]).then_inc(st_high, 1)
            dve.wait_ge(st_high, 1)
            nc.vector.tensor_tensor(m["st_parts"][:, :, 1], m["st"][:], m["st_parts"][:, :, 0].bitcast(F32), ALU.subtract)
            nc.vector.tensor_reduce(top[0:NP, :], maxima[:], X, ALU.max).then_inc(max_step, 1)
            dve.wait_ge(max_pe, 1)
            nc.vector.tensor_reduce(bound[0:2, 0:1], bank[6][0:2, 0:NP], X, ALU.max).then_inc(max_step, 1)
            dve.wait_ge(max_pe, 2)
            nc.vector.tensor_copy(bound[:, 1:2], bank[7][:, 0:1]).then_inc(max_step, 1)
            dve.wait_ge(max_step, 3)
            nc.vector.tensor_scalar(top[:, 0:1], bound[:, 1:2], SLOPE, None, ALU.mult).then_inc(max_step, 1)
            dve.wait_ge(max_step, 4)
            nc.vector.tensor_tensor(top[:, 1:2], top[:, 0:1], bound[:, 1:2], ALU.max).then_inc(max_step, 1)
            dve.wait_ge(max_step, 5)
            nc.vector.tensor_scalar(m["neg_bound"][:], top[:, 1:2], -1.0, None, ALU.mult)

        @block.tensor
        def _(pe):
            pe.wait_ge(w_loaded, 16 * LOADS)
            for k in range(KD):
                at = slice(k * P, (k + 1) * P)
                for c in range(KD):
                    nc.tensor.transpose(bank[3 * k][:, c * P:(c + 1) * P], wp[:, c, at], m["ident"][:])
                    nc.tensor.transpose(bank[3 * k + 1][:, c * P:(c + 1) * P], wskip[:, c, at], m["ident"][:])
                if k == 0:
                    pe.wait_ge(heads, 2 * H)
                for c in range(KD):
                    mm = nc.tensor.matmul(bank[3 * k + 2][:, 0:2 * H], wp[:, c, at], a_heads[:, c, :],
                                          start=(c == 0), stop=(c == KD - 1))
                mm.then_inc(w_turned, 1)
            pe.wait_ge(w_ready, 4 * KD)
            with pe.Fori(0, NT // 2) as i:
                for u in range(2):
                    pe.wait_ge(xn_ready[u], i + 1)
                    pe.wait_ge(xt_ready[u], i)
                    for k in range(KD):
                        mm = nc.tensor.transpose(bank[u][:, k * P:k * P + NP], xn[:, u, k * P:(k + 1) * P],
                                                 m["ident"][0:NP, 0:NP])
                    mm.then_inc(xt_psum[u], 1)
                for u in range(2):
                    pe.wait_ge(xt_ready[u], i + 1)
                    pe.wait_ge(trow_ready[u], i)
                    pe.wait_ge(dve_out[u], 2 * i)
                    for w, b in ((w_table, 2 + u), (w_skip, 4 + u)):
                        for k in range(KD):
                            mm = nc.tensor.matmul(bank[b][0:NP, 0:ROW], xt[:, u, k, :], w[:, k, :],
                                                  start=(k == 0), stop=(k == KD - 1))
                    mm.then_inc(projected[u], 1)
            pe.wait_ge(max_step, 1)
            nc.tensor.transpose(bank[6][0:2, 0:NP], top[0:NP, :], m["ident"][0:NP, 0:NP]).then_inc(max_pe, 1)
            pe.wait_ge(max_step, 2)
            nc.tensor.matmul(bank[7][:, 0:1], m["ones"][0:2, :], bound[0:2, 0:1], start=True,
                             stop=True).then_inc(max_pe, 1)

        @block.scalar
        def _(act):
            act.wait_ge(begun, 1)
            nc.scalar.activation(m["warm"][1][:], m["ln_eps"][:], ACT.Sqrt)
            with act.Fori(0, NT // 2) as i:
                for u in range(2):
                    act.wait_ge(norm_step[u], 3 * i + 2)
                    nc.scalar.activation(std[:, u:u + 1], mv[:, u, 1:2], ACT.Sqrt, bias=m["ln_eps"][0:NP, :]
                                         ).then_inc(std_done[u], 1)
                for u in range(2):
                    act.wait_ge(xt_psum[u], i + 1)
                    act.wait_ge(projected[u], i)
                    nc.scalar.copy(xt[:, u, :, :], bank[u][:, 0:KD * P].rearrange("p (k n) -> p k n", k=KD)[:, :, 0:NP]
                                   ).then_inc(xt_ready[u], 1)
                for u in range(2):
                    t = 2 * i + u
                    act.wait_ge(projected[u], i + 1)
                    act.wait_ge(trow_stored[u], 16 * i)
                    act.wait_ge(dve_out[u], 2 * i)
                    nc.scalar.copy(trow[:, u, :], bank[2 + u][0:NP, 0:ROW]).then_inc(trow_ready[u], 1)
                    act.wait_ge(trow_ready[u], i + 1)
                    act.dma_start(table[tile(t), :], trow[:, u, :]).then_inc(trow_stored[u], 16)
                    act.wait_ge(srow_ready[u], i + 1)
                    act.dma_start(skip_rows[tile(t), :], srow[:, u, :]).then_inc(srow_stored[u], 16)
            for u in range(2):
                act.wait_ge(trow_stored[u], 16 * (NT // 2))
                act.wait_ge(srow_stored[u], 16 * (NT // 2))


def edge_phase(nc, m, bank, table):
    with ExitStack() as ctx:
        def sb(name, shape, dt=F32):
            return ctx.enter_context(nc.sbuf_tensor(name, shape, dt))

        def sem(name):
            return ctx.enter_context(nc.semaphore(name))

        def sems(*names):
            return [[sem(f"{name}{k}") for k in range(K)] for name in names]

        def tiles(name, shape, dt=F32):
            return [sb(f"{name}{k}", shape, dt) for k in range(K)]

        idx, rows = tiles("idx", [P, SET], I32), tiles("rows", [P, SET, ROW])
        onehot, onehot_t = tiles("onehot", [P, SET, NP], F32R), tiles("onehot_t", [NP, SET * P], F32R)
        half_score, raw_score, score = (tiles(name, [P, SET, H]) for name in ("half_score", "raw_score", "score"))
        weighed = tiles("weighed", [P, SET, ROW])
        high, low = tiles("high", [P, SET, ROW], F32R), tiles("low", [P, SET, ROW], F32R)
        masked, runmax = tiles("masked", [P, SET, H]), tiles("runmax", [P, SET, H])
        top, peak = sb("edge_top", [P, K + 1]), sb("peak", [1, 1])
        acc_bank, turn_bank = bank[0], bank[1:1 + K]
        z = [b[:, 0:SET * 2 * ST].rearrange("p (s h) -> p s h", s=SET) for b in bank[1 + K:1 + 2 * K]]
        idx_ready, gathered, onehot_ready, turned, turn_copied, z_ready = sems(
            "idx_ready", "gathered", "onehot_ready", "turned", "turn_copied", "z_ready")
        half_added, added, scored, weight_ready, rounded = sems("half_added", "added", "scored", "weight_ready", "rounded")
        weighed_done, max_done, low_done, sum_done = sems(
            "weighed_done", "max_done", "low_done", "sum_done")
        begun = m["begun"]
        block_summed, acc_done = sem("block_summed"), sem("acc_done")
        peak_dve = sem("peak_dve")
        block = ctx.enter_context(nc.Block())

        def over_steps(engine, b, body):
            _, (lo, first, last, next_lo) = nc.values_load_multi_w_load_instructions(
                m["ranges"][0:1, bass.ds(b, 1), 0:4].rearrange("p a k -> p (a k)"),
                engines=[engine.engine], min_val=0, max_val=NT * NSUB,
                skip_runtime_bounds_check_because=BY_TABLE)
            first, last = (nc.s_assert_within(v, 1, NT * NSUB) for v in (first, last))

            def column(s):
                return nc.s_assert_within(engine.snap((s - first) * G + lo), 0, COLS - 2 * G,
                                         skip_runtime_bounds_check_because=BY_TABLE)

            with engine.Fori(first, last) as s:
                col = column(s)
                body(s, col, col + G, b)
            next_col = nc.s_assert_within(next_lo, 0, NSUB, skip_runtime_bounds_check_because=BY_TABLE)
            body(last, column(last), next_col, b + 1)

        @block.gpsimd
        def _(pool):
            def gather(s, *_):
                now = value_of(pool, s)
                for k in range(K):
                    pool.wait_ge(begun, 1)
                    pool.wait_ge(idx_ready[k], now)
                    pool.wait_ge(weighed_done[k], now)
                    for i in range(SET):
                        nc.gpsimd.indirect_dma_start(
                            rows[k][:, i, :], None, table,
                            bass.IndirectOffsetOnAxis(ap=idx[k][:, i:i + 1], axis=0)).then_inc(gathered[k], 16)

            with pool.Fori(0, NT) as b:
                _, (first, last) = nc.values_load_multi_w_load_instructions(
                    m["ranges"][0:1, bass.ds(b, 1), 1:3].rearrange("p a k -> p (a k)"),
                    engines=[pool.engine], min_val=0, max_val=NT * NSUB)
                with pool.Fori(first, last + 1) as s:
                    gather(s)

        @block.tensor
        def _(pe):
            def turn(k, s):
                pe.wait_ge(onehot_ready[k], s)
                for i in range(SET):
                    mm = nc.tensor.matmul(turn_bank[k][0:NP, i * P:(i + 1) * P], onehot[k][:, i, :],
                                          m["ident_r"][:], start=True, stop=True)
                mm.then_inc(turned[k], 1)

            def target_scores(k, s, b):
                pe.wait_ge(turn_copied[k], s)
                pe.wait_ge(max_done[k], 2 * s)
                for i in range(SET):
                    mm = nc.tensor.matmul(z[k][:, i, :], onehot_t[k][:, i * P:(i + 1) * P],
                                          m["st_parts"][:, bass.ds(b, 1)].rearrange("p a c h -> p (a c h)"),
                                          start=True, stop=True)
                mm.then_inc(z_ready[k], 1)

            def sum_high(k, s):
                pe.wait_ge(rounded[k], s)
                for i in range(SET):
                    nc.tensor.matmul(acc_bank[0:NP, 0:ROW], onehot[k][:, i, :], high[k][:, i, :],
                                     start=False, stop=False, skip_group_check=True)

            def sum_low(k, s):
                pe.wait_ge(low_done[k], s + 1)
                for i in range(SET):
                    mm = nc.tensor.matmul(acc_bank[0:NP, 0:ROW], onehot[k][:, i, :], low[k][:, i, :],
                                          start=False, stop=False, skip_group_check=True)
                mm.then_inc(sum_done[k], 1)

            def body(s, col, next_col, next_b, b):
                turn(2, s)
                sum_high(0, s)
                target_scores(2, s, b)
                sum_low(0, s)
                sum_high(1, s)
                turn(0, s + 1)
                sum_low(1, s)
                target_scores(0, s + 1, next_b)
                sum_high(2, s)
                turn(1, s + 1)
                sum_low(2, s)
                target_scores(1, s + 1, next_b)

            for k in range(K):
                pe.sem_inc(sum_done[k], 1)
            for k in range(2):
                turn(k, 1)
                target_scores(k, 1, 0)
            with pe.Fori(0, NT) as b:
                pe.wait_ge(acc_done, b + 1)
                nc.tensor.matmul(acc_bank[0:NP, 0:ROW], m["zero16"][:, 0:NP], m["zero16"][:], start=True,
                                 stop=False, skip_group_check=True)
                over_steps(pe, b, lambda s, col, next_col, next_b: body(s, col, next_col, next_b, b))
                nc.tensor.matmul(acc_bank[0:NP, 0:ROW], m["zero16"][:, 0:NP], m["zero16"][:], start=False,
                                 stop=True, skip_group_check=True).then_inc(block_summed, 1)
            pe.wait_ge(peak_dve, K + 1)
            nc.tensor.transpose(bank[7][0:1, 0:P], top[:, K:K + 1], m["ident"][:]).then_inc(block_summed, 1)
            pe.wait_ge(peak_dve, K + 2)
            nc.tensor.matmul(bank[7][:, P:P + 1], m["ones"][0:1, :], peak[:], start=True, stop=True).then_inc(block_summed, 1)

        @block.vector
        def _(dve):
            def compare(k, s, col, b):
                dve.wait_ge(sum_done[k], s)
                shape = [P, SET, NP]
                nc.vector.scalar_tensor_tensor(
                    onehot[k][:], m["iota"][:, 0:NP].unsqueeze(1).to_broadcast(shape),
                    m["block_start"][:, bass.ds(b, 1)],
                    m["dst_tab"][:, bass.ds(col + k * SET, SET)].unsqueeze(2).to_broadcast(shape),
                    ALU.add, ALU.is_equal).then_inc(onehot_ready[k], 1)

            def add(k, s):
                dve.wait_ge(z_ready[k], s)
                dve.wait_ge(gathered[k], 16 * SET * s)
                nc.vector.tensor_tensor(half_score[k][:], rows[k][:, :, D:ROW], z[k][:, :, 0:H], ALU.add
                                        ).then_inc(half_added[k], 1)
                dve.wait_ge(half_added[k], s)
                nc.vector.tensor_tensor(raw_score[k][:], half_score[k][:], z[k][:, :, ST:ST + H], ALU.add
                                        ).then_inc(added[k], 1)
                dve.wait_ge(added[k], s)
                nc.vector.scalar_tensor_tensor(score[k][:], raw_score[k][:], SLOPE, raw_score[k][:],
                                               ALU.mult, ALU.max).then_inc(scored[k], 1)

            def weigh(k, s):
                dve.wait_ge(weight_ready[k], s)
                shape = [P, SET, H, FO]
                nc.vector.tensor_tensor(
                    weighed[k][:, :, 0:D].rearrange("p s (h f) -> p s h f", h=H),
                    rows[k][:, :, 0:D].rearrange("p s (h f) -> p s h f", h=H),
                    weighed[k][:, :, D:ROW].unsqueeze(3).to_broadcast(shape), ALU.mult).then_inc(weighed_done[k], 1)

            def largest(k, s):
                nc.vector.tensor_tensor(masked[k][:], weighed[k][:, :, D:ROW],
                                        z[k][:, :, H:H + 1].to_broadcast([P, SET, H]), ALU.mult
                                        ).then_inc(max_done[k], 1)
                dve.wait_ge(max_done[k], 2 * s + 1)
                nc.vector.tensor_tensor(runmax[k][:], runmax[k][:], masked[k][:], ALU.max).then_inc(max_done[k], 1)

            def remainder(k, s):
                dve.wait_ge(rounded[k], s)
                nc.vector.tensor_tensor(low[k][:], weighed[k][:], high[k][:].bitcast(F32), ALU.subtract
                                        ).then_inc(low_done[k], 1)

            def body(s, col, next_col, next_b, b):
                add(0, s)
                compare(2, s, col, b)
                weigh(0, s)
                add(1, s)
                largest(0, s)
                remainder(0, s)
                weigh(1, s)
                add(2, s)
                largest(1, s)
                remainder(1, s)
                compare(0, s + 1, next_col, next_b)
                weigh(2, s)
                largest(2, s)
                compare(1, s + 1, next_col, next_b)
                remainder(2, s)

            for k in range(K):
                for used in (weighed_done, max_done, low_done):
                    dve.sem_inc(used[k], 1)
                nc.vector.memset(runmax[k][:], 0.0).then_inc(max_done[k], 1)
            _, (lo,) = nc.values_load_multi_w_load_instructions(
                m["ranges"][0:1, 0, 0:1], engines=[dve.engine], min_val=0, max_val=NSUB)
            for k in range(2):
                compare(k, 1, lo, 0)
            with dve.Fori(0, NT) as b:
                over_steps(dve, b, lambda s, col, next_col, next_b: body(s, col, next_col, next_b, b))
            dve.wait_ge(block_summed, NT)
            for k in range(K):
                nc.vector.tensor_reduce(top[:, k:k + 1], runmax[k][:].rearrange("p s h -> p (s h)"), X, ALU.max
                                        ).then_inc(peak_dve, 1)
            dve.wait_ge(peak_dve, K)
            nc.vector.tensor_reduce(top[:, K:K + 1], top[:, 0:K], X, ALU.max).then_inc(peak_dve, 1)
            dve.wait_ge(block_summed, NT + 1)
            nc.vector.tensor_reduce(peak[:], bank[7][0:1, 0:P], X, ALU.max).then_inc(peak_dve, 1)
            dve.wait_ge(block_summed, NT + 2)
            nc.vector.tensor_scalar(m["eps"][:], bank[7][:, P:P + 1], DEN_EPS, None, ALU.mult)

        @block.scalar
        def _(act):
            def indices(k, s, col):
                nc.scalar.copy(idx[k][:], m["src_tab"][:, bass.ds(col + k * SET, SET)]).then_inc(idx_ready[k], 1)

            def copy_turned(k, s):
                act.wait_ge(turned[k], s)
                nc.scalar.copy(onehot_t[k][:], turn_bank[k][0:NP, 0:SET * P]).then_inc(turn_copied[k], 1)

            def exponentials(k, s):
                act.wait_ge(scored[k], s)
                act.wait_ge(low_done[k], s)
                nc.scalar.activation(weighed[k][:, :, D:ROW], score[k][:], ACT.Exp, bias=m["neg_bound"][:]
                                     ).then_inc(weight_ready[k], 1)

            def round_off(k, s):
                act.wait_ge(weighed_done[k], s + 1)
                act.wait_ge(sum_done[k], s)
                nc.scalar.copy(high[k][:], weighed[k][:]).then_inc(rounded[k], 1)

            def body(s, col, next_col, next_b, b):
                exponentials(0, s)
                indices(0, s + 1, next_col)
                round_off(0, s)
                exponentials(1, s)
                indices(1, s + 1, next_col)
                copy_turned(2, s)
                round_off(1, s)
                exponentials(2, s)
                indices(2, s + 1, next_col)
                copy_turned(0, s + 1)
                round_off(2, s)
                copy_turned(1, s + 1)

            act.sem_inc(acc_done, 1)
            nc.scalar.activation(m["warm"][0][:], m["neg_bound"][:], ACT.Exp)
            _, (lo,) = nc.values_load_multi_w_load_instructions(
                m["ranges"][0:1, 0, 0:1], engines=[act.engine], min_val=0, max_val=NSUB)
            for k in range(K):
                indices(k, 1, lo)
            for k in range(2):
                copy_turned(k, 1)
            with act.Fori(0, NT) as b:
                over_steps(act, b, lambda s, col, next_col, next_b: body(s, col, next_col, next_b, b))
                act.wait_ge(block_summed, b + 1)
                nc.scalar.copy(m["acc"][:, bass.ds(b, 1), :].rearrange("p a d -> p (a d)"), acc_bank[0:NP, 0:ROW]
                               ).then_inc(acc_done, 1)


def route_phase(nc, m, bank, x, skip_rows, xg):
    with ExitStack() as ctx:
        def sb(name, shape, dt=F32):
            return ctx.enter_context(nc.sbuf_tensor(name, shape, dt))

        def sem(name):
            return ctx.enter_context(nc.semaphore(name))

        def sems(name, n=2):
            return [sem(f"{name}{k}") for k in range(n)]

        xin, skin = sb("r_xin", [NP, 2, D]), sb("r_skip", [NP, 2, D])
        den = sb("den", [NP, 2, H])
        att, low, ex = sb("att", [NP, 2, D]), sb("low", [NP, 2, D]), sb("ex", [NP, 2, D])
        stats, mv = sb("r_stats", [NP, 2, 6]), sb("r_mv", [NP, NT, 2])
        mv_tile = sb("mv_tile", [NP, 2])
        std1, rstd1, var2, std2, rstd2 = (sb(s, [NP, NT]) for s in ("std1", "rstd1", "var2", "std2", "rstd2"))
        xl, xlt, xn = sb("xl", [NP, 2, D]), sb("xlt", [P, 2, KD, NP]), sb("r_xn", [NP, 2, 2, XROW])
        logits, top8, pick8 = sb("logits", [NP, NX]), sb("top8", [NP, 8]), sb("pick8", [NP, 8], U32)
        pick = sb("pick", [NP, 2])
        one = sb("one", [NP, 2, NX])
        mask, before, rank = sb("mask", [NP, NX]), sb("before", [NP, NX]), sb("rank", [NP, NX])
        place, junk = sb("place", [NP, 2]), sb("junk", [NP, 2, NX])
        slot = [[sb(f"slot{u}{k}", [NP, 1], I32) for k in range(2)] for u in range(2)]
        padding = sb("padding", [P, FILL // P, XROW])
        crow, cwhole = sb("count_row", [1, 6, NX]), sb("count_whole", [1, NX], I32)
        wtmp = sb("wtmp", [NP, NT])

        begun = m["begun"]
        loaded = sems("r_loaded")
        res_step, dve_step, norm_dve, norm_act, end_step = (
            sem(s) for s in ("res_step", "route_step", "norm_dve", "norm_act", "end_step"))
        low_ready, ex_ready, xl_ready, xlt_psum, xlt_ready, xn_ready, logit_psum, mask_ready, ranked = (sems(s) for s in (
            "low_ready", "ex_ready", "xl_ready", "xlt_psum", "xlt_ready", "r_xn_ready", "logit_psum", "mask_ready",
            "ranked"))
        x_used, slot_ready, sent = sems("x_used"), sems("slot_ready"), sems("sent")
        zero_ready, counted, count_ready, filled = (
            sem(s) for s in ("zero_ready", "counted", "count_ready", "filled"))
        block = ctx.enter_context(nc.Block())

        @block.sync
        def _(sp):
            with sp.Fori(0, NT // 2) as i:
                for u in range(2):
                    sp.wait_ge(x_used[u], i)
                    sp.dma_start(xin[:, u, :], x[tile(2 * i + u), :]).then_inc(loaded[u], 16)
                    sp.dma_start(skin[:, u, :], skip_rows[tile(2 * i + u), :]).then_inc(loaded[u], 16)
            sp.wait_ge(zero_ready, 1 + FILL // P)
            sp.wait_ge(count_ready, 1)
            with sp.Fori(0, NX) as e:
                n = nc.values_load(m["counts"][0:1, bass.ds(e, 1), 0:1].rearrange("p a k -> p (a k)"),
                                   engines=[sp.engine], min_val=0, max_val=N)
                sp.dma_start(xg[bass.ds(e * CAP + n, FILL), :].rearrange("(h p) d -> p h d", p=P), padding[:]
                             ).then_inc(filled, 16)
            sp.wait_ge(filled, 16 * NX)

        @block.vector
        def _(dve):
            nc.vector.memset(padding[:, :, 0:D], 0.0).then_inc(zero_ready, 1)
            for h in range(FILL // P):
                nc.vector.tensor_scalar(padding[:, h, D:XROW], m["iota_p"][:], float(2 * N), None, ALU.add
                                        ).then_inc(zero_ready, 1)
            nc.vector.memset(before[:], 0.0).then_inc(zero_ready, 1)
            RES_STEPS = 14
            with dve.Fori(0, NT // 2) as i:
                steps = [0]

                def step(ins):
                    steps[0] += 1
                    ins.then_inc(res_step, 1)

                def settle(constant=None):
                    count = value_of(dve, steps[0] + i * RES_STEPS)
                    if constant is not None:
                        dve.wait_ge(constant, 1)
                    dve.wait_ge(res_step, count)

                for u in range(2):
                    t = 2 * i + u
                    x1 = m["acc"][:, bass.ds(t, 1), 0:D].rearrange("p a d -> p (a d)")
                    sums = m["acc"][:, bass.ds(t, 1), D:ROW].rearrange("p a d -> p (a d)")
                    step(nc.vector.tensor_scalar(den[:, u, :], sums, m["eps"][0:NP, :], None, ALU.add))
                    settle()
                    step(nc.vector.reciprocal(den[:, u, :], den[:, u, :]))
                    settle()
                    step(nc.vector.tensor_tensor(
                        att[:, u, :].rearrange("p (h f) -> p h f", h=H), x1.rearrange("p (h f) -> p h f", h=H),
                        den[:, u, :].unsqueeze(2).to_broadcast([NP, H, FO]), ALU.mult))
                    settle()
                    dve.wait_ge(loaded[u], 32 * (i + 1))
                    step(nc.vector.tensor_tensor(att[:, u, :], att[:, u, :], skin[:, u, :], ALU.add))
                    settle()
                    nc.vector.tensor_scalar(low[:, u, :], att[:, u, :], 0.0, None, ALU.min
                                            ).then_inc(low_ready[u], 1)
                for u in range(2):
                    t = 2 * i + u
                    x1 = m["acc"][:, bass.ds(t, 1), 0:D].rearrange("p a d -> p (a d)")
                    dve.wait_ge(ex_ready[u], i + 1)
                    step(nc.vector.scalar_tensor_tensor(att[:, u, :], att[:, u, :], 0.0, ex[:, u, :], ALU.max, ALU.add))
                    settle()
                    nc.vector.scalar_tensor_tensor(x1, att[:, u, :], -1.0, xin[:, u, :], ALU.add, ALU.add
                                                   ).then_inc(x_used[u], 1)
                    after = value_of(dve, i + 1)
                    dve.wait_ge(begun, 1)
                    dve.wait_ge(x_used[u], after)
                    step(nc.vector.bn_stats(stats[:, u, :], x1))
                    settle(begun)
                    step(nc.vector.bn_aggr(mv_tile[:], stats[:, u, :]))
                    settle()
                    nc.vector.tensor_copy(m_v(mv, t), mv_tile[:]).then_inc(norm_dve, 1)
                assert steps[0] == RES_STEPS, steps[0]
            dve.wait_ge(norm_act, 1)
            nc.vector.reciprocal(rstd1[:], std1[:]).then_inc(norm_dve, 1)
            dve.wait_ge(norm_dve, NT + 1)
            nc.vector.tensor_tensor(var2[:], rstd1[:], rstd1[:], ALU.mult).then_inc(norm_dve, 1)
            dve.wait_ge(norm_dve, NT + 2)
            nc.vector.tensor_tensor(var2[:], var2[:], mv[:, :, 1], ALU.mult).then_inc(norm_dve, 1)
            dve.wait_ge(norm_act, 2)
            nc.vector.reciprocal(rstd2[:], std2[:]).then_inc(norm_dve, 1)
            PER = 22
            with dve.Fori(0, NT // 2) as i:
                route = [0]

                def step(ins):
                    route[0] += 1
                    ins.then_inc(dve_step, 1)

                def settle(constant=None):
                    count = value_of(dve, route[0] + i * PER)
                    if constant is not None:
                        dve.wait_ge(constant, 1)
                    dve.wait_ge(dve_step, count)

                for u in range(2):
                    t = 2 * i + u
                    x1 = m["acc"][:, bass.ds(t, 1), 0:D].rearrange("p a d -> p (a d)")
                    dve.wait_ge(xlt_psum[u], i)
                    dve.wait_ge(xn_ready[u], i)
                    nc.vector.tensor_scalar(xl[:, u, :], x1, m_v(mv, t)[:, 0:1], rstd1[:, bass.ds(t, 1)],
                                            ALU.subtract, ALU.mult).then_inc(xl_ready[u], 1)
                for u in range(2):
                    t = 2 * i + u
                    dve.wait_ge(logit_psum[u], i + 1)
                    step(nc.vector.tensor_tensor(logits[:], bank[4 + u][0:NP, 0:NX], m["br"][:], ALU.add))
                    settle(begun)
                    step(nc.vector.max(top8[:], logits[:]))
                    settle(begun)
                    step(nc.vector.max_index(pick8[:], top8[:], logits[:]))
                    step(nc.vector.tensor_tensor(m["gaps"][:, bass.ds(t, 1)], top8[:, 1:2], top8[:, 0:1], ALU.subtract))
                    settle()
                    step(nc.vector.tensor_copy(pick[:], pick8[:, 0:2]))
                    settle()
                    for k in range(2):
                        step(nc.vector.tensor_scalar(one[:, k, :], m["iota"][0:NP, 0:NX], pick[:, k:k + 1], None,
                                                     ALU.is_equal))
                    settle()
                    nc.vector.tensor_tensor(mask[:], one[:, 0, :], one[:, 1, :], ALU.add).then_inc(mask_ready[u], 1)
                    dve.wait_ge(ranked[u], i + 1)
                    step(nc.vector.tensor_tensor(rank[:], bank[6 + u][0:NP, 0:NX], m["cap_row"][0:NP, :], ALU.add))
                    step(nc.vector.tensor_tensor(before[:], before[:], mask[:], ALU.add))
                    settle()
                    step(nc.vector.tensor_tensor(junk[:], one[:], rank[:].unsqueeze(1).to_broadcast([NP, 2, NX]),
                                                 ALU.mult))
                    settle()
                    step(nc.vector.tensor_reduce(place[:], junk[:], X, ALU.add))
                    settle()
                    dve.wait_ge(sent[u], 32 * i)
                    for k in range(2):
                        nc.vector.tensor_copy(slot[u][k][:], place[:, k:k + 1]).then_inc(slot_ready[u], 1)
                    nc.vector.tensor_copy(xn[:, u, :, D:XROW].rearrange("p k o -> p (k o)"),
                                          m["result_row"][:, bass.ds(t, 1), :].rearrange("p a k -> p (a k)")
                                          ).then_inc(slot_ready[u], 1)
                    dve.wait_ge(slot_ready[u], 3 * (i + 1))
                assert route[0] == PER, route[0]
            dve.wait_ge(counted, 1)
            last = [0]

            def then(ins):
                last[0] += 1
                ins.then_inc(end_step, 1)
                dve.wait_ge(end_step, last[0])

            CNT, UP, TILES, GE, GS, ZERO = range(6)
            then(nc.vector.tensor_copy(crow[:, CNT], bank[3][0:1, 0:NX]))
            then(nc.vector.memset(crow[:, ZERO], 0.0))
            then(nc.vector.tensor_scalar(crow[:, UP], crow[:, CNT], 1.0, float(TOK - 1), ALU.max, ALU.add))
            then(nc.vector.tensor_copy(cwhole[:], crow[:, UP]))
            then(nc.vector.tensor_scalar(cwhole[:], cwhole[:], TOK.bit_length() - 1, None, ALU.arith_shift_right))
            then(nc.vector.tensor_copy(crow[:, TILES], cwhole[:]))
            then(nc.vector.tensor_tensor_scan(crow[:, GE], crow[:, TILES], crow[:, ZERO], 0.0, ALU.add, ALU.add))
            then(nc.vector.tensor_tensor(crow[:, GS], crow[:, GE], crow[:, TILES], ALU.subtract))
            for k, r in enumerate((CNT, GS, GE)):
                then(nc.vector.tensor_copy(m["counts"][:, :, k], crow[:, r]))
            then(nc.vector.tensor_scalar(crow[:, ZERO], crow[:, GE], -1.0, None, ALU.add))
            nc.vector.tensor_copy(m["counts"][:, :, 3], crow[:, ZERO]).then_inc(count_ready, 1)
            dve.wait_ge(norm_act, 3)
            then(nc.vector.tensor_scalar(wtmp[:], m["gaps"][:], 1.0, None, ALU.add))
            then(nc.vector.reciprocal(m["weights"][:, :, 0], wtmp[:]))
            then(nc.vector.tensor_tensor(m["weights"][:, :, 1], m["weights"][:, :, 0], m["gaps"][:], ALU.mult))

        @block.scalar
        def _(act):
            with act.Fori(0, NT // 2) as i:
                for u in range(2):
                    act.wait_ge(low_ready[u], i + 1)
                    nc.scalar.activation(ex[:, u, :], low[:, u, :], ACT.Exp).then_inc(ex_ready[u], 1)
            act.wait_ge(norm_dve, NT)
            nc.scalar.activation(std1[:], mv[:, :, 1], ACT.Sqrt, bias=m["ln_eps"][0:NP, :]).then_inc(norm_act, 1)
            act.wait_ge(norm_dve, NT + 3)
            nc.scalar.activation(std2[:], var2[:], ACT.Sqrt, bias=m["ln_eps"][0:NP, :]).then_inc(norm_act, 1)
            act.wait_ge(norm_dve, NT + 4)
            with act.Fori(0, NT // 2) as i:
                for u in range(2):
                    act.wait_ge(xlt_psum[u], i + 1)
                    nc.scalar.copy(xlt[:, u, :, :], bank[u][:, 0:KD * P].rearrange("p (k n) -> p k n", k=KD)[:, :, 0:NP]
                                   ).then_inc(xlt_ready[u], 1)
                for u in range(2):
                    act.wait_ge(sent[u], 32 * i)
                    nc.scalar.activation(xn[:, u, :, 0:D], xl[:, u, :].unsqueeze(1).to_broadcast([NP, 2, D]), ACT.Copy,
                                         scale=rstd2[:, bass.ds(2 * i + u, 1)]
                                         ).then_inc(xn_ready[u], 1)
            act.wait_ge(count_ready, 1)
            nc.scalar.activation(m["gaps"][:], m["gaps"][:], ACT.Exp).then_inc(norm_act, 1)

        @block.tensor
        def _(pe):
            pe.wait_ge(zero_ready, 2 + FILL // P)
            with pe.Fori(0, NT // 2) as i:
                for u in range(2):
                    pe.wait_ge(xl_ready[u], i + 1)
                    for k in range(KD):
                        mm = nc.tensor.transpose(bank[u][:, k * P:k * P + NP], xl[:, u, k * P:(k + 1) * P],
                                                 m["ident"][0:NP, 0:NP])
                    mm.then_inc(xlt_psum[u], 1)
                for u in range(2):
                    pe.wait_ge(xlt_ready[u], i + 1)
                    for k in range(KD):
                        mm = nc.tensor.matmul(bank[4 + u][0:NP, 0:NX], xlt[:, u, k, :], m["wr"][:, k, :],
                                              start=(k == 0), stop=(k == KD - 1))
                    mm.then_inc(logit_psum[u], 1)
                for u in range(2):
                    pe.wait_ge(mask_ready[u], i + 1)
                    nc.tensor.matmul(bank[6 + u][0:NP, 0:NX], m["ones"][0:NP, 0:NP], before[:], start=True, stop=False)
                    nc.tensor.matmul(bank[6 + u][0:NP, 0:NX], m["lower"][0:NP, 0:NP], mask[:], start=False,
                                     stop=True).then_inc(ranked[u], 1)
            pe.wait_ge(slot_ready[1], 3 * (NT // 2))
            nc.tensor.matmul(bank[3][0:1, 0:NX], m["ones"][0:NP, 0:1], before[:], start=True,
                             stop=True).then_inc(counted, 1)

        @block.gpsimd
        def _(pool):
            with pool.Fori(0, NT // 2) as i:
                for u in range(2):
                    three, after = value_of(pool, 3 * (i + 1)), value_of(pool, i + 1)
                    pool.wait_ge(begun, 1)
                    pool.wait_ge(slot_ready[u], three)
                    pool.wait_ge(xn_ready[u], after)
                    for k in range(2):
                        nc.gpsimd.indirect_dma_start(
                            xg, bass.IndirectOffsetOnAxis(ap=slot[u][k][:], axis=0), xn[:, u, k, :], None
                        ).then_inc(sent[u], 16)
            for u in range(2):
                pool.wait_ge(sent[u], 32 * (NT // 2))


def expert_phase(nc, m, bank, xg, y2, ln_g, ln_b, W1, b1, W2, b2):
    with ExitStack() as ctx:
        def sb(name, shape, dt=F32):
            return ctx.enter_context(nc.sbuf_tensor(name, shape, dt))

        def sem(name):
            return ctx.enter_context(nc.semaphore(name))

        def sems(name, n=2):
            return [sem(f"{name}{k}") for k in range(n)]

        w1_raw, w2_raw = sb("w1_raw", [P, KD, HID]), sb("w2_raw", [P, JH, D])
        params_raw, params = sb("params_raw", [P, 2 * KD + JH + D]), sb("params", [P, 2, 2 * KD + JH + D])
        w1h, w1l = sb("w1h", [P, 2, KD, HID], F32R), sb("w1l", [P, 2, KD, HID], F32R)
        w2h, w2l = sb("w2h", [P, 2, JH, D], F32R), sb("w2l", [P, 2, JH, D], F32R)
        GAIN, SHIFT, B1, B2 = 0, KD, 2 * KD, 2 * KD + JH
        xrow = sb("xrow", [P, HALF, XROW])
        xt, xth, xtl = sb("f_xt", [P, KD, TOK]), sb("f_xth", [P, KD, TOK], F32R), sb("f_xtl", [P, KD, TOK], F32R)
        hid = sb("hid", [P, JH, TOK])
        hidh, hidl = sb("hidh", [P, JH, TOK], F32R), sb("hidl", [P, JH, TOK], F32R)
        yrow = sb("yrow", [P, HALF, D])
        goes_next = sb("goes_next", [P, HALF])
        goes_to = [sb(f"goes_to{h}", [P, 1], I32) for h in range(HALF)]
        x_bank, y_bank, h_bank = bank[0:HALF], bank[5:5 + HALF], [bank[k] for k in (2, 3, 4, 7)]
        HB = len(h_bank)
        raw_loaded, w_high, w_low, xt_step, hid_high, hid_low = (
            sem(s) for s in ("f_raw_loaded", "f_w_high", "f_w_low", "f_xt_step", "f_hid_high", "f_hid_low"))
        row_loaded, row_used, goes_ready, stored, y_psum, y_ready = (sems(s, HALF) for s in (
            "f_row_loaded", "f_row_used", "f_goes_ready", "f_stored", "f_y_psum", "f_y_ready"))
        h_psum, h_ready = sems("f_h_psum", HB), sems("f_h_ready", HB)
        block = ctx.enter_context(nc.Block())
        W_LOADS = 6
        XT_STEPS = KD * HALF + 2

        def tiles_of(engine, e):
            _, got = nc.values_load_multi_w_load_instructions(
                m["counts"][0:1, bass.ds(e, 1), 1:4].rearrange("p a k -> p (a k)"),
                engines=[engine.engine], min_val=0, max_val=NX * CAP // TOK)
            return got

        def over_experts(engine, body):
            with engine.Fori(0, NX // 2 - 1) as i:
                body(i, 0, True)
                body(i, 1, True)
            body(NX // 2 - 1, 0, True)
            body(NX // 2 - 1, 1, False)

        @block.sync
        def _(sp):
            def load_rows(g, row):
                rows = [sp.snap(row + h * P) if h else row for h in range(HALF)]
                steps = value_of(sp, XT_STEPS * g)
                for h in range(HALF):
                    sp.wait_ge(row_used[h], g)
                    sp.wait_ge(xt_step, steps)
                    sp.dma_start(xrow[:, h, :], xg[bass.ds(rows[h], P), :]).then_inc(row_loaded[h], 16)

            with sp.Fori(0, NX) as e:
                first, end, _ = tiles_of(sp, e)
                with sp.Fori(first, end) as g:
                    load_rows(g, nc.s_assert_within(sp.snap((g - first) * TOK + e * CAP), 0, NX * CAP - TOK,
                                                    skip_runtime_bounds_check_because=BY_TABLE))
            _, end, _ = tiles_of(sp, NX - 1)
            load_rows(end, sp.snap(sp.to_reg(0)))

        @block.tensor
        def _(pe):
            def turn_rows(g):
                for h in range(HALF):
                    pe.wait_ge(row_loaded[h], 16 * (g + 1))
                    for k in range(KD):
                        mm = nc.tensor.transpose(x_bank[h][:, k * P:(k + 1) * P],
                                                 xrow[:, h, k * P:(k + 1) * P], m["ident"][:])
                    mm.then_inc(row_used[h], 1)

            def body(g, s):
                pe.wait_ge(xt_step, XT_STEPS * (g + 1))
                for j in range(JH):
                    pe.wait_ge(h_ready[j % HB], JH // HB * g + j // HB)
                    for k in range(KD):
                        at = slice(j * P, (j + 1) * P)
                        for n, (w, v) in enumerate(((w1h, xth), (w1h, xtl), (w1l, xth))):
                            mm = nc.tensor.matmul(h_bank[j % HB][:, 0:TOK], w[:, s, k, at], v[:, k, :],
                                                  start=(k == 0 and n == 0), stop=(k == KD - 1 and n == 2))
                    mm.then_inc(h_psum[j % HB], 1)
                turn_rows(g + 1)
                for h in range(HALF):
                    pe.wait_ge(y_ready[h], g)
                for j in range(JH):
                    for n, (v, w) in enumerate(((hidh, w2h), (hidh, w2l), (hidl, w2h))):
                        if n == 0:
                            pe.wait_ge(hid_high, JH * g + j + 1)
                        if n == 2:
                            pe.wait_ge(hid_low, JH * g + j + 1)
                        for h in range(HALF):
                            mm = nc.tensor.matmul(y_bank[h][:, 0:D], v[:, j, h * P:(h + 1) * P], w[:, s, j, :],
                                                  start=(j == 0 and n == 0), stop=(j == JH - 1 and n == 2))
                            if j == JH - 1 and n == 2:
                                mm.then_inc(y_psum[h], 1)

            turn_rows(0)
            with pe.Fori(0, NX // 2) as i:
                for s in range(2):
                    first, end, _ = tiles_of(pe, 2 * i + s)
                    with pe.Fori(first, end) as g:
                        pe.wait_ge(w_high, 2 * (2 * i + s + 1))
                        pe.wait_ge(w_low, 3 * (2 * i + s + 1))
                        body(g, s)

        @block.scalar
        def _(act):
            def split_high(e, s):
                act.wait_ge(raw_loaded, 16 * W_LOADS * (e + 1))
                nc.scalar.copy(w1h[:, s], w1_raw[:]).then_inc(w_high, 1)
                nc.scalar.copy(w2h[:, s], w2_raw[:]).then_inc(w_high, 1)

            def gelus(g, s):
                def rounded(j):
                    act.wait_ge(h_ready[j % HB], JH // HB * g + j // HB + 1)
                    nc.scalar.copy(hidh[:, j, :], hid[:, j, :]).then_inc(hid_high, 1)

                for j in range(JH):
                    act.wait_ge(h_psum[j % HB], JH // HB * g + j // HB + 1)
                    if j == 0:
                        act.wait_ge(hid_low, JH * g)
                    nc.scalar.activation(hid[:, j, :], h_bank[j % HB][:, 0:TOK], ACT.Gelu,
                                         bias=params[:, s, B1 + j:B1 + j + 1]).then_inc(h_ready[j % HB], 1)
                    if j:
                        rounded(j - 1)
                rounded(JH - 1)

            def expert(i, s, more):
                first, end, _ = tiles_of(act, 2 * i + s)
                if more:
                    act.wait_ge(y_ready[HALF - 1], first)
                    split_high(2 * i + s + 1, 1 - s)
                act.wait_ge(w_low, 3 * (2 * i + s + 1))
                with act.Fori(first, end) as g:
                    gelus(g, s)

            nc.scalar.activation(m["warm"][2][:], m["ln_eps"][:], ACT.Gelu)
            split_high(0, 0)
            over_experts(act, expert)

        @block.vector
        def _(dve):
            def split_low(e, s):
                dve.wait_ge(raw_loaded, 16 * W_LOADS * (e + 1))
                nc.vector.tensor_copy(params[:, s], params_raw[:]).then_inc(w_low, 1)
                for n, (low, raw, high) in enumerate(((w1l, w1_raw, w1h), (w2l, w2_raw, w2h))):
                    dve.wait_ge(w_high, 2 * e + n + 1)
                    nc.vector.tensor_tensor(low[:, s], raw[:], high[:, s].bitcast(F32), ALU.subtract
                                            ).then_inc(w_low, 1)

            def normalize(g, s):
                for h in range(HALF):
                    dve.wait_ge(row_used[h], g + 1)
                    nc.vector.tensor_copy(goes_next[:, h:h + 1], xrow[:, h, D:XROW])
                    for k in range(KD):
                        nc.vector.tensor_scalar(xt[:, k, h * P:(h + 1) * P], x_bank[h][:, k * P:(k + 1) * P],
                                                params[:, s, GAIN + k:GAIN + k + 1], params[:, s, SHIFT + k:SHIFT + k + 1],
                                                ALU.mult, ALU.add).then_inc(xt_step, 1)
                dve.wait_ge(xt_step, XT_STEPS * g + XT_STEPS - 2)
                nc.vector.tensor_copy(xth[:], xt[:]).then_inc(xt_step, 1)
                dve.wait_ge(xt_step, XT_STEPS * g + XT_STEPS - 1)
                nc.vector.tensor_tensor(xtl[:], xt[:], xth[:].bitcast(F32), ALU.subtract).then_inc(xt_step, 1)

            def body(g, s, next_s, parameters):
                for j in range(JH):
                    dve.wait_ge(hid_high, JH * g + j + 1)
                    nc.vector.tensor_tensor(hidl[:, j, :], hid[:, j, :], hidh[:, j, :].bitcast(F32), ALU.subtract
                                            ).then_inc(hid_low, 1)
                dve.wait_ge(xt_step, XT_STEPS * (g + 1))
                for h in range(HALF):
                    dve.wait_ge(stored[h], 16 * g)
                    nc.vector.tensor_copy(goes_to[h][:], goes_next[:, h:h + 1]).then_inc(goes_ready[h], 1)
                for h in range(HALF):
                    dve.wait_ge(goes_ready[h], g + 1)
                dve.wait_ge(w_low, parameters)
                normalize(g + 1, next_s)
                for h in range(HALF):
                    dve.wait_ge(y_psum[h], g + 1)
                    nc.vector.tensor_tensor(yrow[:, h, :], y_bank[h][:, 0:D], params[:, s, B2:B2 + D], ALU.add
                                            ).then_inc(y_ready[h], 1)

            def expert(i, s, more):
                first, _, last = tiles_of(dve, 2 * i + s)
                if more:
                    for h in range(HALF):
                        dve.wait_ge(y_ready[h], first)
                    split_low(2 * i + s + 1, 1 - s)
                with dve.Fori(first, last) as g:
                    body(g, s, s, 3 * (2 * i + s + 1))
                body(last, s, 1 - s if more else s, 3 * (2 * i + s + (2 if more else 1)))

            split_low(0, 0)
            dve.wait_ge(w_low, 3)
            normalize(0, 0)
            over_experts(dve, expert)

        @block.gpsimd
        def _(pool):
            def load(e):
                def one(w):
                    return w[bass.ds(e, 1)]

                pool.wait_ge(w_low, 3 * e)
                pool.wait_ge(w_high, 2 * e)
                with nc.allow_non_contiguous_dma(reason="small rows of parameters, once an expert"):
                    for to, of in (
                        (w1_raw[:], one(W1).rearrange("o (k p) h -> p (o k) h", p=P)),
                        (w2_raw[:], one(W2).rearrange("o (j p) d -> p (o j) d", p=P)),
                        (params_raw[:, GAIN:GAIN + KD], one(ln_g).rearrange("o (k p) -> p (o k)", p=P)),
                        (params_raw[:, SHIFT:SHIFT + KD], one(ln_b).rearrange("o (k p) -> p (o k)", p=P)),
                        (params_raw[:, B1:B1 + JH], one(b1).rearrange("o (j p) -> p (o j)", p=P)),
                        (params_raw[:, B2:B2 + D], one(b2).to_broadcast([P, D])),
                    ):
                        pool.dma_start(to, of).then_inc(raw_loaded, 16)

            def scatters(e):
                first, end, _ = tiles_of(pool, e)
                with pool.Fori(first, end) as g:
                    after = value_of(pool, g + 1)
                    sent, sent_after = value_of(pool, 16 * g), value_of(pool, 16 * (g + 1))
                    for h in range(HALF):
                        pool.wait_ge(m["begun"], 1)
                        pool.wait_ge(goes_ready[h], after)
                        pool.wait_ge(y_ready[h], after)
                        pool.wait_ge(stored[0], sent_after if h else sent)
                        pool.wait_ge(stored[1], sent)
                        nc.gpsimd.indirect_dma_start(
                            y2, bass.IndirectOffsetOnAxis(ap=goes_to[h][:], axis=0), yrow[:, h, :], None
                        ).then_inc(stored[h], 16)
                return end

            load(0)
            load(1)
            with pool.Fori(0, NX - 2) as e:
                load(e + 2)
                scatters(e)
            scatters(NX - 2)
            end = scatters(NX - 1)
            for h in range(HALF):
                pool.wait_ge(stored[h], end * 16)


def combine_phase(nc, m, y2, out):
    with ExitStack() as ctx:
        def sb(name, shape, dt=F32):
            return ctx.enter_context(nc.sbuf_tensor(name, shape, dt))

        def sems(name, n=2):
            return [ctx.enter_context(nc.semaphore(f"{name}{k}")) for k in range(n)]

        y, mid, total = sb("c_y", [NP, 2, 2, D]), sb("c_mid", [NP, 2, D]), sb("c_total", [NP, 2, D])
        loaded, summed, stored = sems("c_loaded"), sems("c_summed"), sems("c_stored")
        block = ctx.enter_context(nc.Block())

        @block.sync
        def _(sp):
            with sp.Fori(0, NT // 2) as i:
                for u in range(2):
                    sp.wait_ge(summed[u], 2 * i)
                    sp.dma_start(y[:, u, :, :], y2[bass.ds((2 * i + u) * 2 * NP, 2 * NP), :]
                                 .rearrange("(p k) d -> p k d", k=2)).then_inc(loaded[u], 16)

        @block.vector
        def _(dve):
            with dve.Fori(0, NT // 2) as i:
                for u in range(2):
                    t = 2 * i + u
                    w = m["weights"][:, bass.ds(t, 1), :].rearrange("p a k -> p (a k)")
                    dve.wait_ge(loaded[u], 16 * (i + 1))
                    nc.vector.scalar_tensor_tensor(
                        mid[:, u, :], y[:, u, 0, :], w[:, 0:1], m["acc"][:, bass.ds(t, 1), 0:D].rearrange("p a d -> p (a d)"),
                        ALU.mult, ALU.add).then_inc(summed[u], 1)
                    dve.wait_ge(summed[u], 2 * i + 1)
                    dve.wait_ge(stored[u], 16 * i)
                    nc.vector.scalar_tensor_tensor(total[:, u, :], y[:, u, 1, :], w[:, 1:2], mid[:, u, :],
                                                   ALU.mult, ALU.add).then_inc(summed[u], 1)

        @block.scalar
        def _(act):
            with act.Fori(0, NT // 2) as i:
                for u in range(2):
                    act.wait_ge(summed[u], 2 * (i + 1))
                    act.dma_start(out[tile(2 * i + u), :], total[:, u, :]).then_inc(stored[u], 16)
            for u in range(2):
                act.wait_ge(stored[u], 16 * (NT // 2))


_INS = ['x', 'src', 'dst', 'L0_gnn_Wp', 'L0_gnn_a_src', 'L0_gnn_a_trg', 'L0_gnn_Wskip', 'L0_gnn_bias',
        'L0_ffn_Wr', 'L0_ffn_br', 'L0_ffn_ln_g', 'L0_ffn_ln_b', 'L0_ffn_W1', 'L0_ffn_b1', 'L0_ffn_W2', 'L0_ffn_b2']


def kernel(**inputs):
    import numpy as _np
    import concourse.bacc as _bacc
    from concourse import mybir as _mybir
    from concourse.bass_utils import run_bass_kernel_spmd as _run

    nc = _bacc.Bacc("TRN2", target_bir_lowering=False, num_devices=1)
    arrays, args = {}, []
    for name in _INS:
        a = _np.ascontiguousarray(inputs[name])
        arrays[f"in_{name}_dram"] = a
        args.append(nc.dram_tensor(f"in_{name}_dram", a.shape, _mybir.dt.from_np(a.dtype), kind="ExternalInput").ap())
    args.append(nc.dram_tensor("out_0_dram", (N, D), _mybir.dt.float32, kind="ExternalOutput").ap())
    gnn_ffn(nc, *args)
    r = _run(nc, [arrays], core_ids=[0])
    return r.results[0]["out_0_dram"]
```

```python
from contextlib import ExitStack

import concourse.bass as bass
from concourse import mybir

F32 = mybir.dt.float32
F32R = mybir.dt.float32r
BF16 = mybir.dt.bfloat16
I32 = mybir.dt.int32
U32 = mybir.dt.uint32
ALU = mybir.AluOpType
ACT = mybir.ActivationFunctionType
X = mybir.AxisListType.X

P = 128
N, D = 6250, 256
E = 200000
H, FO = 8, 32
NX, HID = 8, 1024
LN_EPS = 1e-5
SLOPE = 0.2
DEN_EPS = 1e-16

NP = 125
NT = N // NP
NODE_PARTS = (slice(0, 112), slice(112, NP))
KD = D // P
ROW = D + H

SUB = 128
SET, K = 3, 3
G = SET * K
DIV_BITS = 14
DIV_BY = -(-(1 << DIV_BITS) // G)
Q = 4
EROW = Q * SUB
ST = H + 2
NSUB = -(-E // SUB)
EC = -(-E // (P * EROW))
EFULL = E // EROW
ETAIL = E - EFULL * EROW
COLS = EC * P * Q
NO_NODE = 16384
BIG = 4096

BY_TABLE = "the chip's own tables hold it, clamped to this range"

TOK = 256
HALF = TOK // P
JH = HID // P
CAP = -(-(N + TOK) // TOK) * TOK
FILL = TOK
XROW = D + 1


def tile(t, n=NP):
    return bass.ds(t * n, n)


def value_of(engine, count):
    return engine.snap(engine.to_reg(count))


def m_v(mv, t):
    return mv[:, bass.ds(t, 1), :].rearrange("p a k -> p (a k)")


def gnn_ffn(nc, x, src, dst, Wp, a_src, a_trg, Wskip, bias, Wr, br, ln_g, ln_b, W1, b1, W2, b2, out):
    table = nc.dram_tensor("proj_table", (N, ROW), F32).ap()
    skip_rows = nc.dram_tensor("skip_rows", (N, D), F32).ap()
    xg = nc.dram_tensor("tokens_by_expert", (NX * CAP, XROW), F32).ap()
    y2 = nc.dram_tensor("results_by_token", (2 * N + P, D), F32).ap()

    with ExitStack() as ctx:
        def sb(name, shape, dt=F32):
            return ctx.enter_context(nc.sbuf_tensor(name, shape, dt))

        bank = [ctx.enter_context(nc.psum_tensor(f"bank{k}", [P, 512], F32)) for k in range(8)]
        m = dict(
            iota=sb("iota", [P, P]), iota_p=sb("iota_p", [P, 1]), ident=sb("ident", [P, P]),
            lower=sb("lower", [P, P]), ones=sb("ones", [P, P]), zero16=sb("zero16", [P, ROW], BF16),
            begun=ctx.enter_context(nc.semaphore("begun")), block_start=sb("block_start", [P, NT + 1]),
            cap_row=sb("cap_row", [P, NX]), ident_r=sb("ident_r", [P, P], F32R),
            st=sb("st", [NP, NT + 1, ST]), st_parts=sb("st_parts", [NP, NT + 1, 2, ST], F32R),
            acc=sb("acc", [NP, NT, ROW]), neg_bound=sb("neg_bound", [P, 1]),
            ln_eps=sb("ln_eps", [P, 1]), eps=sb("eps", [P, 1]),
            gaps=sb("gaps", [NP, NT]), warm=[sb(f"warm{k}", [P, 1]) for k in range(3)], weights=sb("weights", [NP, NT, 2]),
            result_row=sb("result_row", [NP, NT, 2]), counts=sb("counts", [1, NX, 4], I32),
            br=sb("br", [NP, NX]), wr=sb("wr", [P, KD, NX]),
        )
        with ExitStack() as edge_ctx:
            def esb(name, shape, dt=F32):
                return edge_ctx.enter_context(nc.sbuf_tensor(name, shape, dt))

            m.update(src_tab=esb("src_tab", [P, COLS], I32), dst_tab=esb("dst_tab", [P, COLS]),
                     ranges=esb("ranges", [1, NT, 4], I32))
            edge_tables(nc, m, bank, src, dst)
            node_phase(nc, m, bank, x, Wp, a_src, a_trg, Wskip, bias, Wr, br, table, skip_rows)
            edge_phase(nc, m, bank, table)
        route_phase(nc, m, bank, x, skip_rows, xg)
        expert_phase(nc, m, bank, xg, y2, ln_g, ln_b, W1, b1, W2, b2)
        combine_phase(nc, m, y2, out)


def edge_tables(nc, m, bank, src, dst):
    with ExitStack() as ctx:
        def sb(name, shape, dt=F32):
            return ctx.enter_context(nc.sbuf_tensor(name, shape, dt))

        def sem(name):
            return ctx.enter_context(nc.semaphore(name))

        raw = {"src": sb("src_raw", [P, EC, EROW], I32), "dst": sb("dst_raw", [P, EC, EROW], I32)}
        rows = {"src": sb("src_rows", [P, EC, EROW]), "dst": sb("dst_rows", [P, EC, EROW])}
        lowest = sb("lowest", [P, EC * Q])
        highest = sb("highest", [P, EC * Q])
        number = sb("number", [P, EC * Q])
        starts = sb("starts", [P, NT])
        starts_ok = sb("starts_ok", [P, NT, EC * Q])
        touched = sb("touched", [P, NT, EC * Q])
        scored = sb("scored", [P, 2, NT, EC * Q])
        best = sb("best", [P, 2, NT])
        best_col = sb("best_col", [2 * NT, 1])
        row, whole = sb("range_row", [1, 8, NT]), sb("range_whole", [1, NT], I32)
        iota_done, consts, loaded = sem("iota_done"), sem("consts"), sem("edges_loaded")
        pe_input, turned = sem("pe_input"), sem("turned")
        dst_out, src_out = sem("dst_out"), sem("src_out")
        dve_step, pe_step = sem("range_dve"), sem("range_pe")
        iota, ident = m["iota"], m["ident"]

        block = ctx.enter_context(nc.Block())

        @block.gpsimd
        def _(pool):
            nc.gpsimd.iota(iota[:], [[1, P]], base=0, channel_multiplier=0,
                           allow_small_or_imprecise_dtypes=True).then_inc(iota_done, 1)
            nc.gpsimd.iota(m["iota_p"][:], [[0, 1]], base=0, channel_multiplier=1,
                           allow_small_or_imprecise_dtypes=True).then_inc(iota_done, 1)
            nc.gpsimd.iota(m["result_row"][:], [[2 * NP, NT], [1, 2]], base=0, channel_multiplier=2,
                           allow_small_or_imprecise_dtypes=True).then_inc(iota_done, 1)
            nc.gpsimd.iota(number[:], [[P * Q, EC], [1, Q]], base=1, channel_multiplier=Q,
                           allow_small_or_imprecise_dtypes=True).then_inc(iota_done, 1)
            nc.gpsimd.iota(starts[:], [[NP, NT]], base=0, channel_multiplier=0,
                           allow_small_or_imprecise_dtypes=True).then_inc(iota_done, 1)

        @block.sync
        def _(sp):
            sp.wait_ge(consts, 2)
            for name, flat in (("dst", dst), ("src", src)):
                to = raw[name]
                whole = (EC - 1) * P * EROW
                sp.dma_start(to[:, 0:EC - 1, :], flat[0:whole].rearrange("(c p e) -> p c e", p=P, e=EROW)
                             ).then_inc(loaded, 16)
                rest = EFULL - (EC - 1) * P
                sp.dma_start(to[0:rest, EC - 1, :], flat[whole:whole + rest * EROW].rearrange("(p e) -> p e", e=EROW)
                             ).then_inc(loaded, 16)
                sp.dma_start(to[rest:rest + 1, EC - 1, 0:ETAIL], flat[EFULL * EROW:E].rearrange("(p e) -> p e", p=1)
                             ).then_inc(loaded, 16)

        @block.vector
        def _(dve):
            steps = [0]

            def step(ins):
                steps[0] += 1
                ins.then_inc(dve_step, 1)

            def settle():
                dve.wait_ge(dve_step, steps[0])

            nc.vector.memset(raw["dst"][:, EC - 1, :], NO_NODE).then_inc(consts, 1)
            nc.vector.memset(raw["src"][:, EC - 1, :], 0).then_inc(consts, 1)
            nc.vector.memset(m["ones"][:], 1.0).then_inc(m["begun"], 1)
            nc.vector.memset(m["zero16"][:], 0.0)
            nc.vector.memset(m["st"][:], 1.0)
            nc.vector.memset(m["ln_eps"][:], LN_EPS)
            dve.wait_ge(iota_done, 5)
            nc.vector.tensor_scalar(ident[:], iota[:], m["iota_p"][:], None, ALU.is_equal).then_inc(consts, 1)
            nc.vector.tensor_scalar(m["lower"][:], iota[:], m["iota_p"][:], None, ALU.is_gt).then_inc(consts, 1)
            nc.vector.tensor_scalar(m["ident_r"][:], iota[:], m["iota_p"][:], None, ALU.is_equal)
            nc.vector.memset(m["block_start"][:, NT:NT + 1], 0.0)
            nc.vector.tensor_copy(m["block_start"][:, 0:NT], starts[:]).then_inc(consts, 1)
            nc.vector.tensor_scalar(m["cap_row"][:], iota[:, 0:NX], float(CAP), None, ALU.mult).then_inc(consts, 1)
            dve.wait_ge(loaded, 16 * 6)
            for name in ("dst", "src"):
                nc.vector.tensor_copy(rows[name][:], raw[name][:]).then_inc(pe_input, 1)
            for c in range(EC):
                dve.wait_ge(turned, 2 * c + 1)
                nc.vector.tensor_copy(
                    m["dst_tab"][:, c * P * Q:(c + 1) * P * Q].rearrange("p (r j) -> p j r", j=Q),
                    bank[2 * (c % 2)][:].rearrange("p (j r) -> p j r", j=Q)).then_inc(dst_out, 1)
            by_sub = rows["dst"][:].rearrange("p c (j e) -> p (c j) e", j=Q)
            step(nc.vector.tensor_reduce(lowest[:], by_sub, X, ALU.min))
            step(nc.vector.tensor_reduce(highest[:], by_sub, X, ALU.max))
            settle()
            shape = [P, NT, EC * Q]

            def over_blocks(v):
                return v[:].unsqueeze(1).to_broadcast(shape)

            start_b = starts[:].unsqueeze(2).to_broadcast(shape)
            step(nc.vector.tensor_tensor(starts_ok[:], over_blocks(highest), start_b, ALU.is_ge))
            step(nc.vector.tensor_scalar(lowest[:], lowest[:], -float(NP - 1), None, ALU.add))
            settle()
            step(nc.vector.tensor_tensor(touched[:], start_b, over_blocks(lowest), ALU.is_ge))
            settle()
            step(nc.vector.tensor_tensor(touched[:], touched[:], starts_ok[:], ALU.mult))
            settle()
            step(nc.vector.tensor_tensor(scored[:, 0], touched[:], over_blocks(number), ALU.mult))
            settle()
            step(nc.vector.tensor_scalar(number[:], number[:], -1.0, float(BIG), ALU.mult, ALU.add))
            settle()
            step(nc.vector.tensor_tensor(scored[:, 1], touched[:], over_blocks(number), ALU.mult))
            settle()
            nc.vector.tensor_reduce(best[:], scored[:], X, ALU.max).then_inc(pe_input, 1)
            dve.wait_ge(pe_step, 1)
            nc.vector.tensor_reduce(best_col[:], bank[4][0:2 * NT, 0:P], X, ALU.max).then_inc(pe_input, 1)
            dve.wait_ge(pe_step, 2)
            LAST, FIRST, LO, END, CNT, GE, GS, ZERO = range(8)
            step(nc.vector.tensor_copy(row[:, LAST:FIRST + 1, :].rearrange("p a b -> p (a b)"),
                                       bank[5][0:1, 0:2 * NT]))
            step(nc.vector.memset(row[:, ZERO], 0.0))
            settle()
            step(nc.vector.tensor_scalar(row[:, LO], row[:, FIRST], -1.0, float(BIG - 1), ALU.mult, ALU.add))
            settle()
            step(nc.vector.tensor_scalar(row[:, LO], row[:, LO], float(NSUB - 1), 0.0, ALU.min, ALU.max))
            settle()
            step(nc.vector.tensor_tensor(row[:, END], row[:, LAST], row[:, LO], ALU.subtract))
            settle()
            step(nc.vector.tensor_scalar(row[:, END], row[:, END], 1.0, float(G - 1), ALU.max, ALU.add))
            settle()
            step(nc.vector.tensor_scalar(row[:, END], row[:, END], float(DIV_BY), None, ALU.mult))
            settle()
            step(nc.vector.tensor_copy(whole[:], row[:, END]))
            settle()
            step(nc.vector.tensor_scalar(whole[:], whole[:], DIV_BITS, None, ALU.arith_shift_right))
            settle()
            step(nc.vector.tensor_copy(row[:, CNT], whole[:]))
            settle()
            step(nc.vector.tensor_tensor_scan(row[:, GE], row[:, CNT], row[:, ZERO], 0.0, ALU.add, ALU.add))
            settle()
            step(nc.vector.tensor_tensor(row[:, GS], row[:, GE], row[:, CNT], ALU.subtract))
            settle()
            step(nc.vector.tensor_scalar(row[:, GS], row[:, GS], 1.0, None, ALU.add))
            settle()
            for k, r in enumerate((LO, GS, GE)):
                step(nc.vector.tensor_copy(m["ranges"][:, :, k], row[:, r]))
            step(nc.vector.tensor_copy(m["ranges"][:, 0:NT - 1, 3], row[:, LO, 1:NT]))
            step(nc.vector.tensor_copy(m["ranges"][:, NT - 1, 3:4], row[:, LO, NT - 1:NT]))
            settle()

        @block.tensor
        def _(pe):
            pe.wait_ge(consts, 3)
            for c in range(EC):
                for k, name in enumerate(("dst", "src")):
                    if c == 0:
                        pe.wait_ge(pe_input, k + 1)
                    if c >= 2:
                        pe.wait_ge((dst_out, src_out)[k], c - 1)
                    for j in range(Q):
                        mm = nc.tensor.transpose(bank[2 * (c % 2) + k][:, j * P:(j + 1) * P],
                                                 rows[name][:, c, j * P:(j + 1) * P], ident[:])
                    mm.then_inc(turned, 1)
            pe.wait_ge(pe_input, 3)
            nc.tensor.transpose(bank[4][0:2 * NT, 0:P], best[:].rearrange("p a b -> p (a b)"),
                                ident[:]).then_inc(pe_step, 1)
            pe.wait_ge(pe_input, 4)
            nc.tensor.matmul(bank[5][0:1, 0:2 * NT], best_col[:], ident[0:2 * NT, 0:2 * NT],
                             start=True, stop=True).then_inc(pe_step, 1)

        @block.scalar
        def _(act):
            for c in range(EC):
                act.wait_ge(turned, 2 * c + 2)
                nc.scalar.copy(m["src_tab"][:, c * P * Q:(c + 1) * P * Q].rearrange("p (r j) -> p j r", j=Q),
                               bank[2 * (c % 2) + 1][:].rearrange("p (j r) -> p j r", j=Q)).then_inc(src_out, 1)


def node_phase(nc, m, bank, x, Wp, a_src, a_trg, Wskip, bias, Wr, br, table, skip_rows):
    with ExitStack() as ctx:
        def sb(name, shape, dt=F32):
            return ctx.enter_context(nc.sbuf_tensor(name, shape, dt))

        def sem(name):
            return ctx.enter_context(nc.semaphore(name))

        def sems(name, n=2):
            return [sem(f"{name}{k}") for k in range(n)]

        wp, wskip = sb("wp", [P, KD, D]), sb("wskip", [P, KD, D])
        a_cols = sb("a_cols", [P, 2, KD])
        a_heads = sb("a_heads", [P, KD, 2 * H])
        bias_b = sb("bias_b", [NP, D])
        w_table, w_skip = sb("w_table", [P, KD, ROW]), sb("w_skip", [P, KD, ROW])
        xin, xn, xt = sb("xin", [NP, 2, D]), sb("xn", [NP, 2, D]), sb("xt", [P, 2, KD, NP])
        stats, mv = sb("stats", [NP, 2, 6]), sb("mv", [NP, 2, 2])
        std, rstd = sb("std", [NP, 2]), sb("rstd", [NP, 2])
        trow, srow = sb("trow", [NP, 2, ROW]), sb("srow", [NP, 2, D])
        maxima, top, bound = sb("maxima", [NP, 2, H]), sb("top", [P, 2]), sb("bound", [P, 2])
        begun, st_high = m["begun"], sem("st_high")
        w_loaded, heads_zero, heads = sem("w_loaded"), sem("heads_zero"), sem("heads")
        w_turned, w_ready, max_step, max_pe = sem("w_turned"), sem("w_ready"), sem("max_step"), sem("max_pe")
        x_loaded, norm_step, std_done, xn_ready = (sems(s) for s in ("x_loaded", "norm_step", "std_done", "xn_ready"))
        xt_psum, xt_ready, projected, trow_ready, srow_ready, dve_out = (sems(s) for s in (
            "xt_psum", "xt_ready", "projected", "trow_ready", "srow_ready", "dve_out"))
        trow_stored, srow_stored = sems("trow_stored"), sems("srow_stored")
        block = ctx.enter_context(nc.Block())
        LOADS = 7

        @block.sync
        def _(sp):
            sp.dma_start(wp[:], Wp.rearrange("(c p) d -> p c d", p=P)).then_inc(w_loaded, 16)
            sp.dma_start(wskip[:], Wskip.rearrange("(c p) d -> p c d", p=P)).then_inc(w_loaded, 16)
            with nc.allow_non_contiguous_dma(reason="256 words, once"):
                for k, a in enumerate((a_src, a_trg)):
                    sp.dma_start(a_cols[:, k, :], a.rearrange("o (c q) f -> (q f) (o c)", c=KD)).then_inc(w_loaded, 16)
            sp.dma_start(bias_b[:], bias.rearrange("(o d) -> o d", o=1).to_broadcast([NP, D])).then_inc(w_loaded, 16)
            sp.dma_start(m["wr"][:], Wr.rearrange("(k p) e -> p k e", p=P)).then_inc(w_loaded, 16)
            sp.dma_start(m["br"][:], br.rearrange("(o e) -> o e", o=1).to_broadcast([NP, NX])).then_inc(w_loaded, 16)
            with sp.Fori(0, NT // 2) as i:
                for u in range(2):
                    sp.wait_ge(xn_ready[u], i)
                    sp.dma_start(xin[:, u, :], x[tile(2 * i + u), :]).then_inc(x_loaded[u], 16)

        @block.vector
        def _(dve):
            nc.vector.memset(a_heads[:], 0.0).then_inc(heads_zero, 1)
            nc.vector.memset(maxima[:], -3e38).then_inc(heads_zero, 1)
            dve.wait_ge(w_loaded, 16 * LOADS)
            dve.wait_ge(heads_zero, 2)
            for k in range(2):
                for c in range(KD):
                    for q in range(P // FO):
                        at = slice(q * FO, (q + 1) * FO)
                        h = k * H + c * (P // FO) + q
                        nc.vector.tensor_copy(a_heads[at, c, h:h + 1], a_cols[at, k, c:c + 1]).then_inc(heads, 1)
            for k in range(KD):
                dve.wait_ge(w_turned, k + 1)
                for w, b, s in ((w_table, 3 * k, 0), (w_skip, 3 * k + 1, H)):
                    nc.vector.tensor_copy(w[:, k, 0:D], bank[b][:, 0:D]).then_inc(w_ready, 1)
                    nc.vector.tensor_copy(w[:, k, D:ROW], bank[3 * k + 2][:, s:s + H]).then_inc(w_ready, 1)
            def normalize(i):
                for u in range(2):
                    dve.wait_ge(x_loaded[u], 16 * (i + 1))
                    nc.vector.bn_stats(stats[:, u, :], xin[:, u, :]).then_inc(norm_step[u], 1)
                    after = value_of(dve, 3 * i + 1)
                    dve.wait_ge(begun, 1)
                    dve.wait_ge(norm_step[u], after)
                    nc.vector.bn_aggr(mv[:, u, :], stats[:, u, :]).then_inc(norm_step[u], 1)
                    dve.wait_ge(std_done[u], i + 1)
                    nc.vector.reciprocal(rstd[:, u:u + 1], std[:, u:u + 1]).then_inc(norm_step[u], 1)
                    dve.wait_ge(norm_step[u], 3 * i + 3)
                    dve.wait_ge(xt_psum[u], i)
                    nc.vector.tensor_scalar(xn[:, u, :], xin[:, u, :], mv[:, u, 0:1], rstd[:, u:u + 1],
                                            ALU.subtract, ALU.mult).then_inc(xn_ready[u], 1)

            def results(i):
                for u in range(2):
                    t = 2 * i + u
                    ps = bank[4 + u]
                    dve.wait_ge(projected[u], i + 1)
                    dve.wait_ge(srow_stored[u], 16 * i)
                    nc.vector.tensor_tensor(srow[:, u, :], ps[0:NP, 0:D], bias_b[:], ALU.add
                                            ).then_inc(srow_ready[u], 1)
                    nc.vector.tensor_copy(m["st"][:, bass.ds(t, 1), 0:H].rearrange("p a h -> p (a h)"),
                                          ps[0:NP, D:ROW])
                    dve.wait_ge(dve_out[1 - u], 2 * i + 2 * u)
                    dve.wait_ge(trow_ready[u], i + 1)
                    nc.vector.tensor_tensor(maxima[:, 0, :], maxima[:, 0, :], trow[:, u, D:ROW], ALU.max
                                            ).then_inc(dve_out[u], 1)
                    nc.vector.tensor_tensor(maxima[:, 1, :], maxima[:, 1, :], ps[0:NP, D:ROW], ALU.max
                                            ).then_inc(dve_out[u], 1)

            normalize(0)
            with dve.Fori(0, NT // 2 - 1) as i:
                normalize(i + 1)
                results(i)
            results(NT // 2 - 1)
            dve.wait_ge(dve_out[1], NT)
            nc.vector.tensor_copy(m["st_parts"][:, :, 0], m["st"][:]).then_inc(st_high, 1)
            dve.wait_ge(st_high, 1)
            nc.vector.tensor_tensor(m["st_parts"][:, :, 1], m["st"][:], m["st_parts"][:, :, 0].bitcast(F32), ALU.subtract)
            nc.vector.tensor_reduce(top[0:NP, :], maxima[:], X, ALU.max).then_inc(max_step, 1)
            dve.wait_ge(max_pe, 1)
            nc.vector.tensor_reduce(bound[0:2, 0:1], bank[6][0:2, 0:NP], X, ALU.max).then_inc(max_step, 1)
            dve.wait_ge(max_pe, 2)
            nc.vector.tensor_copy(bound[:, 1:2], bank[7][:, 0:1]).then_inc(max_step, 1)
            dve.wait_ge(max_step, 3)
            nc.vector.tensor_scalar(top[:, 0:1], bound[:, 1:2], SLOPE, None, ALU.mult).then_inc(max_step, 1)
            dve.wait_ge(max_step, 4)
            nc.vector.tensor_tensor(top[:, 1:2], top[:, 0:1], bound[:, 1:2], ALU.max).then_inc(max_step, 1)
            dve.wait_ge(max_step, 5)
            nc.vector.tensor_scalar(m["neg_bound"][:], top[:, 1:2], -1.0, None, ALU.mult)

        @block.tensor
        def _(pe):
            pe.wait_ge(w_loaded, 16 * LOADS)
            for k in range(KD):
                at = slice(k * P, (k + 1) * P)
                for c in range(KD):
                    nc.tensor.transpose(bank[3 * k][:, c * P:(c + 1) * P], wp[:, c, at], m["ident"][:])
                    nc.tensor.transpose(bank[3 * k + 1][:, c * P:(c + 1) * P], wskip[:, c, at], m["ident"][:])
                if k == 0:
                    pe.wait_ge(heads, 2 * H)
                for c in range(KD):
                    mm = nc.tensor.matmul(bank[3 * k + 2][:, 0:2 * H], wp[:, c, at], a_heads[:, c, :],
                                          start=(c == 0), stop=(c == KD - 1))
                mm.then_inc(w_turned, 1)
            pe.wait_ge(w_ready, 4 * KD)
            def turn(i):
                for u in range(2):
                    pe.wait_ge(xn_ready[u], i + 1)
                    pe.wait_ge(xt_ready[u], i)
                    for k in range(KD):
                        mm = nc.tensor.transpose(bank[u][:, k * P:k * P + NP], xn[:, u, k * P:(k + 1) * P],
                                                 m["ident"][0:NP, 0:NP])
                    mm.then_inc(xt_psum[u], 1)

            def project(i):
                for u in range(2):
                    pe.wait_ge(xt_ready[u], i + 1)
                    pe.wait_ge(trow_ready[u], i)
                    pe.wait_ge(dve_out[u], 2 * i)
                    for w, b in ((w_table, 2 + u), (w_skip, 4 + u)):
                        for k in range(KD):
                            mm = nc.tensor.matmul(bank[b][0:NP, 0:ROW], xt[:, u, k, :], w[:, k, :],
                                                  start=(k == 0), stop=(k == KD - 1))
                    mm.then_inc(projected[u], 1)

            turn(0)
            with pe.Fori(0, NT // 2 - 1) as i:
                project(i)
                turn(i + 1)
            project(NT // 2 - 1)
            pe.wait_ge(max_step, 1)
            nc.tensor.transpose(bank[6][0:2, 0:NP], top[0:NP, :], m["ident"][0:NP, 0:NP]).then_inc(max_pe, 1)
            pe.wait_ge(max_step, 2)
            nc.tensor.matmul(bank[7][:, 0:1], m["ones"][0:2, :], bound[0:2, 0:1], start=True,
                             stop=True).then_inc(max_pe, 1)

        @block.scalar
        def _(act):
            act.wait_ge(begun, 1)
            nc.scalar.activation(m["warm"][1][:], m["ln_eps"][:], ACT.Sqrt)
            def deviations(i):
                for u in range(2):
                    act.wait_ge(norm_step[u], 3 * i + 2)
                    nc.scalar.activation(std[:, u:u + 1], mv[:, u, 1:2], ACT.Sqrt, bias=m["ln_eps"][0:NP, :]
                                         ).then_inc(std_done[u], 1)

            def copy_turned(i, u):
                act.wait_ge(xt_psum[u], i + 1)
                act.wait_ge(projected[u], i)
                nc.scalar.copy(xt[:, u, :, :], bank[u][:, 0:KD * P].rearrange("p (k n) -> p k n", k=KD)[:, :, 0:NP]
                               ).then_inc(xt_ready[u], 1)

            def results(i, u):
                t = 2 * i + u
                act.wait_ge(projected[u], i + 1)
                act.wait_ge(trow_stored[u], 16 * i)
                act.wait_ge(dve_out[u], 2 * i)
                nc.scalar.copy(trow[:, u, :], bank[2 + u][0:NP, 0:ROW]).then_inc(trow_ready[u], 1)

            def store(i, u):
                t = 2 * i + u
                act.wait_ge(trow_ready[u], i + 1)
                act.dma_start(table[tile(t), :], trow[:, u, :]).then_inc(trow_stored[u], 16)
                act.wait_ge(srow_ready[u], i + 1)
                act.dma_start(skip_rows[tile(t), :], srow[:, u, :]).then_inc(srow_stored[u], 16)

            deviations(0)
            for u in range(2):
                copy_turned(0, u)
            with act.Fori(0, NT // 2 - 1) as i:
                deviations(i + 1)
                for u in range(2):
                    copy_turned(i + 1, u)
                    results(i, u)
                for u in range(2):
                    store(i, u)
            for u in range(2):
                results(NT // 2 - 1, u)
                store(NT // 2 - 1, u)
            for u in range(2):
                act.wait_ge(trow_stored[u], 16 * (NT // 2))
                act.wait_ge(srow_stored[u], 16 * (NT // 2))


def edge_phase(nc, m, bank, table):
    with ExitStack() as ctx:
        def sb(name, shape, dt=F32):
            return ctx.enter_context(nc.sbuf_tensor(name, shape, dt))

        def sem(name):
            return ctx.enter_context(nc.semaphore(name))

        def sems(*names):
            return [[sem(f"{name}{k}") for k in range(K)] for name in names]

        def tiles(name, shape, dt=F32):
            return [sb(f"{name}{k}", shape, dt) for k in range(K)]

        idx, rows = tiles("idx", [P, SET], I32), tiles("rows", [P, SET, ROW])
        onehot, onehot_t = tiles("onehot", [P, SET, NP], F32R), tiles("onehot_t", [NP, SET * P], F32R)
        half_score, raw_score, score = (tiles(name, [P, SET, H]) for name in ("half_score", "raw_score", "score"))
        weighed = tiles("weighed", [P, SET, ROW])
        high, low = tiles("high", [P, SET, ROW], F32R), tiles("low", [P, SET, ROW], F32R)
        masked, runmax = tiles("masked", [P, SET, H]), tiles("runmax", [P, SET, H])
        top, peak = sb("edge_top", [P, K + 1]), sb("peak", [1, 1])
        acc_bank, turn_bank = bank[0], bank[1:1 + K]
        z = [b[:, 0:SET * 2 * ST].rearrange("p (s h) -> p s h", s=SET) for b in bank[1 + K:1 + 2 * K]]
        idx_ready, gathered, onehot_ready, turned, turn_copied, z_ready = sems(
            "idx_ready", "gathered", "onehot_ready", "turned", "turn_copied", "z_ready")
        half_added, added, scored, weight_ready, rounded = sems("half_added", "added", "scored", "weight_ready", "rounded")
        weighed_done, max_done, low_done, sum_done = sems(
            "weighed_done", "max_done", "low_done", "sum_done")
        begun = m["begun"]
        block_summed, acc_done = sem("block_summed"), sem("acc_done")
        peak_dve = sem("peak_dve")
        block = ctx.enter_context(nc.Block())

        def over_steps(engine, b, body):
            _, (lo, first, last, next_lo) = nc.values_load_multi_w_load_instructions(
                m["ranges"][0:1, bass.ds(b, 1), 0:4].rearrange("p a k -> p (a k)"),
                engines=[engine.engine], min_val=0, max_val=NT * NSUB,
                skip_runtime_bounds_check_because=BY_TABLE)
            first, last = (nc.s_assert_within(v, 1, NT * NSUB) for v in (first, last))

            def column(s):
                return nc.s_assert_within(engine.snap((s - first) * G + lo), 0, COLS - 2 * G,
                                         skip_runtime_bounds_check_because=BY_TABLE)

            with engine.Fori(first, last) as s:
                col = column(s)
                body(s, col, col + G, b)
            next_col = nc.s_assert_within(next_lo, 0, NSUB, skip_runtime_bounds_check_because=BY_TABLE)
            body(last, column(last), next_col, b + 1)

        @block.gpsimd
        def _(pool):
            def gather(s, *_):
                now = value_of(pool, s)
                for k in range(K):
                    pool.wait_ge(begun, 1)
                    pool.wait_ge(idx_ready[k], now)
                    pool.wait_ge(weighed_done[k], now)
                    for i in range(SET):
                        nc.gpsimd.indirect_dma_start(
                            rows[k][:, i, :], None, table,
                            bass.IndirectOffsetOnAxis(ap=idx[k][:, i:i + 1], axis=0)).then_inc(gathered[k], 16)

            with pool.Fori(0, NT) as b:
                _, (first, last) = nc.values_load_multi_w_load_instructions(
                    m["ranges"][0:1, bass.ds(b, 1), 1:3].rearrange("p a k -> p (a k)"),
                    engines=[pool.engine], min_val=0, max_val=NT * NSUB)
                with pool.Fori(first, last + 1) as s:
                    gather(s)

        @block.tensor
        def _(pe):
            def turn(k, s):
                pe.wait_ge(onehot_ready[k], s)
                for i in range(SET):
                    mm = nc.tensor.matmul(turn_bank[k][0:NP, i * P:(i + 1) * P], onehot[k][:, i, :],
                                          m["ident_r"][:], start=True, stop=True)
                mm.then_inc(turned[k], 1)

            def target_scores(k, s, b):
                pe.wait_ge(turn_copied[k], s)
                pe.wait_ge(max_done[k], 2 * s)
                for i in range(SET):
                    mm = nc.tensor.matmul(z[k][:, i, :], onehot_t[k][:, i * P:(i + 1) * P],
                                          m["st_parts"][:, bass.ds(b, 1)].rearrange("p a c h -> p (a c h)"),
                                          start=True, stop=True)
                mm.then_inc(z_ready[k], 1)

            def sum_high(k, s):
                pe.wait_ge(rounded[k], s)
                for i in range(SET):
                    nc.tensor.matmul(acc_bank[0:NP, 0:ROW], onehot[k][:, i, :], high[k][:, i, :],
                                     start=False, stop=False, skip_group_check=True)

            def sum_low(k, s):
                pe.wait_ge(low_done[k], s + 1)
                for i in range(SET):
                    mm = nc.tensor.matmul(acc_bank[0:NP, 0:ROW], onehot[k][:, i, :], low[k][:, i, :],
                                          start=False, stop=False, skip_group_check=True)
                mm.then_inc(sum_done[k], 1)

            def body(s, col, next_col, next_b, b):
                turn(2, s)
                sum_high(0, s)
                target_scores(2, s, b)
                sum_low(0, s)
                sum_high(1, s)
                turn(0, s + 1)
                sum_low(1, s)
                target_scores(0, s + 1, next_b)
                sum_high(2, s)
                turn(1, s + 1)
                sum_low(2, s)
                target_scores(1, s + 1, next_b)

            for k in range(K):
                pe.sem_inc(sum_done[k], 1)
            for k in range(2):
                turn(k, 1)
                target_scores(k, 1, 0)
            with pe.Fori(0, NT) as b:
                pe.wait_ge(acc_done, b + 1)
                nc.tensor.matmul(acc_bank[0:NP, 0:ROW], m["zero16"][:, 0:NP], m["zero16"][:], start=True,
                                 stop=False, skip_group_check=True)
                over_steps(pe, b, lambda s, col, next_col, next_b: body(s, col, next_col, next_b, b))
                nc.tensor.matmul(acc_bank[0:NP, 0:ROW], m["zero16"][:, 0:NP], m["zero16"][:], start=False,
                                 stop=True, skip_group_check=True).then_inc(block_summed, 1)
            pe.wait_ge(peak_dve, K + 1)
            nc.tensor.transpose(bank[7][0:1, 0:P], top[:, K:K + 1], m["ident"][:]).then_inc(block_summed, 1)
            pe.wait_ge(peak_dve, K + 2)
            nc.tensor.matmul(bank[7][:, P:P + 1], m["ones"][0:1, :], peak[:], start=True, stop=True).then_inc(block_summed, 1)

        @block.vector
        def _(dve):
            def compare(k, s, col, b):
                dve.wait_ge(sum_done[k], s)
                shape = [P, SET, NP]
                nc.vector.scalar_tensor_tensor(
                    onehot[k][:], m["iota"][:, 0:NP].unsqueeze(1).to_broadcast(shape),
                    m["block_start"][:, bass.ds(b, 1)],
                    m["dst_tab"][:, bass.ds(col + k * SET, SET)].unsqueeze(2).to_broadcast(shape),
                    ALU.add, ALU.is_equal).then_inc(onehot_ready[k], 1)

            def add(k, s):
                dve.wait_ge(z_ready[k], s)
                dve.wait_ge(gathered[k], 16 * SET * s)
                nc.vector.tensor_tensor(half_score[k][:], rows[k][:, :, D:ROW], z[k][:, :, 0:H], ALU.add
                                        ).then_inc(half_added[k], 1)
                dve.wait_ge(half_added[k], s)
                nc.vector.tensor_tensor(raw_score[k][:], half_score[k][:], z[k][:, :, ST:ST + H], ALU.add
                                        ).then_inc(added[k], 1)
                dve.wait_ge(added[k], s)
                nc.vector.scalar_tensor_tensor(score[k][:], raw_score[k][:], SLOPE, raw_score[k][:],
                                               ALU.mult, ALU.max).then_inc(scored[k], 1)

            def weigh(k, s):
                dve.wait_ge(weight_ready[k], s)
                shape = [P, SET, H, FO]
                nc.vector.tensor_tensor(
                    weighed[k][:, :, 0:D].rearrange("p s (h f) -> p s h f", h=H),
                    rows[k][:, :, 0:D].rearrange("p s (h f) -> p s h f", h=H),
                    weighed[k][:, :, D:ROW].unsqueeze(3).to_broadcast(shape), ALU.mult).then_inc(weighed_done[k], 1)

            def largest(k, s):
                nc.vector.tensor_tensor(masked[k][:], weighed[k][:, :, D:ROW],
                                        z[k][:, :, H:H + 1].to_broadcast([P, SET, H]), ALU.mult
                                        ).then_inc(max_done[k], 1)
                dve.wait_ge(max_done[k], 2 * s + 1)
                nc.vector.tensor_tensor(runmax[k][:], runmax[k][:], masked[k][:], ALU.max).then_inc(max_done[k], 1)

            def remainder(k, s):
                dve.wait_ge(rounded[k], s)
                nc.vector.tensor_tensor(low[k][:], weighed[k][:], high[k][:].bitcast(F32), ALU.subtract
                                        ).then_inc(low_done[k], 1)

            def body(s, col, next_col, next_b, b):
                add(0, s)
                weigh(0, s)
                compare(2, s, col, b)
                add(1, s)
                largest(0, s)
                remainder(0, s)
                weigh(1, s)
                add(2, s)
                largest(1, s)
                remainder(1, s)
                compare(0, s + 1, next_col, next_b)
                weigh(2, s)
                largest(2, s)
                compare(1, s + 1, next_col, next_b)
                remainder(2, s)

            for k in range(K):
                for used in (weighed_done, max_done, low_done):
                    dve.sem_inc(used[k], 1)
                nc.vector.memset(runmax[k][:], 0.0).then_inc(max_done[k], 1)
            _, (lo,) = nc.values_load_multi_w_load_instructions(
                m["ranges"][0:1, 0, 0:1], engines=[dve.engine], min_val=0, max_val=NSUB)
            for k in range(2):
                compare(k, 1, lo, 0)
            with dve.Fori(0, NT) as b:
                over_steps(dve, b, lambda s, col, next_col, next_b: body(s, col, next_col, next_b, b))
            dve.wait_ge(block_summed, NT)
            for k in range(K):
                nc.vector.tensor_reduce(top[:, k:k + 1], runmax[k][:].rearrange("p s h -> p (s h)"), X, ALU.max
                                        ).then_inc(peak_dve, 1)
            dve.wait_ge(peak_dve, K)
            nc.vector.tensor_reduce(top[:, K:K + 1], top[:, 0:K], X, ALU.max).then_inc(peak_dve, 1)
            dve.wait_ge(block_summed, NT + 1)
            nc.vector.tensor_reduce(peak[:], bank[7][0:1, 0:P], X, ALU.max).then_inc(peak_dve, 1)
            dve.wait_ge(block_summed, NT + 2)
            nc.vector.tensor_scalar(m["eps"][:], bank[7][:, P:P + 1], DEN_EPS, None, ALU.mult)

        @block.scalar
        def _(act):
            def indices(k, s, col):
                nc.scalar.copy(idx[k][:], m["src_tab"][:, bass.ds(col + k * SET, SET)]).then_inc(idx_ready[k], 1)

            def copy_turned(k, s):
                act.wait_ge(turned[k], s)
                nc.scalar.copy(onehot_t[k][:], turn_bank[k][0:NP, 0:SET * P]).then_inc(turn_copied[k], 1)

            def exponentials(k, s):
                act.wait_ge(scored[k], s)
                act.wait_ge(low_done[k], s)
                nc.scalar.activation(weighed[k][:, :, D:ROW], score[k][:], ACT.Exp, bias=m["neg_bound"][:]
                                     ).then_inc(weight_ready[k], 1)

            def round_off(k, s):
                act.wait_ge(weighed_done[k], s + 1)
                act.wait_ge(sum_done[k], s)
                nc.scalar.copy(high[k][:], weighed[k][:]).then_inc(rounded[k], 1)

            def body(s, col, next_col, next_b, b):
                exponentials(0, s)
                indices(0, s + 1, next_col)
                round_off(0, s)
                exponentials(1, s)
                indices(1, s + 1, next_col)
                copy_turned(2, s)
                round_off(1, s)
                exponentials(2, s)
                indices(2, s + 1, next_col)
                copy_turned(0, s + 1)
                round_off(2, s)
                copy_turned(1, s + 1)

            act.sem_inc(acc_done, 1)
            nc.scalar.activation(m["warm"][0][:], m["neg_bound"][:], ACT.Exp)
            _, (lo,) = nc.values_load_multi_w_load_instructions(
                m["ranges"][0:1, 0, 0:1], engines=[act.engine], min_val=0, max_val=NSUB)
            for k in range(K):
                indices(k, 1, lo)
            for k in range(2):
                copy_turned(k, 1)
            with act.Fori(0, NT) as b:
                over_steps(act, b, lambda s, col, next_col, next_b: body(s, col, next_col, next_b, b))
                act.wait_ge(block_summed, b + 1)
                nc.scalar.copy(m["acc"][:, bass.ds(b, 1), :].rearrange("p a d -> p (a d)"), acc_bank[0:NP, 0:ROW]
                               ).then_inc(acc_done, 1)


def route_phase(nc, m, bank, x, skip_rows, xg):
    with ExitStack() as ctx:
        def sb(name, shape, dt=F32):
            return ctx.enter_context(nc.sbuf_tensor(name, shape, dt))

        def sem(name):
            return ctx.enter_context(nc.semaphore(name))

        def sems(name, n=2):
            return [sem(f"{name}{k}") for k in range(n)]

        xin, skin = sb("r_xin", [NP, 2, D]), sb("r_skin", [NP, 2, D])
        den = sb("den", [NP, NT, H])
        att, low, ex = sb("att", [NP, 2, D]), sb("low", [NP, 2, D]), sb("ex", [NP, 2, D])
        stats, mv = sb("r_stats", [NP, 2, 6]), sb("r_mv", [NP, NT, 2])
        mv_pair = sb("mv_pair", [NP, 2, 2])
        std1, rstd1, var2, std2, rstd2, rstd12 = (
            sb(s, [NP, NT]) for s in ("std1", "rstd1", "var2", "std2", "rstd2", "rstd12"))
        xl, xlt, xn = sb("xl", [NP, 2, D]), sb("xlt", [P, 2, KD, NP]), sb("r_xn", [NP, 2, 2, XROW])
        logits, top8, pick8 = sb("logits", [NP, 2, NX]), sb("top8", [NP, 2, 8]), sb("pick8", [NP, 2, 8], U32)
        pick, one = sb("pick", [NP, 2, 2]), sb("one", [NP, 2, 2, NX])
        mask, before = sb("mask", [NP, 2, NX], BF16), sb("before", [NP, NX], BF16)
        lower16, ones16 = sb("lower16", [NP, NP], BF16), sb("ones16", [NP, NP], BF16)
        rank, place, junk = sb("rank", [NP, 2, NX]), sb("place", [NP, 2, 2]), sb("junk", [NP, 2, 2, NX])
        slot = [[sb(f"slot{u}{k}", [NP, 1], I32) for k in range(2)] for u in range(2)]
        padding = sb("padding", [P, FILL // P, XROW])
        crow, cwhole = sb("count_row", [1, 6, NX]), sb("count_whole", [1, NX], I32)
        wtmp = sb("wtmp", [NP, NT])

        begun = m["begun"]
        skin_loaded, xin_loaded, low_ready, ex_ready, x_used, mask_ready, ranked = (sem(s) for s in (
            "skin_loaded", "xin_loaded", "low_ready", "ex_ready", "x_used", "mask_ready", "ranked"))
        res_step, dve_step, norm_dve, norm_act, end_step = (
            sem(s) for s in ("res_step", "route_step", "norm_dve", "norm_act", "end_step"))
        xl_ready, xlt_psum, xlt_ready, xn_first, xn_ready, logit_psum, slot_ready, sent = (sems(s) for s in (
            "xl_ready", "xlt_psum", "xlt_ready", "xn_first", "r_xn_ready", "logit_psum", "slot_ready", "sent"))
        zero_ready, counted, count_ready, filled = (
            sem(s) for s in ("zero_ready", "counted", "count_ready", "filled"))
        block = ctx.enter_context(nc.Block())
        PAIRS = NT // 2
        MEANS = 2 + PAIRS

        @block.sync
        def _(sp):
            def pair(rows, i):
                return rows[bass.ds(i * 2 * NP, 2 * NP), :].rearrange("(u p) d -> p u d", u=2)

            with sp.Fori(0, PAIRS) as i:
                sp.wait_ge(low_ready, i)
                sp.dma_start(skin[:], pair(skip_rows, i)).then_inc(skin_loaded, 16)
                sp.wait_ge(x_used, i)
                sp.dma_start(xin[:], pair(x, i)).then_inc(xin_loaded, 16)
            sp.wait_ge(zero_ready, 1 + FILL // P)
            sp.wait_ge(count_ready, 1)
            with sp.Fori(0, NX) as e:
                n = nc.values_load(m["counts"][0:1, bass.ds(e, 1), 0:1].rearrange("p a k -> p (a k)"),
                                   engines=[sp.engine], min_val=0, max_val=N)
                sp.dma_start(xg[bass.ds(e * CAP + n, FILL), :].rearrange("(h p) d -> p h d", p=P), padding[:]
                             ).then_inc(filled, 16)
            sp.wait_ge(filled, 16 * NX)

        @block.vector
        def _(dve):
            nc.vector.memset(padding[:, :, 0:D], 0.0).then_inc(zero_ready, 1)
            for h in range(FILL // P):
                nc.vector.tensor_scalar(padding[:, h, D:XROW], m["iota_p"][:], float(2 * N), None, ALU.add
                                        ).then_inc(zero_ready, 1)
            nc.vector.memset(before[:], 0.0).then_inc(zero_ready, 1)
            nc.vector.tensor_copy(lower16[:], m["lower"][0:NP, 0:NP]).then_inc(zero_ready, 1)
            nc.vector.tensor_copy(ones16[:], m["ones"][0:NP, 0:NP]).then_inc(zero_ready, 1)
            nc.vector.tensor_scalar(den[:], m["acc"][:, :, D:ROW], m["eps"][0:NP, :], None, ALU.add
                                    ).then_inc(norm_dve, 1)
            dve.wait_ge(norm_dve, 1)
            nc.vector.reciprocal(den[:], den[:]).then_inc(norm_dve, 1)
            dve.wait_ge(norm_dve, 2)
            RES_STEPS = 7
            with dve.Fori(0, PAIRS) as i:
                steps = [0]

                def step(ins):
                    steps[0] += 1
                    ins.then_inc(res_step, 1)

                def settle(constant=None):
                    count = value_of(dve, steps[0] + i * RES_STEPS)
                    if constant is not None:
                        dve.wait_ge(constant, 1)
                    dve.wait_ge(res_step, count)

                x1 = m["acc"][:, bass.ds(2 * i, 2), 0:D]
                shape = [NP, 2, H, FO]
                step(nc.vector.tensor_tensor(
                    att[:].rearrange("p u (h f) -> p u h f", h=H), x1.rearrange("p u (h f) -> p u h f", h=H),
                    den[:, bass.ds(2 * i, 2), :].unsqueeze(3).to_broadcast(shape), ALU.mult))
                settle()
                dve.wait_ge(skin_loaded, 16 * (i + 1))
                step(nc.vector.tensor_tensor(att[:], att[:], skin[:], ALU.add))
                settle()
                nc.vector.tensor_scalar(low[:], att[:], 0.0, None, ALU.min).then_inc(low_ready, 1)
                dve.wait_ge(ex_ready, i + 1)
                step(nc.vector.scalar_tensor_tensor(att[:], att[:], 0.0, ex[:], ALU.max, ALU.add))
                settle()
                dve.wait_ge(xin_loaded, 16 * (i + 1))
                nc.vector.scalar_tensor_tensor(x1, att[:], -1.0, xin[:], ALU.add, ALU.add).then_inc(x_used, 1)
                after = value_of(dve, i + 1)
                dve.wait_ge(begun, 1)
                dve.wait_ge(x_used, after)
                for u in range(2):
                    step(nc.vector.bn_stats(stats[:, u, :], m["acc"][:, bass.ds(2 * i + u, 1), 0:D]
                                            .rearrange("p a d -> p (a d)")))
                settle(begun)
                for u in range(2):
                    step(nc.vector.bn_aggr(mv_pair[:, u, :], stats[:, u, :]))
                settle()
                nc.vector.tensor_copy(mv[:, bass.ds(2 * i, 2), :], mv_pair[:]).then_inc(norm_dve, 1)
                assert steps[0] == RES_STEPS, steps[0]
            dve.wait_ge(norm_act, 1)
            nc.vector.reciprocal(rstd1[:], std1[:]).then_inc(norm_dve, 1)
            dve.wait_ge(norm_dve, MEANS + 1)
            nc.vector.tensor_tensor(var2[:], rstd1[:], rstd1[:], ALU.mult).then_inc(norm_dve, 1)
            dve.wait_ge(norm_dve, MEANS + 2)
            nc.vector.tensor_tensor(var2[:], var2[:], mv[:, :, 1], ALU.mult).then_inc(norm_dve, 1)
            dve.wait_ge(norm_act, 2)
            nc.vector.reciprocal(rstd2[:], std2[:]).then_inc(norm_dve, 1)
            dve.wait_ge(norm_dve, MEANS + 4)
            nc.vector.tensor_tensor(rstd12[:], rstd1[:], rstd2[:], ALU.mult).then_inc(norm_dve, 1)
            dve.wait_ge(norm_dve, MEANS + 5)
            PER = 14

            def x1_of(t):
                return m["acc"][:, bass.ds(t, 1), 0:D].rearrange("p a d -> p (a d)")

            def first_norm(i):
                for u in range(2):
                    t = 2 * i + u
                    dve.wait_ge(xlt_psum[u], i)
                    nc.vector.tensor_scalar(xl[:, u, :], x1_of(t), m_v(mv, t)[:, 0:1], rstd1[:, bass.ds(t, 1)],
                                            ALU.subtract, ALU.mult).then_inc(xl_ready[u], 1)

            def route(i, more):
                done = [0]

                def step(ins):
                    done[0] += 1
                    ins.then_inc(dve_step, 1)

                def settle(constant=None):
                    count = value_of(dve, done[0] + i * PER)
                    if constant is not None:
                        dve.wait_ge(constant, 1)
                    dve.wait_ge(dve_step, count)

                for u in range(2):
                    dve.wait_ge(logit_psum[u], i + 1)
                    step(nc.vector.tensor_tensor(logits[:, u, :], bank[4 + u][0:NP, 0:NX], m["br"][:], ALU.add))
                settle(begun)
                for u in range(2):
                    step(nc.vector.max(top8[:, u, :], logits[:, u, :]))
                settle(begun)
                for u in range(2):
                    step(nc.vector.max_index(pick8[:, u, :], top8[:, u, :], logits[:, u, :]))
                step(nc.vector.tensor_tensor(m["gaps"][:, bass.ds(2 * i, 2)], top8[:, :, 1], top8[:, :, 0], ALU.subtract))
                settle()
                step(nc.vector.tensor_copy(pick[:], pick8[:, :, 0:2]))
                settle()
                shape = [NP, 4, NX]
                step(nc.vector.tensor_tensor(
                    one[:].rearrange("p u k e -> p (u k) e"), m["iota"][0:NP, 0:NX].unsqueeze(1).to_broadcast(shape),
                    pick[:].rearrange("p u k -> p (u k)").unsqueeze(2).to_broadcast(shape), ALU.is_equal))
                settle()
                nc.vector.tensor_tensor(mask[:], one[:, :, 0, :], one[:, :, 1, :], ALU.add).then_inc(mask_ready, 1)
                if more:
                    first_norm(i + 1)
                dve.wait_ge(ranked, i + 1)
                step(nc.vector.tensor_tensor(rank[:], bank[6][0:NP, 0:2 * NX].rearrange("p (u e) -> p u e", u=2),
                                             m["cap_row"][0:NP, :].unsqueeze(1).to_broadcast([NP, 2, NX]), ALU.add))
                step(nc.vector.tensor_tensor(before[:], before[:], mask[:, 0, :], ALU.add))
                settle()
                step(nc.vector.tensor_tensor(before[:], before[:], mask[:, 1, :], ALU.add))
                step(nc.vector.tensor_tensor(junk[:], one[:], rank[:].unsqueeze(2).to_broadcast([NP, 2, 2, NX]), ALU.mult))
                settle()
                step(nc.vector.tensor_reduce(place[:], junk[:], X, ALU.add))
                settle()
                for u in range(2):
                    t = 2 * i + u
                    dve.wait_ge(sent[u], 32 * i)
                    for k in range(2):
                        nc.vector.tensor_copy(slot[u][k][:], place[:, u, k:k + 1]).then_inc(slot_ready[u], 1)
                    nc.vector.tensor_copy(xn[:, u, :, D:XROW].rearrange("p k o -> p (k o)"),
                                          m["result_row"][:, bass.ds(t, 1), :].rearrange("p a k -> p (a k)")
                                          ).then_inc(slot_ready[u], 1)
                    dve.wait_ge(xn_ready[u], i)
                    nc.vector.tensor_scalar(xn[:, u, 0, 0:D], x1_of(t), m_v(mv, t)[:, 0:1], rstd12[:, bass.ds(t, 1)],
                                            ALU.subtract, ALU.mult).then_inc(xn_first[u], 1)
                assert done[0] == PER, done[0]

            first_norm(0)
            with dve.Fori(0, PAIRS - 1) as i:
                route(i, True)
            route(PAIRS - 1, False)
            dve.wait_ge(dve_step, PER * PAIRS)
            dve.sem_inc(zero_ready, 1)
            dve.wait_ge(counted, 1)
            last = [0]

            def then(ins):
                last[0] += 1
                ins.then_inc(end_step, 1)
                dve.wait_ge(end_step, last[0])

            CNT, UP, TILES, GE, GS, ZERO = range(6)
            then(nc.vector.tensor_copy(crow[:, CNT], bank[3][0:1, 0:NX]))
            then(nc.vector.memset(crow[:, ZERO], 0.0))
            then(nc.vector.tensor_scalar(crow[:, UP], crow[:, CNT], 1.0, float(TOK - 1), ALU.max, ALU.add))
            then(nc.vector.tensor_copy(cwhole[:], crow[:, UP]))
            then(nc.vector.tensor_scalar(cwhole[:], cwhole[:], TOK.bit_length() - 1, None, ALU.arith_shift_right))
            then(nc.vector.tensor_copy(crow[:, TILES], cwhole[:]))
            then(nc.vector.tensor_tensor_scan(crow[:, GE], crow[:, TILES], crow[:, ZERO], 0.0, ALU.add, ALU.add))
            then(nc.vector.tensor_tensor(crow[:, GS], crow[:, GE], crow[:, TILES], ALU.subtract))
            for k, r in enumerate((CNT, GS, GE)):
                then(nc.vector.tensor_copy(m["counts"][:, :, k], crow[:, r]))
            then(nc.vector.tensor_scalar(crow[:, ZERO], crow[:, GE], -1.0, None, ALU.add))
            nc.vector.tensor_copy(m["counts"][:, :, 3], crow[:, ZERO]).then_inc(count_ready, 1)
            dve.wait_ge(norm_act, 3)
            then(nc.vector.tensor_scalar(wtmp[:], m["gaps"][:], 1.0, None, ALU.add))
            then(nc.vector.reciprocal(m["weights"][:, :, 0], wtmp[:]))
            then(nc.vector.tensor_tensor(m["weights"][:, :, 1], m["weights"][:, :, 0], m["gaps"][:], ALU.mult))

        @block.scalar
        def _(act):
            with act.Fori(0, PAIRS) as i:
                act.wait_ge(low_ready, i + 1)
                nc.scalar.activation(ex[:], low[:], ACT.Exp).then_inc(ex_ready, 1)
            act.wait_ge(norm_dve, MEANS)
            nc.scalar.activation(std1[:], mv[:, :, 1], ACT.Sqrt, bias=m["ln_eps"][0:NP, :]).then_inc(norm_act, 1)
            act.wait_ge(norm_dve, MEANS + 3)
            nc.scalar.activation(std2[:], var2[:], ACT.Sqrt, bias=m["ln_eps"][0:NP, :]).then_inc(norm_act, 1)

            def copy_turned(i):
                for u in range(2):
                    act.wait_ge(xlt_psum[u], i + 1)
                    nc.scalar.copy(xlt[:, u, :, :], bank[u][:, 0:KD * P].rearrange("p (k n) -> p k n", k=KD)[:, :, 0:NP]
                                   ).then_inc(xlt_ready[u], 1)

            def second_copy(i):
                for u in range(2):
                    act.wait_ge(xn_first[u], i + 1)
                    nc.scalar.copy(xn[:, u, 1, 0:D], xn[:, u, 0, 0:D]).then_inc(xn_ready[u], 1)

            copy_turned(0)
            with act.Fori(0, PAIRS - 1) as i:
                copy_turned(i + 1)
                second_copy(i)
            second_copy(PAIRS - 1)
            act.wait_ge(count_ready, 1)
            nc.scalar.activation(m["gaps"][:], m["gaps"][:], ACT.Exp).then_inc(norm_act, 1)

        @block.tensor
        def _(pe):
            def logits_of(i):
                for u in range(2):
                    pe.wait_ge(xl_ready[u], i + 1)
                    for k in range(KD):
                        mm = nc.tensor.transpose(bank[u][:, k * P:k * P + NP], xl[:, u, k * P:(k + 1) * P],
                                                 m["ident"][0:NP, 0:NP])
                    mm.then_inc(xlt_psum[u], 1)
                for u in range(2):
                    pe.wait_ge(xlt_ready[u], i + 1)
                    for k in range(KD):
                        mm = nc.tensor.matmul(bank[4 + u][0:NP, 0:NX], xlt[:, u, k, :], m["wr"][:, k, :],
                                              start=(k == 0), stop=(k == KD - 1))
                    mm.then_inc(logit_psum[u], 1)

            def ranks_of(i):
                pe.wait_ge(mask_ready, i + 1)
                for u in range(2):
                    parts = [(ones16, before[:])] + [(ones16, mask[:, v, :]) for v in range(u)] + [(lower16, mask[:, u, :])]
                    for n, (w, v) in enumerate(parts):
                        mm = nc.tensor.matmul(bank[6][0:NP, u * NX:(u + 1) * NX], w[:], v,
                                              start=(n == 0), stop=(n == len(parts) - 1))
                mm.then_inc(ranked, 1)

            pe.wait_ge(zero_ready, 4 + FILL // P)
            logits_of(0)
            with pe.Fori(0, PAIRS - 1) as i:
                ranks_of(i)
                logits_of(i + 1)
            ranks_of(PAIRS - 1)
            pe.wait_ge(zero_ready, 5 + FILL // P)
            nc.tensor.matmul(bank[3][0:1, 0:NX], ones16[:, 0:1], before[:], start=True,
                             stop=True).then_inc(counted, 1)

        @block.gpsimd
        def _(pool):
            with pool.Fori(0, PAIRS) as i:
                for u in range(2):
                    three, after = value_of(pool, 3 * (i + 1)), value_of(pool, i + 1)
                    pool.wait_ge(begun, 1)
                    pool.wait_ge(slot_ready[u], three)
                    pool.wait_ge(xn_ready[u], after)
                    for k in range(2):
                        nc.gpsimd.indirect_dma_start(
                            xg, bass.IndirectOffsetOnAxis(ap=slot[u][k][:], axis=0), xn[:, u, k, :], None
                        ).then_inc(sent[u], 16)
            for u in range(2):
                pool.wait_ge(sent[u], 32 * PAIRS)


def expert_phase(nc, m, bank, xg, y2, ln_g, ln_b, W1, b1, W2, b2):
    with ExitStack() as ctx:
        def sb(name, shape, dt=F32):
            return ctx.enter_context(nc.sbuf_tensor(name, shape, dt))

        def sem(name):
            return ctx.enter_context(nc.semaphore(name))

        def sems(name, n=2):
            return [sem(f"{name}{k}") for k in range(n)]

        w1_raw, w2_raw = sb("w1_raw", [P, KD, HID]), sb("w2_raw", [P, JH, D])
        params_raw, params = sb("params_raw", [P, 2 * KD + JH + D]), sb("params", [P, 2, 2 * KD + JH + D])
        w1h, w1l = sb("w1h", [P, 2, KD, HID], F32R), sb("w1l", [P, 2, KD, HID], F32R)
        w2h, w2l = sb("w2h", [P, 2, JH, D], F32R), sb("w2l", [P, 2, JH, D], F32R)
        GAIN, SHIFT, B1, B2 = 0, KD, 2 * KD, 2 * KD + JH
        xrow = sb("xrow", [P, HALF, XROW])
        xt, xth, xtl = sb("f_xt", [P, KD, TOK]), sb("f_xth", [P, KD, TOK], F32R), sb("f_xtl", [P, KD, TOK], F32R)
        hid = sb("hid", [P, JH, TOK])
        hidh, hidl = sb("hidh", [P, JH, TOK], F32R), sb("hidl", [P, JH, TOK], F32R)
        yrow = sb("yrow", [P, HALF, D])
        goes_next = sb("goes_next", [P, HALF])
        goes_to = [sb(f"goes_to{h}", [P, 1], I32) for h in range(HALF)]
        x_bank, y_bank, h_bank = bank[0:HALF], bank[5:5 + HALF], [bank[k] for k in (2, 3, 4, 7)]
        HB = len(h_bank)
        raw_loaded, w_high, w_low, xt_step, hid_high, hid_low = (
            sem(s) for s in ("f_raw_loaded", "f_w_high", "f_w_low", "f_xt_step", "f_hid_high", "f_hid_low"))
        row_loaded, row_used, goes_ready, stored, y_psum, y_ready = (sems(s, HALF) for s in (
            "f_row_loaded", "f_row_used", "f_goes_ready", "f_stored", "f_y_psum", "f_y_ready"))
        h_psum, h_ready = sems("f_h_psum", HB), sems("f_h_ready", HB)
        block = ctx.enter_context(nc.Block())
        W_LOADS = 6
        XT_STEPS = KD * HALF + 2

        def tiles_of(engine, e):
            _, got = nc.values_load_multi_w_load_instructions(
                m["counts"][0:1, bass.ds(e, 1), 1:4].rearrange("p a k -> p (a k)"),
                engines=[engine.engine], min_val=0, max_val=NX * CAP // TOK)
            return got

        def over_experts(engine, body):
            with engine.Fori(0, NX // 2 - 1) as i:
                body(i, 0, True)
                body(i, 1, True)
            body(NX // 2 - 1, 0, True)
            body(NX // 2 - 1, 1, False)

        @block.sync
        def _(sp):
            def load_rows(g, row):
                rows = [sp.snap(row + h * P) if h else row for h in range(HALF)]
                steps = value_of(sp, XT_STEPS * g)
                for h in range(HALF):
                    sp.wait_ge(row_used[h], g)
                    sp.wait_ge(xt_step, steps)
                    sp.dma_start(xrow[:, h, :], xg[bass.ds(rows[h], P), :]).then_inc(row_loaded[h], 16)

            with sp.Fori(0, NX) as e:
                first, end, _ = tiles_of(sp, e)
                with sp.Fori(first, end) as g:
                    load_rows(g, nc.s_assert_within(sp.snap((g - first) * TOK + e * CAP), 0, NX * CAP - TOK,
                                                    skip_runtime_bounds_check_because=BY_TABLE))
            _, end, _ = tiles_of(sp, NX - 1)
            load_rows(end, sp.snap(sp.to_reg(0)))

        @block.tensor
        def _(pe):
            def turn_rows(g):
                for h in range(HALF):
                    pe.wait_ge(row_loaded[h], 16 * (g + 1))
                    for k in range(KD):
                        mm = nc.tensor.transpose(x_bank[h][:, k * P:(k + 1) * P],
                                                 xrow[:, h, k * P:(k + 1) * P], m["ident"][:])
                    mm.then_inc(row_used[h], 1)

            def body(g, s):
                pe.wait_ge(xt_step, XT_STEPS * (g + 1))
                for j in range(JH):
                    pe.wait_ge(h_ready[j % HB], JH // HB * g + j // HB)
                    for k in range(KD):
                        at = slice(j * P, (j + 1) * P)
                        for n, (w, v) in enumerate(((w1h, xth), (w1h, xtl), (w1l, xth))):
                            mm = nc.tensor.matmul(h_bank[j % HB][:, 0:TOK], w[:, s, k, at], v[:, k, :],
                                                  start=(k == 0 and n == 0), stop=(k == KD - 1 and n == 2))
                    mm.then_inc(h_psum[j % HB], 1)
                turn_rows(g + 1)
                for h in range(HALF):
                    pe.wait_ge(y_ready[h], g)
                for j in range(JH):
                    for n, (v, w) in enumerate(((hidh, w2h), (hidh, w2l), (hidl, w2h))):
                        if n == 0:
                            pe.wait_ge(hid_high, JH * g + j + 1)
                        if n == 2:
                            pe.wait_ge(hid_low, JH * g + j + 1)
                        for h in range(HALF):
                            mm = nc.tensor.matmul(y_bank[h][:, 0:D], v[:, j, h * P:(h + 1) * P], w[:, s, j, :],
                                                  start=(j == 0 and n == 0), stop=(j == JH - 1 and n == 2))
                            if j == JH - 1 and n == 2:
                                mm.then_inc(y_psum[h], 1)

            turn_rows(0)
            with pe.Fori(0, NX // 2) as i:
                for s in range(2):
                    first, end, _ = tiles_of(pe, 2 * i + s)
                    with pe.Fori(first, end) as g:
                        pe.wait_ge(w_high, 2 * (2 * i + s + 1))
                        pe.wait_ge(w_low, 3 * (2 * i + s + 1))
                        body(g, s)

        @block.scalar
        def _(act):
            def split_high(e, s):
                act.wait_ge(raw_loaded, 16 * W_LOADS * (e + 1))
                nc.scalar.copy(w1h[:, s], w1_raw[:]).then_inc(w_high, 1)
                nc.scalar.copy(w2h[:, s], w2_raw[:]).then_inc(w_high, 1)

            def gelus(g, s):
                def rounded(j):
                    act.wait_ge(h_ready[j % HB], JH // HB * g + j // HB + 1)
                    nc.scalar.copy(hidh[:, j, :], hid[:, j, :]).then_inc(hid_high, 1)

                for j in range(JH):
                    act.wait_ge(h_psum[j % HB], JH // HB * g + j // HB + 1)
                    if j == 0:
                        act.wait_ge(hid_low, JH * g)
                    nc.scalar.activation(hid[:, j, :], h_bank[j % HB][:, 0:TOK], ACT.Gelu,
                                         bias=params[:, s, B1 + j:B1 + j + 1]).then_inc(h_ready[j % HB], 1)
                    if j:
                        rounded(j - 1)
                rounded(JH - 1)

            def expert(i, s, more):
                first, end, _ = tiles_of(act, 2 * i + s)
                if more:
                    act.wait_ge(y_ready[HALF - 1], first)
                    split_high(2 * i + s + 1, 1 - s)
                act.wait_ge(w_low, 3 * (2 * i + s + 1))
                with act.Fori(first, end) as g:
                    gelus(g, s)

            nc.scalar.activation(m["warm"][2][:], m["ln_eps"][:], ACT.Gelu)
            split_high(0, 0)
            over_experts(act, expert)

        @block.vector
        def _(dve):
            def split_low(e, s):
                dve.wait_ge(raw_loaded, 16 * W_LOADS * (e + 1))
                nc.vector.tensor_copy(params[:, s], params_raw[:]).then_inc(w_low, 1)
                for n, (low, raw, high) in enumerate(((w1l, w1_raw, w1h), (w2l, w2_raw, w2h))):
                    dve.wait_ge(w_high, 2 * e + n + 1)
                    nc.vector.tensor_tensor(low[:, s], raw[:], high[:, s].bitcast(F32), ALU.subtract
                                            ).then_inc(w_low, 1)

            def normalize(g, s):
                for h in range(HALF):
                    dve.wait_ge(row_used[h], g + 1)
                    nc.vector.tensor_copy(goes_next[:, h:h + 1], xrow[:, h, D:XROW])
                    for k in range(KD):
                        nc.vector.tensor_scalar(xt[:, k, h * P:(h + 1) * P], x_bank[h][:, k * P:(k + 1) * P],
                                                params[:, s, GAIN + k:GAIN + k + 1], params[:, s, SHIFT + k:SHIFT + k + 1],
                                                ALU.mult, ALU.add).then_inc(xt_step, 1)
                dve.wait_ge(xt_step, XT_STEPS * g + XT_STEPS - 2)
                nc.vector.tensor_copy(xth[:], xt[:]).then_inc(xt_step, 1)
                dve.wait_ge(xt_step, XT_STEPS * g + XT_STEPS - 1)
                nc.vector.tensor_tensor(xtl[:], xt[:], xth[:].bitcast(F32), ALU.subtract).then_inc(xt_step, 1)

            def body(g, s, next_s, parameters):
                for j in range(JH):
                    dve.wait_ge(hid_high, JH * g + j + 1)
                    nc.vector.tensor_tensor(hidl[:, j, :], hid[:, j, :], hidh[:, j, :].bitcast(F32), ALU.subtract
                                            ).then_inc(hid_low, 1)
                dve.wait_ge(xt_step, XT_STEPS * (g + 1))
                for h in range(HALF):
                    dve.wait_ge(stored[h], 16 * g)
                    nc.vector.tensor_copy(goes_to[h][:], goes_next[:, h:h + 1]).then_inc(goes_ready[h], 1)
                for h in range(HALF):
                    dve.wait_ge(goes_ready[h], g + 1)
                dve.wait_ge(w_low, parameters)
                normalize(g + 1, next_s)
                for h in range(HALF):
                    dve.wait_ge(y_psum[h], g + 1)
                    nc.vector.tensor_tensor(yrow[:, h, :], y_bank[h][:, 0:D], params[:, s, B2:B2 + D], ALU.add
                                            ).then_inc(y_ready[h], 1)

            def expert(i, s, more):
                first, _, last = tiles_of(dve, 2 * i + s)
                if more:
                    for h in range(HALF):
                        dve.wait_ge(y_ready[h], first)
                    split_low(2 * i + s + 1, 1 - s)
                with dve.Fori(first, last) as g:
                    body(g, s, s, 3 * (2 * i + s + 1))
                body(last, s, 1 - s if more else s, 3 * (2 * i + s + (2 if more else 1)))

            split_low(0, 0)
            dve.wait_ge(w_low, 3)
            normalize(0, 0)
            over_experts(dve, expert)

        @block.gpsimd
        def _(pool):
            def load(e):
                def one(w):
                    return w[bass.ds(e, 1)]

                if not isinstance(e, int) or e > 0:
                    pool.wait_ge(w_low, 3 * e)
                    pool.wait_ge(w_high, 2 * e)
                with nc.allow_non_contiguous_dma(reason="small rows of parameters, once an expert"):
                    for to, of in (
                        (w1_raw[:], one(W1).rearrange("o (k p) h -> p (o k) h", p=P)),
                        (w2_raw[:], one(W2).rearrange("o (j p) d -> p (o j) d", p=P)),
                        (params_raw[:, GAIN:GAIN + KD], one(ln_g).rearrange("o (k p) -> p (o k)", p=P)),
                        (params_raw[:, SHIFT:SHIFT + KD], one(ln_b).rearrange("o (k p) -> p (o k)", p=P)),
                        (params_raw[:, B1:B1 + JH], one(b1).rearrange("o (j p) -> p (o j)", p=P)),
                        (params_raw[:, B2:B2 + D], one(b2).to_broadcast([P, D])),
                    ):
                        pool.dma_start(to, of).then_inc(raw_loaded, 16)

            def scatters(e):
                first, end, _ = tiles_of(pool, e)
                with pool.Fori(first, end) as g:
                    after = value_of(pool, g + 1)
                    sent, sent_after = value_of(pool, 16 * g), value_of(pool, 16 * (g + 1))
                    for h in range(HALF):
                        pool.wait_ge(m["begun"], 1)
                        pool.wait_ge(goes_ready[h], after)
                        pool.wait_ge(y_ready[h], after)
                        pool.wait_ge(stored[0], sent_after if h else sent)
                        pool.wait_ge(stored[1], sent)
                        nc.gpsimd.indirect_dma_start(
                            y2, bass.IndirectOffsetOnAxis(ap=goes_to[h][:], axis=0), yrow[:, h, :], None
                        ).then_inc(stored[h], 16)
                return end

            load(0)
            load(1)
            with pool.Fori(0, NX - 2) as e:
                load(e + 2)
                scatters(e)
            scatters(NX - 2)
            end = scatters(NX - 1)
            for h in range(HALF):
                pool.wait_ge(stored[h], end * 16)


def combine_phase(nc, m, y2, out):
    with ExitStack() as ctx:
        def sb(name, shape, dt=F32):
            return ctx.enter_context(nc.sbuf_tensor(name, shape, dt))

        def sems(name, n=2):
            return [ctx.enter_context(nc.semaphore(f"{name}{k}")) for k in range(n)]

        C = 5
        CHUNKS = NT // C
        assert CHUNKS % 2 == 0
        y, mid, total = sb("c_y", [NP, 2, C, 2, D]), sb("c_mid", [NP, 2, C, D]), sb("c_total", [NP, 2, C, D])
        loaded, summed, stored = sems("c_loaded"), sems("c_summed"), sems("c_stored")
        block = ctx.enter_context(nc.Block())

        @block.sync
        def _(sp):
            with sp.Fori(0, CHUNKS // 2) as i:
                for u in range(2):
                    sp.wait_ge(summed[u], 2 * C * i)
                    rows = y2[bass.ds((2 * i + u) * C * 2 * NP, C * 2 * NP), :].rearrange(
                        "(c p k) d -> p c k d", c=C, k=2)
                    for part in NODE_PARTS:
                        sp.dma_start(y[part, u], rows[part]).then_inc(loaded[u], 16)

        @block.vector
        def _(dve):
            with dve.Fori(0, CHUNKS // 2) as i:
                for u in range(2):
                    first = (2 * i + u) * C
                    dve.wait_ge(loaded[u], 16 * len(NODE_PARTS) * (i + 1))
                    for c in range(C):
                        w = m["weights"][:, bass.ds(first + c, 1), :].rearrange("p a k -> p (a k)")
                        x1 = m["acc"][:, bass.ds(first + c, 1), 0:D].rearrange("p a d -> p (a d)")
                        nc.vector.scalar_tensor_tensor(mid[:, u, c, :], y[:, u, c, 0, :], w[:, 0:1], x1,
                                                       ALU.mult, ALU.add).then_inc(summed[u], 1)
                    dve.wait_ge(summed[u], 2 * C * i + C)
                    dve.wait_ge(stored[u], 16 * len(NODE_PARTS) * i)
                    for c in range(C):
                        w = m["weights"][:, bass.ds(first + c, 1), :].rearrange("p a k -> p (a k)")
                        nc.vector.scalar_tensor_tensor(total[:, u, c, :], y[:, u, c, 1, :], w[:, 1:2], mid[:, u, c, :],
                                                       ALU.mult, ALU.add).then_inc(summed[u], 1)

        @block.scalar
        def _(act):
            with act.Fori(0, CHUNKS // 2) as i:
                for u in range(2):
                    act.wait_ge(summed[u], 2 * C * (i + 1))
                    rows = out[bass.ds((2 * i + u) * C * NP, C * NP), :].rearrange("(c p) d -> p c d", c=C)
                    for part in NODE_PARTS:
                        act.dma_start(rows[part], total[part, u]).then_inc(stored[u], 16)
            for u in range(2):
                act.wait_ge(stored[u], 16 * len(NODE_PARTS) * (CHUNKS // 2))


_INS = ['x', 'src', 'dst', 'L0_gnn_Wp', 'L0_gnn_a_src', 'L0_gnn_a_trg', 'L0_gnn_Wskip', 'L0_gnn_bias',
        'L0_ffn_Wr', 'L0_ffn_br', 'L0_ffn_ln_g', 'L0_ffn_ln_b', 'L0_ffn_W1', 'L0_ffn_b1', 'L0_ffn_W2', 'L0_ffn_b2']


def kernel(**inputs):
    import numpy as _np
    import concourse.bacc as _bacc
    from concourse import mybir as _mybir
    from concourse.bass_utils import run_bass_kernel_spmd as _run

    nc = _bacc.Bacc("TRN2", target_bir_lowering=False, num_devices=1)
    arrays, args = {}, []
    for name in _INS:
        a = _np.ascontiguousarray(inputs[name])
        arrays[f"in_{name}_dram"] = a
        args.append(nc.dram_tensor(f"in_{name}_dram", a.shape, _mybir.dt.from_np(a.dtype), kind="ExternalInput").ap())
    args.append(nc.dram_tensor("out_0_dram", (N, D), _mybir.dt.float32, kind="ExternalOutput").ap())
    gnn_ffn(nc, *args)
    r = _run(nc, [arrays], core_ids=[0])
    return r.results[0]["out_0_dram"]
```
